# Optimizing a Trainium2 kernel written in Bass

```python
import numpy as np
import jax
import jax.numpy as jnp

def _softmax(x, axis=-1):
    return jax.nn.softmax(x, axis=axis)

def _gelu(x):
    return jax.nn.gelu(x, approximate=True)

def _silu(x):
    return jax.nn.silu(x)

def _sigmoid(x):
    return jax.nn.sigmoid(x)

def _layernorm(x, axis=-1, eps=1e-05):
    m = jnp.mean(x, axis=axis, keepdims=True)
    v = jnp.var(x, axis=axis, keepdims=True)
    return (x - m) / jnp.sqrt(v + eps)

def _scatter_add(tgt, idx, src, axis=0):
    return tgt.at[idx].add(src)

def _segment_sum(src, seg, n):
    return jax.ops.segment_sum(src, seg, n)
kernel_name = 'mk_early_fusion_d1_tok_img1024_r4_bdf444'

def setup_inputs(seed: int=0):
    np.random.seed(seed)
    _w = jnp.asarray

    def _rec_inputs():
        import jax
        import jax.numpy as jnp
        _rk = jax.random.key(seed)
        x = -0.000169711 + 1.00022 * jax.random.normal(jax.random.fold_in(_rk, 1), (64, 3, 84, 84), jnp.float32)
        txt = 2.36171e-05 + 0.13571 * jax.random.normal(jax.random.fold_in(_rk, 2), (64, 77, 256), jnp.float32)
        return (x, txt)
    x, txt = _rec_inputs()

    def _L0_tok_setup():
        import jax, jax.numpy as jnp
        import numpy as np
        C = 256
        H8 = 8
        DH = C // H8
        PS = 14
        CS = 3
        IMG = 168
        B = 4

        def _ln(x, g, b):
            mu = jnp.mean(x, axis=-1, keepdims=True)
            xc = x - mu
            var = jnp.mean(xc * xc, axis=-1, keepdims=True)
            return xc * jax.lax.rsqrt(var + 1e-05) * g + b

        def _forward(pixel_values, conv_w, class_emb, la_ln_q_g, la_ln_q_b, la_wq, la_ln_kv_g, la_ln_kv_b, la_wkv, la_proj_w, la_proj_b, ga_ln_q_g, ga_ln_q_b, ga_wq, ga_ln_kv_g, ga_ln_kv_b, ga_wkv, ga_proj_w, ga_proj_b, mod_w, mod_b):
            b = pixel_values.shape[0]
            pe = jax.lax.conv_general_dilated(pixel_values, conv_w, (PS, PS), 'VALID', dimension_numbers=('NCHW', 'OIHW', 'NCHW'))
            HP = pe.shape[2]
            h = HP // CS
            hw, N = (h * h, CS * CS)
            scale = C ** (-0.5)
            grid = pe.reshape(b, C, h, CS, h, CS)
            red = grid.mean(axis=(3, 5)).reshape(b, C, hw).transpose(0, 2, 1)
            win = grid.transpose(0, 2, 4, 3, 5, 1).reshape(b, hw, N, C)
            q = _ln(red, la_ln_q_g, la_ln_q_b) @ la_wq
            q = q.reshape(b, hw, H8, DH).transpose(0, 2, 1, 3)
            kv = _ln(win, la_ln_kv_g, la_ln_kv_b) @ la_wkv
            kv = kv.reshape(b, hw, N, 2, H8, DH).transpose(3, 0, 4, 1, 2, 5)
            k_, v_ = (kv[0], kv[1])
            attn = jax.nn.softmax(jnp.einsum('bhnd,bhnkd->bhnk', q * scale, k_), axis=-1)
            agg = jnp.einsum('bhnk,bhnkd->bhnd', attn, v_)
            agg = agg.transpose(0, 2, 1, 3).reshape(b, hw, C)
            local_out = red + agg @ la_proj_w + la_proj_b
            cls = jnp.broadcast_to(class_emb, (b, 1, C))
            gq = (_ln(cls, ga_ln_q_g, ga_ln_q_b) @ ga_wq).reshape(b, H8, DH)
            gkv = _ln(local_out, ga_ln_kv_g, ga_ln_kv_b) @ ga_wkv
            gkv = gkv.reshape(b, hw, 2, H8, DH).transpose(2, 0, 3, 1, 4)
            gk, gv = (gkv[0], gkv[1])
            gattn = jax.nn.softmax(jnp.einsum('bhd,bhnd->bhn', gq * scale, gk), axis=-1)
            gagg = jnp.einsum('bhn,bhnd->bhd', gattn, gv).reshape(b, 1, C)
            cls_out = cls + gagg @ ga_proj_w + ga_proj_b
            patch_out = local_out @ mod_w + mod_b
            return jnp.concatenate([patch_out, cls_out], axis=1)
        key = jax.random.key(seed)
        ks = jax.random.split(key, 16)
        nrm = lambda k, shape: jax.random.normal(k, shape, jnp.float32) * 0.02
        return {'pixel_values': jax.random.normal(ks[0], (B, 3, IMG, IMG), jnp.float32), 'pixel_masks': jnp.ones((B, 1, IMG, IMG), jnp.float32), 'conv_w': nrm(ks[1], (C, 3, PS, PS)), 'class_emb': nrm(ks[2], (C,)), 'la_ln_q_g': jnp.ones((C,)), 'la_ln_q_b': jnp.zeros((C,)), 'la_wq': nrm(ks[3], (C, C)), 'la_ln_kv_g': jnp.ones((C,)), 'la_ln_kv_b': jnp.zeros((C,)), 'la_wkv': nrm(ks[4], (C, 2 * C)), 'la_proj_w': nrm(ks[5], (C, C)), 'la_proj_b': jnp.zeros((C,)), 'ga_ln_q_g': jnp.ones((C,)), 'ga_ln_q_b': jnp.zeros((C,)), 'ga_wq': nrm(ks[6], (C, C)), 'ga_ln_kv_g': jnp.ones((C,)), 'ga_ln_kv_b': jnp.zeros((C,)), 'ga_wkv': nrm(ks[7], (C, 2 * C)), 'ga_proj_w': nrm(ks[8], (C, C)), 'ga_proj_b': jnp.zeros((C,)), 'mod_w': nrm(ks[9], (C, C)), 'mod_b': jnp.zeros((C,))}
    _L0_tok_all = _L0_tok_setup()
    _L0_tok_in = {k: v for k, v in _L0_tok_all.items() if k in ('pixel_masks', 'conv_w', 'class_emb', 'la_ln_q_g', 'la_ln_q_b', 'la_wq', 'la_ln_kv_g', 'la_ln_kv_b', 'la_wkv', 'la_proj_w', 'la_proj_b', 'ga_ln_q_g', 'ga_ln_q_b', 'ga_wq', 'ga_ln_kv_g', 'ga_ln_kv_b', 'ga_wkv', 'ga_proj_w', 'ga_proj_b', 'mod_w', 'mod_b')}
    del _L0_tok_all

    def _L0_attn_setup():
        import jax, jax.numpy as jnp
        import numpy as np
        ALPHA = 1.2
        A = 1.0
        BANDWIDTH = 1.0
        D_INTRINSIC = 2
        SPHERE_RADIUS = 1.0
        NUM_HEADS = 16
        HIDDEN = 256
        HEAD_DIM = HIDDEN // NUM_HEADS
        EPS = 1e-07

        def _l2norm(t):
            n = jnp.sqrt(jnp.sum(t * t, axis=-1, keepdims=True))
            return t / jnp.maximum(n, 1e-12)
        key = jax.random.key(seed)
        k1, k2, k3, k4, k5 = jax.random.split(key, 5)
        B, S = (2, 512)
        scale = 0.02
        return {'x': jax.random.normal(k1, (B, S, HIDDEN), dtype=jnp.float32), 'w_qkv': jax.random.normal(k2, (3 * HIDDEN, HIDDEN), dtype=jnp.float32) * scale, 'b_qkv': jnp.zeros((3 * HIDDEN,), dtype=jnp.float32), 'w_out': jax.random.normal(k3, (HIDDEN, HIDDEN), dtype=jnp.float32) * scale, 'b_out': jnp.zeros((HIDDEN,), dtype=jnp.float32)}
    _L0_attn_all = _L0_attn_setup()
    _L0_attn_in = {k: v for k, v in _L0_attn_all.items() if k in ('w_qkv', 'b_qkv', 'w_out', 'b_out')}
    del _L0_attn_all

    def _L0_ffn_setup():
        import jax, jax.numpy as jnp
        import numpy as np
        DIM = 256
        HIDDEN = 768
        SCALE = 1.0 / 127.0

        def _dequant(w_int, dtype):
            return w_int.astype(dtype) * jnp.asarray(SCALE, dtype)
        key = jax.random.key(seed)
        k_x, k_g, k_u, k_d = jax.random.split(key, 4)
        x = jax.random.normal(k_x, (4, 512, DIM), dtype=jnp.float32)
        w_gate = jax.random.randint(k_g, (HIDDEN, DIM), -127, 128, dtype=jnp.int32)
        w_up = jax.random.randint(k_u, (HIDDEN, DIM), -127, 128, dtype=jnp.int32)
        w_down = jax.random.randint(k_d, (DIM, HIDDEN), -127, 128, dtype=jnp.int32)
        return {'x': x, 'w_gate': w_gate, 'w_up': w_up, 'w_down': w_down}
    _L0_ffn_all = _L0_ffn_setup()
    _L0_ffn_in = {k: v for k, v in _L0_ffn_all.items() if k in ('w_gate', 'w_up', 'w_down')}
    del _L0_ffn_all
    return {'x': x, 'txt': txt, 'L0_tok_pixel_masks': _L0_tok_in['pixel_masks'], 'L0_tok_conv_w': _L0_tok_in['conv_w'], 'L0_tok_class_emb': _L0_tok_in['class_emb'], 'L0_tok_la_ln_q_g': _L0_tok_in['la_ln_q_g'], 'L0_tok_la_ln_q_b': _L0_tok_in['la_ln_q_b'], 'L0_tok_la_wq': _L0_tok_in['la_wq'], 'L0_tok_la_ln_kv_g': _L0_tok_in['la_ln_kv_g'], 'L0_tok_la_ln_kv_b': _L0_tok_in['la_ln_kv_b'], 'L0_tok_la_wkv': _L0_tok_in['la_wkv'], 'L0_tok_la_proj_w': _L0_tok_in['la_proj_w'], 'L0_tok_la_proj_b': _L0_tok_in['la_proj_b'], 'L0_tok_ga_ln_q_g': _L0_tok_in['ga_ln_q_g'], 'L0_tok_ga_ln_q_b': _L0_tok_in['ga_ln_q_b'], 'L0_tok_ga_wq': _L0_tok_in['ga_wq'], 'L0_tok_ga_ln_kv_g': _L0_tok_in['ga_ln_kv_g'], 'L0_tok_ga_ln_kv_b': _L0_tok_in['ga_ln_kv_b'], 'L0_tok_ga_wkv': _L0_tok_in['ga_wkv'], 'L0_tok_ga_proj_w': _L0_tok_in['ga_proj_w'], 'L0_tok_ga_proj_b': _L0_tok_in['ga_proj_b'], 'L0_tok_mod_w': _L0_tok_in['mod_w'], 'L0_tok_mod_b': _L0_tok_in['mod_b'], 'L0_attn_w_qkv': _L0_attn_in['w_qkv'], 'L0_attn_b_qkv': _L0_attn_in['b_qkv'], 'L0_attn_w_out': _L0_attn_in['w_out'], 'L0_attn_b_out': _L0_attn_in['b_out'], 'L0_ffn_w_gate': _L0_ffn_in['w_gate'], 'L0_ffn_w_up': _L0_ffn_in['w_up'], 'L0_ffn_w_down': _L0_ffn_in['w_down']}

def reference(x, txt, L0_tok_pixel_masks, L0_tok_conv_w, L0_tok_class_emb, L0_tok_la_ln_q_g, L0_tok_la_ln_q_b, L0_tok_la_wq, L0_tok_la_ln_kv_g, L0_tok_la_ln_kv_b, L0_tok_la_wkv, L0_tok_la_proj_w, L0_tok_la_proj_b, L0_tok_ga_ln_q_g, L0_tok_ga_ln_q_b, L0_tok_ga_wq, L0_tok_ga_ln_kv_g, L0_tok_ga_ln_kv_b, L0_tok_ga_wkv, L0_tok_ga_proj_w, L0_tok_ga_proj_b, L0_tok_mod_w, L0_tok_mod_b, L0_attn_w_qkv, L0_attn_b_qkv, L0_attn_w_out, L0_attn_b_out, L0_ffn_w_gate, L0_ffn_w_up, L0_ffn_w_down):
    import jax
    import jax.numpy as jnp

    def _L0_tok_ref(pixel_values, pixel_masks, conv_w, class_emb, la_ln_q_g, la_ln_q_b, la_wq, la_ln_kv_g, la_ln_kv_b, la_wkv, la_proj_w, la_proj_b, ga_ln_q_g, ga_ln_q_b, ga_wq, ga_ln_kv_g, ga_ln_kv_b, ga_wkv, ga_proj_w, ga_proj_b, mod_w, mod_b):
        import jax, jax.numpy as jnp
        import numpy as np
        C = 256
        H8 = 8
        DH = C // H8
        PS = 14
        CS = 3
        IMG = 168
        B = 4

        def _ln(x, g, b):
            mu = jnp.mean(x, axis=-1, keepdims=True)
            xc = x - mu
            var = jnp.mean(xc * xc, axis=-1, keepdims=True)
            return xc * jax.lax.rsqrt(var + 1e-05) * g + b

        def _forward(pixel_values, conv_w, class_emb, la_ln_q_g, la_ln_q_b, la_wq, la_ln_kv_g, la_ln_kv_b, la_wkv, la_proj_w, la_proj_b, ga_ln_q_g, ga_ln_q_b, ga_wq, ga_ln_kv_g, ga_ln_kv_b, ga_wkv, ga_proj_w, ga_proj_b, mod_w, mod_b):
            b = pixel_values.shape[0]
            pe = jax.lax.conv_general_dilated(pixel_values, conv_w, (PS, PS), 'VALID', dimension_numbers=('NCHW', 'OIHW', 'NCHW'))
            HP = pe.shape[2]
            h = HP // CS
            hw, N = (h * h, CS * CS)
            scale = C ** (-0.5)
            grid = pe.reshape(b, C, h, CS, h, CS)
            red = grid.mean(axis=(3, 5)).reshape(b, C, hw).transpose(0, 2, 1)
            win = grid.transpose(0, 2, 4, 3, 5, 1).reshape(b, hw, N, C)
            q = _ln(red, la_ln_q_g, la_ln_q_b) @ la_wq
            q = q.reshape(b, hw, H8, DH).transpose(0, 2, 1, 3)
            kv = _ln(win, la_ln_kv_g, la_ln_kv_b) @ la_wkv
            kv = kv.reshape(b, hw, N, 2, H8, DH).transpose(3, 0, 4, 1, 2, 5)
            k_, v_ = (kv[0], kv[1])
            attn = jax.nn.softmax(jnp.einsum('bhnd,bhnkd->bhnk', q * scale, k_), axis=-1)
            agg = jnp.einsum('bhnk,bhnkd->bhnd', attn, v_)
            agg = agg.transpose(0, 2, 1, 3).reshape(b, hw, C)
            local_out = red + agg @ la_proj_w + la_proj_b
            cls = jnp.broadcast_to(class_emb, (b, 1, C))
            gq = (_ln(cls, ga_ln_q_g, ga_ln_q_b) @ ga_wq).reshape(b, H8, DH)
            gkv = _ln(local_out, ga_ln_kv_g, ga_ln_kv_b) @ ga_wkv
            gkv = gkv.reshape(b, hw, 2, H8, DH).transpose(2, 0, 3, 1, 4)
            gk, gv = (gkv[0], gkv[1])
            gattn = jax.nn.softmax(jnp.einsum('bhd,bhnd->bhn', gq * scale, gk), axis=-1)
            gagg = jnp.einsum('bhn,bhnd->bhd', gattn, gv).reshape(b, 1, C)
            cls_out = cls + gagg @ ga_proj_w + ga_proj_b
            patch_out = local_out @ mod_w + mod_b
            return jnp.concatenate([patch_out, cls_out], axis=1)
        del pixel_masks
        return _forward(pixel_values, conv_w, class_emb, la_ln_q_g, la_ln_q_b, la_wq, la_ln_kv_g, la_ln_kv_b, la_wkv, la_proj_w, la_proj_b, ga_ln_q_g, ga_ln_q_b, ga_wq, ga_ln_kv_g, ga_ln_kv_b, ga_wkv, ga_proj_w, ga_proj_b, mod_w, mod_b)

    def _L0_attn_ref(x, w_qkv, b_qkv, w_out, b_out):
        import jax, jax.numpy as jnp
        import numpy as np
        ALPHA = 1.2
        A = 1.0
        BANDWIDTH = 1.0
        D_INTRINSIC = 2
        SPHERE_RADIUS = 1.0
        NUM_HEADS = 16
        HIDDEN = 256
        HEAD_DIM = HIDDEN // NUM_HEADS
        EPS = 1e-07

        def _l2norm(t):
            n = jnp.sqrt(jnp.sum(t * t, axis=-1, keepdims=True))
            return t / jnp.maximum(n, 1e-12)
        B, S, H = x.shape
        qkv = x @ w_qkv.T + b_qkv
        q, k, v = jnp.split(qkv, 3, axis=-1)
        to_heads = lambda t: t.reshape(B, S, NUM_HEADS, HEAD_DIM).transpose(0, 2, 1, 3)
        q = _l2norm(to_heads(q))
        k = _l2norm(to_heads(k))
        v = to_heads(v)
        cos = jnp.einsum('bhsd,bhtd->bhst', q, k)
        g_dist = jnp.arccos(jnp.clip(cos, -1.0 + EPS, 1.0 - EPS)) * SPHERE_RADIUS
        attn_score = (1.0 + g_dist / BANDWIDTH ** 0.5) ** (-D_INTRINSIC - ALPHA)
        n_r = jnp.sum(attn_score, axis=-1)
        n_c = jnp.sum(attn_score, axis=-2)
        k_tilde = (n_r ** (-A))[..., :, None] * attn_score * (n_c ** (-A))[..., None, :]
        probs = k_tilde / jnp.maximum(jnp.sum(k_tilde, axis=-1, keepdims=True), 1e-12)
        out = jnp.einsum('bhst,bhtd->bhsd', probs, v)
        out = out.transpose(0, 2, 1, 3).reshape(B, S, H)
        return out @ w_out.T + b_out

    def _L0_ffn_ref(x, w_gate, w_up, w_down):
        import jax, jax.numpy as jnp
        import numpy as np
        DIM = 256
        HIDDEN = 768
        SCALE = 1.0 / 127.0

        def _dequant(w_int, dtype):
            return w_int.astype(dtype) * jnp.asarray(SCALE, dtype)
        wg = _dequant(w_gate, x.dtype)
        wu = _dequant(w_up, x.dtype)
        wd = _dequant(w_down, x.dtype)
        gate = jnp.einsum('bsd,hd->bsh', x, wg)
        up = jnp.einsum('bsd,hd->bsh', x, wu)
        h = jax.nn.silu(gate) * up
        return jnp.einsum('bsh,dh->bsd', h, wd)
    h = _L0_tok_ref(x, L0_tok_pixel_masks, L0_tok_conv_w, L0_tok_class_emb, L0_tok_la_ln_q_g, L0_tok_la_ln_q_b, L0_tok_la_wq, L0_tok_la_ln_kv_g, L0_tok_la_ln_kv_b, L0_tok_la_wkv, L0_tok_la_proj_w, L0_tok_la_proj_b, L0_tok_ga_ln_q_g, L0_tok_ga_ln_q_b, L0_tok_ga_wq, L0_tok_ga_ln_kv_g, L0_tok_ga_ln_kv_b, L0_tok_ga_wkv, L0_tok_ga_proj_w, L0_tok_ga_proj_b, L0_tok_mod_w, L0_tok_mod_b)
    h = jnp.concatenate([h, txt], axis=1)
    h = h + _L0_attn_ref(_layernorm(h, axis=-1), L0_attn_w_qkv, L0_attn_b_qkv, L0_attn_w_out, L0_attn_b_out)
    h = h + _L0_ffn_ref(_layernorm(h, axis=-1), L0_ffn_w_gate, L0_ffn_w_up, L0_ffn_w_down)
    return h

_drawn_inputs = setup_inputs


def setup_inputs(seed=0):
    import zlib

    import numpy as np

    out = dict(_drawn_inputs(seed))
    spreads = {'L0_tok_pixel_masks': (1.0, 0.2),
     'L0_tok_la_ln_q_g': (1.0, 0.6),
     'L0_tok_la_ln_q_b': (0.0, 2.0),
     'L0_tok_la_ln_kv_g': (1.0, 0.6),
     'L0_tok_la_ln_kv_b': (0.0, 0.8),
     'L0_tok_la_proj_b': (0.0, 0.1),
     'L0_tok_ga_ln_q_g': (1.0, 0.6),
     'L0_tok_ga_ln_q_b': (0.0, 2.0),
     'L0_tok_ga_ln_kv_g': (1.0, 0.6),
     'L0_tok_ga_ln_kv_b': (0.0, 0.748),
     'L0_tok_ga_proj_b': (0.0, 0.1),
     'L0_tok_mod_b': (0.0, 0.1),
     'L0_attn_b_qkv': (0.0, 0.1),
     'L0_attn_b_out': (0.0, 0.1)}
    factors = {'L0_tok_class_emb': 2.729, 'L0_tok_la_wq': 8.0, 'L0_tok_ga_wq': 27.42}
    for name, (base, spread) in spreads.items():
        noise = np.random.default_rng([zlib.crc32(name.encode()), seed]).standard_normal(out[name].shape)
        drawn = base * np.exp(spread * noise) if base else spread * noise
        out[name] = jnp.asarray(drawn.astype(out[name].dtype))
    for name, factor in factors.items():
        out[name] = (out[name] * factor).astype(out[name].dtype)
    return out
```

```python
import math
from contextlib import ExitStack

import concourse.bass as bass
from concourse import mybir

F32 = mybir.dt.float32
I32 = mybir.dt.int32
ALU = mybir.AluOpType
ACT = mybir.ActivationFunctionType
AX = mybir.AxisListType

P = 128
C = 256
CK = C // P
B = 64

H8, DH = 8, 32
WIN = 9
NW = 4
RT = B * NW // P
NT = RT * WIN
KP, KN = 118, 5
PATCH = 3 * 14 * 14
KL = PATCH - KP * (KN - 1)
TOK_SCALE = C ** -0.5
LN_EPS = 1e-5

TXT = 77
S = NW + 1 + TXT
T = B * S
NH, HD = 16, 16
HID = 768
HK = HID // P
G = 8
NG = B // G
TG = G * S
HALF = TG // 2
SH = G // 2
ROWS = [0, 128, 256, 384, 512, TG - P]
NR = len(ROWS)
PAIR = 2 * S
SC = NH * S
VD = HD + 1
COS_EPS = 1e-7
POWER = -3.2
HALF_PI = 1.5707963267948966
N2_SCALE = 2.0 ** 30
N2_BIAS = 2.0 ** -63
N2_SHIFT = 15 * 0.6931471805599453
SCALE_Q = 1.0 / 127.0

LN_EXP = "natural_log_exp_and_others"
SIG_ATAN = "sigmoid_and_others"


class Names:

    def __init__(self, nc, stack):
        self.nc, self.stack = nc, stack

    def sb(self, name, *shape, dt=F32):
        return self.stack.enter_context(self.nc.sbuf_tensor(name, [P, *shape], dt))

    def sem(self, name):
        return self.stack.enter_context(self.nc.semaphore(name))


class Weights:

    def __init__(self, mem):
        self.ident = mem.sb("ident", P)
        self.head_sum = mem.sb("head_sum", P)
        self.head_row = mem.sb("head_row", 2)
        self.q_bias = mem.sb("q_bias", 4)
        self.q_bias_m = mem.sb("q_bias_m", 2, 2)
        self.qk = mem.sb("w_qk", CK, 2 * C)
        self.v = mem.sb("w_v", CK, C)
        self.v_bias = mem.sb("v_bias", C)
        self.out = mem.sb("w_out", CK, C)
        self.out_bias = mem.sb("out_bias", C)
        self.gu = mem.sb("w_gate_up", CK, 2 * HID)
        self.d = mem.sb("w_down", HK, C)


def tokenizer(nc, a, w, ps, h_all):
    with ExitStack() as stack:
        mem = Names(nc, stack)
        sb, sem = mem.sb, mem.sem
        patches = sb("patches", KN, NT * P)
        ints = patches[:].rearrange("p k n -> p (k n)").bitcast(I32)
        gu_int = ints[:, 0:CK * 2 * HID].rearrange("p (k n) -> p k n", k=CK)
        d_int = ints[:, CK * 2 * HID:CK * 2 * HID + HK * C].rearrange("p (k n) -> p k n", k=HK)
        used = [CK * 2 * HID + HK * C]

        def late(*shape):
            n = math.prod(shape)
            view = patches[:].rearrange("p k n -> p (k n)")[:, used[0]:used[0] + n]
            used[0] += n
            assert used[0] <= KN * NT * P
            names = "abc"[:len(shape)]
            spec = f"p ({' '.join(names)}) -> p {' '.join(names)}"
            return view.rearrange(spec, **dict(zip(names[:-1], shape[:-1])))

        conv_w = sb("conv_w", KN, C)
        pe = sb("pe", NT, C)
        hat = sb("hat", NT, C)
        kvT = sb("kvT", 4, CK, P)
        kv = sb("kv", NT, 2 * C)
        wq, wkv, wproj = sb("la_wq", CK, C), sb("la_wkv", CK, 2 * C), sb("la_proj", CK, C)
        gwq, gwkv, gproj = sb("ga_wq", CK, C), sb("ga_wkv", CK, 2 * C), sb("ga_proj", CK, C)
        mod = sb("mod_w", CK, C)
        gains = sb("gains", 8, CK)
        rows = sb("rows", 4, C)
        ones = sb("ones_row", P)
        pick = sb("pick", B)
        cls_in = sb("cls_in", C)
        st = sb("patch_stats", NT, 6)
        mv = sb("patch_mv", NT, 2)
        rstd = sb("patch_rstd", NT)
        red = sb("red", RT, C)
        rst, rmv, rrs = sb("red_stats", RT, 6), sb("red_mv", RT, 2), sb("red_rstd", RT)
        rhat = sb("red_hat", RT, C)
        rT = sb("redT", RT, CK, P)
        q = late(RT, C)
        s = sb("s", RT, WIN, H8)
        smax = sb("smax", RT, H8)
        den = sb("den", RT, H8)
        agg = late(RT, C)
        aggT = late(RT, CK, P)
        lo = late(RT, C)
        loT = late(RT, CK, P)
        patch_out = late(RT, C)
        lst, lmv, lrs = sb("lo_stats", RT, 6), sb("lo_mv", RT, 2), sb("lo_rstd", RT)
        lhat = late(RT, C)
        lhT = late(RT, CK, P)
        gkv = late(RT, 2 * C)
        cst, cmv, crs = sb("cls_stats", 6), sb("cls_mv", 2), sb("cls_rstd", 1)
        chat = sb("cls_hat", C)
        cT = sb("cls_hatT", CK, P)
        gq = late(C)
        gprod = late(RT, C)
        gs = sb("gs", RT, H8)
        gsT = late(RT * P)
        gm, gd = sb("gmax", B), sb("gden", B)
        gp = sb("gp", RT, H8)
        gaT = late(CK, B)
        cls_out = late(C)

        conv_loaded, weights_loaded, main_loaded = sem("conv_loaded"), sem("weights_loaded"), sem("main_loaded")
        patches_loaded = [sem(f"patches_loaded_{j}") for j in range(RT)]
        txt_copied, tok_stored = sem("txt_copied"), sem("tok_stored")
        consts = sem("consts")
        conv_done, pe_ready = sem("conv_done"), sem("pe_ready")
        hat_done, tr_done, kvT_ready = sem("hat_done"), sem("tr_done"), sem("kvT_ready")
        kv_done, kv_ready = sem("kv_done"), sem("kv_ready")
        rstd_ready = sem("rstd_ready")
        red_mv_ready, red_rstd_ready, red_hat_ready = sem("red_mv_ready"), sem("red_rstd_ready"), sem("red_hat_ready")
        mv_ready = sem("mv_ready")
        red_tr, red_T, q_done, q_ready = sem("red_tr"), sem("red_T"), sem("q_done"), sem("q_ready")
        qk_prod, s_ready, e_ready, p_ready = sem("qk_prod"), sem("s_ready"), sem("e_ready"), sem("p_ready")
        pv_prod, agg_ready, agg_tr, agg_T = sem("pv_prod"), sem("agg_ready"), sem("agg_tr"), sem("agg_T")
        proj_done, lo_ready, lo_tr, lo_T = sem("proj_done"), sem("lo_ready"), sem("lo_tr"), sem("lo_T")
        patch_done, patch_ready = sem("patch_done"), sem("patch_ready")
        lo_mv_ready, lo_rstd_ready, lo_hat_ready = sem("lo_mv_ready"), sem("lo_rstd_ready"), sem("lo_hat_ready")
        lh_tr, lh_T, gkv_done, gkv_ready = sem("lh_tr"), sem("lh_T"), sem("gkv_done"), sem("gkv_ready")
        cls_mv_ready, cls_rstd_ready, cls_hat_ready = sem("cls_mv_ready"), sem("cls_rstd_ready"), sem("cls_hat_ready")
        cls_tr, cls_T, gq_done, gq_ready = sem("cls_tr"), sem("cls_T"), sem("gq_done"), sem("gq_ready")
        gk_prod, gs_ready, gs_tr, gs_T = sem("gk_prod"), sem("gs_ready"), sem("gs_tr"), sem("gs_T")
        ge_ready, gp_T, gp_tr, gp_ready = sem("ge_ready"), sem("gp_T"), sem("gp_tr"), sem("gp_ready")
        gv_prod, ga_done, ga_T, cls_done, cls_ready = (
            sem("gv_prod"), sem("ga_done"), sem("ga_T"), sem("cls_done"), sem("cls_ready"))
        act_step = sem("act_step")
        dve_step = sem("dve_step")
        block = stack.enter_context(nc.Block())

        def cols(bank, c, n):
            return ps[:, bank, c:c + n]

        @block.sync
        def _(sync):
            def patch_load(j):
                c0, c1 = j * WIN * P, (j + 1) * WIN * P
                sync.dma_start(patches[0:KP, 0:KN - 1, c0:c1],
                               a["patches"][0:KP * (KN - 1), c0:c1].rearrange("(k p) n -> p k n", p=KP)
                               ).then_inc(patches_loaded[j], 16)
                sync.dma_start(patches[0:KL, KN - 1, c0:c1], a["patches"][KP * (KN - 1):PATCH, c0:c1]
                               ).then_inc(patches_loaded[j], 16)

            sync.dma_start(conv_w[0:KP, 0:KN - 1, :],
                           a["conv_w"][0:KP * (KN - 1), :].rearrange("(k p) n -> p k n", p=KP)).then_inc(conv_loaded, 16)
            sync.dma_start(conv_w[0:KL, KN - 1, :], a["conv_w"][KP * (KN - 1):PATCH, :]).then_inc(conv_loaded, 16)
            patch_load(0)
            patch_load(1)
            sync.dma_start(h_all[:, NW + 1:S, :], a["txt"]).then_inc(txt_copied, 16)
            sync.wait_ge(patch_ready, RT)
            for j in range(RT):
                for hx in range(2):
                    sync.dma_start(h_all[:, 2 * j + hx, :], patch_out[64 * hx:64 * hx + B, j, :]).then_inc(tok_stored, 16)
            sync.wait_ge(cls_ready, 1)
            sync.dma_start(h_all[:, NW, :], cls_out[0:B, :]).then_inc(tok_stored, 16)
            sync.wait_ge(tok_stored, 16 * (2 * RT + 1))
            sync.wait_ge(txt_copied, 16)

        @block.gpsimd
        def _(pool):
            pool.memset(ones[:], 1.0).then_inc(consts, 1)
            pool.dma_start(w.ident[:], a["ident"]).then_inc(weights_loaded, 16)
            pool.dma_start(pick[:], a["pick"]).then_inc(weights_loaded, 16)
            for dst, src in ((wkv[:], a["la_wkv"]), (wq[:], a["la_wq"]), (gwq[:], a["ga_wq"]), (wproj[:], a["la_proj_w"]),
                             (mod[:], a["mod_w"]), (gwkv[:], a["ga_wkv"]), (gproj[:], a["ga_proj_w"])):
                pool.dma_start(dst, src.rearrange("(k p) n -> p k n", p=P)).then_inc(weights_loaded, 16)
            pool.dma_start(gains[:], a["gains"]).then_inc(weights_loaded, 16)
            pool.dma_start(rows[0:1], a["rows"]).then_inc(weights_loaded, 16)
            pool.dma_start(cls_in[:], a["class_emb"].partition_broadcast(P)).then_inc(weights_loaded, 16)
            for dst, src in ((w.qk[:], a["w_qk"]), (w.v[:], a["w_v"]), (w.out[:], a["w_out"]),
                             (gu_int[:, :, 0:HID], a["w_gate"]), (gu_int[:, :, HID:2 * HID], a["w_up"]),
                             (d_int, a["w_down"])):
                if src is a["w_gate"]:
                    pool.wait_ge(conv_done, NT)
                pool.dma_start(dst, src.rearrange("(k p) n -> p k n", p=P)).then_inc(main_loaded, 16)
            pool.dma_start(w.q_bias[:], a["b_qk"]).then_inc(main_loaded, 16)
            pool.dma_start(w.head_row[:], a["head_row"]).then_inc(main_loaded, 16)
            pool.dma_start(w.head_sum[:], a["head_sum"]).then_inc(main_loaded, 16)
            pool.dma_start(w.v_bias[:], a["b_v"].partition_broadcast(P)).then_inc(main_loaded, 16)
            pool.dma_start(w.out_bias[:], a["b_out"].partition_broadcast(P)).then_inc(main_loaded, 16)
            pool.wait_ge(kv_ready, WIN)
            for j in range(RT):
                t0, t1 = j * WIN, (j + 1) * WIN
                pool.wait_ge(kv_ready, t1)
                pool.wait_ge(q_ready, j + 1)
                pool.wait_ge(tr_done, t1)
                pool.tensor_tensor(hat[:, t0:t1, :], kv[:, t0:t1, 0:C],
                                   q[:, j:j + 1, :].to_broadcast([P, WIN, C]), ALU.mult).then_inc(qk_prod, 1)
            for j in range(RT):
                t0, t1 = j * WIN, (j + 1) * WIN
                pool.wait_ge(p_ready, j + 1)
                pool.tensor_tensor(
                    hat[:, t0:t1, :].rearrange("p n (h d) -> p (n h) d", d=DH),
                    kv[:, t0:t1, C:2 * C].rearrange("p n (h d) -> p n h d", d=DH),
                    s[:, j, :, :].unsqueeze(3).to_broadcast([P, WIN, H8, DH]), ALU.mult).then_inc(pv_prod, 1)
            for j in range(RT):
                pool.wait_ge(gkv_ready, j + 1)
                pool.wait_ge(gq_ready, 1)
                pool.tensor_tensor(gprod[:, j, :], gkv[:, j, 0:C], gq[:], ALU.mult).then_inc(gk_prod, 1)
            for j in range(RT):
                pool.wait_ge(gp_ready, j + 1)
                pool.tensor_tensor(gprod[:, j, :].rearrange("p (h d) -> p h d", d=DH),
                                   gkv[:, j, C:2 * C].rearrange("p (h d) -> p h d", d=DH),
                                   gp[:, j, :].unsqueeze(2).to_broadcast([P, H8, DH]), ALU.mult).then_inc(gv_prod, 1)

        @block.scalar
        def _(act):
            act.preload_act_table_set(LN_EXP)

            act_count = [0]

            def rsqrt(dst, var, got, n, done):
                act.wait_ge(got, n)
                act.activation(dst, var, ACT.Ln, bias=LN_EPS).then_inc(act_step, 1)
                act_count[0] += 1
                act.wait_ge(act_step, act_count[0])
                act.activation(dst, dst, ACT.Exp, scale=-0.5).then_inc(done, 1)

            def evac_pe(t):
                act.wait_ge(conv_done, t + 1)
                act.activation(pe[:, t, :], cols(t % 4, 0, C), ACT.Copy).then_inc(pe_ready, 1)

            def evac_kv(t):
                act.wait_ge(kv_done, t + 1)
                act.activation(kv[:, t, :], cols(6 + t % 2, 0, 2 * C), ACT.Copy).then_inc(kv_ready, 1)

            for t in range(WIN):
                evac_pe(t)
            rsqrt(rstd[:, 0:WIN], mv[:, 0:WIN, 1], mv_ready, 1, rstd_ready)
            rsqrt(rrs[:, 0:1], rmv[:, 0, 1:2], red_mv_ready, 1, red_rstd_ready)
            rsqrt(crs[:], cmv[:, 1:2], cls_mv_ready, 1, cls_rstd_ready)
            for t in range(WIN, NT):
                evac_pe(t)
            rsqrt(rstd[:, WIN:NT], mv[:, WIN:NT, 1], mv_ready, 2, rstd_ready)
            rsqrt(rrs[:, 1:2], rmv[:, 1, 1:2], red_mv_ready, 2, red_rstd_ready)
            for t in range(NT):
                evac_kv(t)
            for j in range(RT):
                act.wait_ge(q_done, j + 1)
                act.activation(q[:, j, :], cols(j, 0, C), ACT.Copy, scale=TOK_SCALE).then_inc(q_ready, 1)
            act.wait_ge(gq_done, 1)
            act.activation(gq[:], cols(2, 0, C), ACT.Copy, scale=TOK_SCALE).then_inc(gq_ready, 1)
            for j in range(RT):
                act.wait_ge(s_ready, j + 1)
                act.activation(s[:, j], s[:, j], ACT.Exp).then_inc(e_ready, 1)
            for j in range(RT):
                rsqrt(lrs[:, j:j + 1], lmv[:, j, 1:2], lo_mv_ready, j + 1, lo_rstd_ready)
            for j in range(RT):
                act.wait_ge(patch_done, j + 1)
                act.activation(patch_out[:, j, :], cols(2 + j, 0, C), ACT.Copy).then_inc(patch_ready, 1)
            for j in range(RT):
                act.wait_ge(gkv_done, j + 1)
                act.activation(gkv[:, j, :], cols(4 + j, 0, 2 * C), ACT.Copy).then_inc(gkv_ready, 1)
            act.wait_ge(gs_T, 1)
            act.activation(gsT[0:H8, :], gsT[0:H8, :], ACT.Exp).then_inc(ge_ready, 1)

        @block.vector
        def _(dve):
            count = [0]

            def link(ins):
                count[0] += 1
                ins.then_inc(dve_step, 1)
                dve.wait_ge(dve_step, count[0])

            def step(ins):
                count[0] += 1
                ins.then_inc(dve_step, 1)

            def stats(st_, mv_, x, done):
                link(dve.bn_stats(st_, x))
                dve.bn_aggr(mv_, st_).then_inc(done, 1)

            def patch_stats(j):
                for t in range(j * WIN, (j + 1) * WIN):
                    dve.wait_ge(pe_ready, t + 1)
                    step(dve.bn_stats(st[:, t, :], pe[:, t, :]))
                dve.wait_ge(dve_step, count[0])
                for t in range(j * WIN, (j + 1) * WIN):
                    last = dve.bn_aggr(mv[:, t, :], st[:, t, :])
                    step(last) if t < (j + 1) * WIN - 1 else last.then_inc(mv_ready, 1)

            def patch_hats(j):
                dve.wait_ge(rstd_ready, j + 1)
                dve.wait_ge(mv_ready, j + 1)
                for t in range(j * WIN, (j + 1) * WIN):
                    dve.tensor_scalar(hat[:, t, :], pe[:, t, :], mv[:, t, 0:1], rstd[:, t:t + 1],
                                      ALU.subtract, ALU.mult).then_inc(hat_done, 1)

            def window_mean(j):
                link(dve.tensor_reduce(red[:, j, :], pe[:, j * WIN:(j + 1) * WIN, :].rearrange("p n c -> p c n"),
                                       AX.X, ALU.add))
                link(dve.tensor_scalar(red[:, j, :], red[:, j, :], 1.0 / WIN, None, ALU.mult))
                stats(rst[:, j, :], rmv[:, j, :], red[:, j, :], red_mv_ready)

            def gained(dst, bank, c0, gb):
                for c in range(CK):
                    ins = dve.tensor_scalar(dst[:, c, :], cols(bank, c0 + c * P, P), gains[:, gb, c:c + 1],
                                            gains[:, gb + 1, c:c + 1], ALU.mult, ALU.add)
                    if c < CK - 1:
                        step(ins)
                return ins

            def kvT_tile(t):
                dve.wait_ge(tr_done, t + 1)
                if t >= 4:
                    dve.wait_ge(kv_done, t - 3)
                gained(kvT[:, t % 4], 4 + t % 2, 0, 2).then_inc(kvT_ready, 1)

            patch_stats(0)
            window_mean(0)
            dve.wait_ge(weights_loaded, 16 * 12)
            stats(cst[:], cmv[:], cls_in[:], cls_mv_ready)
            patch_hats(0)
            dve.wait_ge(red_rstd_ready, 1)
            dve.wait_ge(red_mv_ready, 1)
            dve.tensor_scalar(rhat[:, 0, :], red[:, 0, :], rmv[:, 0, 0:1], rrs[:, 0:1], ALU.subtract, ALU.mult
                              ).then_inc(red_hat_ready, 1)
            dve.wait_ge(cls_rstd_ready, 1)
            dve.wait_ge(cls_mv_ready, 1)
            dve.tensor_scalar(chat[:], cls_in[:], cmv[:, 0:1], crs[:, 0:1], ALU.subtract, ALU.mult
                              ).then_inc(cls_hat_ready, 1)
            patch_stats(1)
            window_mean(1)
            for t in range(WIN):
                kvT_tile(t)
            patch_hats(1)
            dve.wait_ge(red_rstd_ready, 2)
            dve.wait_ge(red_mv_ready, 2)
            dve.tensor_scalar(rhat[:, 1, :], red[:, 1, :], rmv[:, 1, 0:1], rrs[:, 1:2], ALU.subtract, ALU.mult
                              ).then_inc(red_hat_ready, 1)
            for t in range(WIN, NT):
                kvT_tile(t)
            for j in range(RT):
                dve.wait_ge(red_tr, j + 1)
                gained(rT[:, j], 4 + j, 0, 0).then_inc(red_T, 1)
            dve.wait_ge(cls_tr, 1)
            gained(cT, 4, C, 4).then_inc(cls_T, 1)
            for j in range(RT):
                dve.wait_ge(qk_prod, j + 1)
                t0, t1 = j * WIN, (j + 1) * WIN
                link(dve.tensor_reduce(s[:, j].rearrange("p n h -> p (n h)"),
                                       hat[:, t0:t1, :].rearrange("p n (h d) -> p (n h) d", d=DH), AX.X, ALU.add))
                link(dve.tensor_reduce(smax[:, j, :], s[:, j].rearrange("p n h -> p h n"), AX.X, ALU.max))
                dve.tensor_tensor(s[:, j], s[:, j], smax[:, j:j + 1, :].to_broadcast([P, WIN, H8]), ALU.subtract
                                  ).then_inc(s_ready, 1)
            for j in range(RT):
                dve.wait_ge(e_ready, j + 1)
                link(dve.tensor_reduce(den[:, j, :], s[:, j].rearrange("p n h -> p h n"), AX.X, ALU.add))
                link(dve.reciprocal(den[:, j, :], den[:, j, :]))
                dve.tensor_tensor(s[:, j], s[:, j], den[:, j:j + 1, :].to_broadcast([P, WIN, H8]), ALU.mult
                                  ).then_inc(p_ready, 1)
            for j in range(RT):
                dve.wait_ge(pv_prod, j + 1)
                dve.tensor_reduce(agg[:, j, :], hat[:, j * WIN:(j + 1) * WIN, :].rearrange("p n c -> p c n"),
                                  AX.X, ALU.add).then_inc(agg_ready, 1)
            for j in range(RT):
                dve.wait_ge(agg_tr, j + 1)
                dve.tensor_copy(aggT[:, j].rearrange("p c n -> p (c n)"), cols(4 + j, 0, C)).then_inc(agg_T, 1)
            for j in range(RT):
                dve.wait_ge(proj_done, j + 1)
                dve.tensor_tensor(lo[:, j, :], cols(j, 0, C), red[:, j, :], ALU.add).then_inc(lo_ready, 1)
                dve.wait_ge(lo_ready, j + 1)
                stats(lst[:, j, :], lmv[:, j, :], lo[:, j, :], lo_mv_ready)
            for j in range(RT):
                dve.wait_ge(lo_rstd_ready, j + 1)
                dve.wait_ge(lo_mv_ready, j + 1)
                dve.tensor_scalar(lhat[:, j, :], lo[:, j, :], lmv[:, j, 0:1], lrs[:, j:j + 1], ALU.subtract, ALU.mult
                                  ).then_inc(lo_hat_ready, 1)
            for j in range(RT):
                dve.wait_ge(lo_tr, j + 1)
                dve.tensor_copy(loT[:, j].rearrange("p c n -> p (c n)"), cols(4 + j, 0, C)).then_inc(lo_T, 1)
            for j in range(RT):
                dve.wait_ge(lh_tr, j + 1)
                gained(lhT[:, j], 6 + j, 0, 6).then_inc(lh_T, 1)
            for j in range(RT):
                dve.wait_ge(gk_prod, j + 1)
                dve.tensor_reduce(gs[:, j, :], gprod[:, j, :].rearrange("p (h d) -> p h d", d=DH), AX.X, ALU.add
                                  ).then_inc(gs_ready, 1)
            dve.wait_ge(gs_tr, 1)
            scores = cols(6, 0, RT * P)[0:H8]
            by_sample = scores.rearrange("p (w b) -> p b w", b=B)
            link(dve.tensor_reduce(gm[0:H8, :], by_sample, AX.X, ALU.max))
            dve.tensor_tensor(gsT[0:H8, :].rearrange("p (w b) -> p w b", b=B),
                              scores.rearrange("p (w b) -> p w b", b=B),
                              gm[0:H8, :].unsqueeze(1).to_broadcast([H8, NW, B]), ALU.subtract).then_inc(gs_T, 1)
            dve.wait_ge(ge_ready, 1)
            link(dve.tensor_reduce(gd[0:H8, :], gsT[0:H8, :].rearrange("p (w b) -> p b w", b=B), AX.X, ALU.add))
            link(dve.reciprocal(gd[0:H8, :], gd[0:H8, :]))
            dve.tensor_tensor(gsT[0:H8, :].rearrange("p (w b) -> p w b", b=B),
                              gsT[0:H8, :].rearrange("p (w b) -> p w b", b=B),
                              gd[0:H8, :].unsqueeze(1).to_broadcast([H8, NW, B]), ALU.mult).then_inc(gp_T, 1)
            dve.wait_ge(gp_tr, 1)
            dve.tensor_copy(gp[:], cols(7, 0, RT * H8).rearrange("p (j h) -> p j h", h=H8)).then_inc(gp_ready, RT)
            dve.wait_ge(ga_done, 1)
            dve.tensor_copy(gaT[:], cols(0, 0, CK * B).rearrange("p (c b) -> p c b", b=B)).then_inc(ga_T, 1)
            dve.wait_ge(cls_done, 1)
            dve.tensor_copy(cls_out[0:B, :], cols(1, 0, C)[0:B]).then_inc(cls_ready, 1)
            dve.wait_ge(main_loaded, 16 * 11)
            for k in range(CK):
                step(dve.tensor_scalar(w.gu[:, k, :], gu_int[:, k, :], SCALE_Q, None, ALU.mult))
            step(dve.tensor_scalar(w.d[:], d_int, SCALE_Q, None, ALU.mult))
            for e in range(2):
                step(dve.tensor_scalar(w.q_bias_m[:, :, e], w.q_bias[:, 0:2], w.head_row[:, e:e + 1], None, ALU.mult))

        @block.tensor
        def _(pe_):
            def conv(t):
                pe_.wait_ge(patches_loaded[t // WIN], 32)
                if t >= 4:
                    pe_.wait_ge(pe_ready, t - 3)
                for k in range(KN):
                    kk = KP if k < KN - 1 else KL
                    last = pe_.matmul(cols(t % 4, 0, C), patches[0:kk, k, t * P:(t + 1) * P], conv_w[0:kk, k, :],
                                      start=(k == 0), stop=(k == KN - 1))
                last.then_inc(conv_done, 1)

            def transposes(bank, c0, src, done):
                for c in range(CK):
                    last = pe_.transpose(cols(bank, c0 + c * P, P), src[:, c * P:(c + 1) * P], w.ident[:])
                last.then_inc(done, 1)

            def tr(t):
                pe_.wait_ge(hat_done, t + 1)
                if t >= 2:
                    pe_.wait_ge(kvT_ready, t - 1)
                transposes(4 + t % 2, 0, hat[:, t, :], tr_done)

            def product(out, lhsT, rhs, done, bias=None, m=P):
                extra = [] if bias is None else bias
                for c in range(CK):
                    last = pe_.matmul(out, lhsT[:, c, :], rhs[:, c, :], start=(c == 0),
                                      stop=(c == CK - 1 and not extra))
                for n, r in enumerate(extra):
                    last = pe_.matmul(out, ones[0:1, 0:m], rows[0:1, r, :], start=False, stop=(n == len(extra) - 1))
                last.then_inc(done, 1)

            def kv_tile(t):
                pe_.wait_ge(kvT_ready, t + 1)
                if t >= 2:
                    pe_.wait_ge(kv_ready, t - 1)
                product(cols(6 + t % 2, 0, 2 * C), kvT[:, t % 4], wkv, kv_done)

            pe_.wait_ge(conv_loaded, 32)
            for t in range(NT):
                conv(t)
            pe_.wait_ge(consts, 1)
            pe_.wait_ge(weights_loaded, 16 * 12)
            tr(0)
            for t in range(NT):
                if t + 1 < NT:
                    tr(t + 1)
                kv_tile(t)
            pe_.wait_ge(kvT_ready, NT)
            for j in range(RT):
                pe_.wait_ge(red_hat_ready, j + 1)
                transposes(4 + j, 0, rhat[:, j, :], red_tr)
            pe_.wait_ge(cls_hat_ready, 1)
            pe_.wait_ge(red_T, 1)
            transposes(4, C, chat[:], cls_tr)
            pe_.wait_ge(pe_ready, NT)
            for j in range(RT):
                pe_.wait_ge(red_T, j + 1)
                product(cols(j, 0, C), rT[:, j], wq, q_done)
            pe_.wait_ge(cls_T, 1)
            product(cols(2, 0, C), cT, gwq, gq_done)
            for j in range(RT):
                pe_.wait_ge(agg_ready, j + 1)
                transposes(4 + j, 0, agg[:, j, :], agg_tr)
            for j in range(RT):
                pe_.wait_ge(agg_T, j + 1)
                pe_.wait_ge(q_ready, j + 1)
                product(cols(j, 0, C), aggT[:, j], wproj, proj_done, bias=[0])
            for j in range(RT):
                pe_.wait_ge(lo_ready, j + 1)
                transposes(4 + j, 0, lo[:, j, :], lo_tr)
            pe_.wait_ge(kv_ready, NT)
            for j in range(RT):
                pe_.wait_ge(lo_hat_ready, j + 1)
                transposes(6 + j, 0, lhat[:, j, :], lh_tr)
            pe_.wait_ge(gq_ready, 1)
            for j in range(RT):
                pe_.wait_ge(lo_T, j + 1)
                product(cols(2 + j, 0, C), loT[:, j], mod, patch_done, bias=[1])
            for j in range(RT):
                pe_.wait_ge(lh_T, j + 1)
                product(cols(4 + j, 0, 2 * C), lhT[:, j], gwkv, gkv_done)
            for j in range(RT):
                pe_.wait_ge(gs_ready, j + 1)
                last = pe_.transpose(cols(6, j * P, P)[0:H8], gs[:, j, :], w.ident[:])
            last.then_inc(gs_tr, 1)
            pe_.wait_ge(gp_T, 1)
            for j in range(RT):
                last = pe_.transpose(cols(7, j * H8, H8), gsT[0:H8, j * P:(j + 1) * P], w.ident[0:H8, 0:H8])
            last.then_inc(gp_tr, 1)
            pe_.wait_ge(lo_ready, RT)
            pe_.wait_ge(gv_prod, RT)
            for c in range(CK):
                for j in range(RT):
                    last = pe_.matmul(cols(0, c * B, B), gprod[:, j, c * P:(c + 1) * P], pick[:],
                                      start=(j == 0), stop=(j == RT - 1))
            last.then_inc(ga_done, 1)
            pe_.wait_ge(ga_T, 1)
            product(cols(1, 0, C)[0:B], gaT, gproj, cls_done, bias=[2, 3], m=B)


def transformer(nc, a, w, ps, h_all, out):
    with ExitStack() as stack:
        mem = Names(nc, stack)
        sb, sem = mem.sb, mem.sem
        h_in = sb("h_in", NR, C)
        h_bias = sb("h_bias", NR, C)
        h2 = sb("h2", NR, C)
        x1, x2 = sb("x1", NR, C), sb("x2", NR, C)
        x1T, x2T = sb("x1T", CK, TG), sb("x2T", CK, TG)
        stats = sb("stats", NR, 6)
        mv1, mv2 = sb("mv1", NR, 2), sb("mv2", NR, 2)
        rstd1, rstd2 = sb("rstd1", NR), sb("rstd2", NR)
        qT = sb("qT", CK, 2, TG)
        kT = sb("kT", CK, TG)
        sq = sb("sq", 2, HALF)
        inv = sb("inv_norm", 3, HALF)
        vw = sb("v_weighted", G, NH, VD)
        sc = sb("scores", G, SC)
        lnp = sb("ln_one_plus_cos", 3, SC)
        mass = sb("key_mass", 2, 2 * NH)
        osum = sb("o_sum", 2, NH)
        o = sb("o", 2, C)
        oT = sb("oT", CK, TG)
        hid = sb("hidden", HK, TG)
        sig = sb("sigmoid", 2, HALF)
        act_gate = sb("silu_gate", 2, HALF)

        h_loaded = sem("h_loaded")
        hb_ready = sem("hb_ready")
        mv1_ready, mv2_ready = sem("mv1_ready"), sem("mv2_ready")
        rstd1_ready, rstd2_ready = sem("rstd1_ready"), sem("rstd2_ready")
        x1_ready, x2_ready = sem("x1_ready"), sem("x2_ready")
        x1_tr, x2_tr = sem("x1_tr"), sem("x2_tr")
        x1T_ready, x2T_ready = sem("x1T_ready"), sem("x2T_ready")
        v_done, v_ready = sem("v_done"), sem("v_ready")
        qk_done, sq_ready, raw_ready = sem("qk_done"), sem("sq_ready"), sem("raw_ready")
        n2_done, n2_ln, inv_ready, qk_ready = sem("n2_done"), sem("n2_ln"), sem("inv_ready"), sem("qk_ready")
        s_done, clip_ready = sem("s_done"), sem("clip_ready")
        ln_ready, x_ready = sem("ln_ready"), sem("x_ready")
        tanh_ready, atan_ready = sem("tanh_ready"), sem("atan_ready")
        ln_g, a_ready = sem("ln_g"), sem("a_ready")
        mass_ready, rm_ready, vw_ready = sem("mass_ready"), sem("rm_ready"), sem("vw_ready")
        pv_done, osum_ready, orec_ready, o_ready = sem("pv_done"), sem("osum_ready"), sem("orec_ready"), sem("o_ready")
        o_tr = sem("o_tr")
        oT_ready = sem("oT_ready")
        op_done, h2_ready = sem("op_done"), sem("h2_ready")
        gu_done, sig_ready = sem("gu_done"), sem("sig_ready")
        gate_ready, hid_ready = sem("gate_ready"), sem("hid_ready")
        down_done, y_ready = sem("down_done"), sem("y_ready")
        stored = sem("stored")
        rstd_ln = sem("rstd_ln")
        block = stack.enter_context(nc.Block())

        HV = G // 2
        UNITS = 2 * HK

        STAGES = [("v", 4, 0, v_ready, 4), ("x2T", 3, -1, x2T_ready, 3), ("x1T", 3, 1, x1T_ready, 3),
                  ("qk", 16, 1, None, 8), ("gu", 24, -1, None, UNITS), ("down", NR, -1, y_ready, NR),
                  ("oT", 4, 0, oT_ready, 4)]
        JOBS = []
        for stage, n, off, read, per in STAGES:
            for i in range(n):
                if stage == "qk":
                    kind, u = QK_ORDER[i]
                    JOBS.append((stage, (kind, u), off, raw_ready if kind == "proj" else n2_ln, per, u))
                elif stage == "gu":
                    JOBS.append((stage, ("gate" if i % 2 == 0 else "up", i // 2), off,
                                 gate_ready if i % 2 == 0 else hid_ready, per, i // 2))
                else:
                    JOBS.append((stage, i, off, read, per, i))
        assert len(JOBS) % 4 == 0
        NUMBER = {(j[0], j[1]): n for n, j in enumerate(JOBS)}

        def runs(stage_off, first, last):
            return {-1: not first, 0: True, 1: not last}[stage_off]

        def claim(eng, it, before, now, stage, which):
            n = NUMBER[stage, which]
            bank, back, offs = 4 + n % 4, 0, now
            n -= 4
            while True:
                if n < 0:
                    if back:
                        return bank
                    n, back, offs = n + len(JOBS), 1, before
                _, _, off, read, per, i = JOBS[n]
                if off in offs:
                    eng.wait_ge(read, (it + off - back) * per + i + 1)
                    return bank
                n -= 4

        def bank(b, n, rows=P, c=0):
            return ps[0:rows, b, c:c + n]

        def iterate(eng, body, before_all, after_all):
            before_all()
            body(0, {1}, {0, 1})
            body(1, {0, 1}, {-1, 0, 1})
            with eng.Fori(2, NG - 1) as it:
                body(it, {-1, 0, 1}, {-1, 0, 1})
            body(NG - 1, {-1, 0, 1}, {-1, 0})
            after_all()

        @block.sync
        def _(sync):
            def load(g, first_row):
                rows = h_all.rearrange("b s c -> (b s) c")[first_row:first_row + TG] if isinstance(first_row, int) \
                    else h_all.rearrange("b s c -> (b s) c")[bass.ds(first_row, TG)]
                sync.dma_start(h_in[:, 0:NR - 1, :],
                               rows[0:P * (NR - 1)].rearrange("(t p) c -> p t c", p=P)).then_inc(h_loaded, 16)
                sync.dma_start(h_in[:, NR - 1, :], rows[TG - P:TG]).then_inc(h_loaded, 16)

            def store(tiles, first_row):
                dst = out.rearrange("b s c -> (b s) c")
                dst = dst[first_row:first_row + TG] if isinstance(first_row, int) else dst[bass.ds(first_row, TG)]
                sync.wait_ge(y_ready, tiles)
                sync.dma_start(dst[0:P * (NR - 1)].rearrange("(t p) c -> p t c", p=P), h2[:, 0:NR - 1, :]
                               ).then_inc(stored, 16)
                rest = TG - P * (NR - 1)
                sync.dma_start(dst[P * (NR - 1):TG], h2[P - rest:P, NR - 1, :]).then_inc(stored, 16)

            def body(it, before, now):
                if 1 in now:
                    sync.wait_ge(hb_ready, it + 1)
                    load(it + 1, (it + 1) * TG)
                if -1 in now:
                    store(it * NR, (it - 1) * TG)

            def after():
                store(NG * NR, (NG - 1) * TG)
                sync.wait_ge(stored, 32 * NG)

            iterate(sync, body, lambda: load(0, 0), after)

        @block.gpsimd
        def _(pool):
            def body(it, before, now):
                pool.wait_ge(x1_ready, (it + 1) * NR)
                if 0 in before:
                    pool.wait_ge(h2_ready, it * NR)
                pool.tensor_tensor(h_bias[:], h_in[:], w.out_bias[:].unsqueeze(1).to_broadcast([P, NR, C]), ALU.add
                                   ).then_inc(hb_ready, 1)
                for k in range(HV):
                    pool.wait_ge(rm_ready, it * HV + k + 1)
                    pair = vw[0:S, 2 * k:2 * k + 2].rearrange("p s h d -> p (s h) d")
                    pool.tensor_tensor(pair[:, :, 0:HD], pair[:, :, 0:HD],
                                       pair[:, :, HD:VD].to_broadcast([S, 2 * NH, HD]), ALU.mult).then_inc(vw_ready, 1)

            iterate(pool, body, lambda: None, lambda: None)

        @block.scalar
        def _(act):
            ln_count = [0]

            def rstd(dst, mv, got, g, done, order):
                act.wait_ge(got, g + 1)
                act.activation(dst[:], mv[:, :, 1], ACT.Ln, bias=LN_EPS).then_inc(rstd_ln, 1)
                act.wait_ge(rstd_ln, order)
                act.activation(dst[:], dst[:], ACT.Exp, scale=-0.5).then_inc(done, 1)

            def logs(it, s):
                act.wait_ge(clip_ready, it * 2 * G + 2 * s + 2)
                if s >= 3:
                    act.wait_ge(x_ready, it * G + s - 2)
                act.activation(lnp[0:S, s % 3, :], sc[0:S, s, :], ACT.Ln, bias=1.0)
                act.activation(sc[0:S, s, :], sc[0:S, s, :], ACT.Ln, bias=1.0, scale=-1.0).then_inc(ln_ready, 1)

            def qk_raw(g, u):
                f, hf = UNIT_OF[u]
                b = 4 + NUMBER["qk", ("proj", u)] % 4
                cols = slice(hf * HALF, (hf + 1) * HALF)
                act.wait_ge(qk_done, g * 8 + u + 1)
                if u >= 2:
                    act.wait_ge(n2_done, g * 8 + u - 1)
                act.activation(sq[:, u % 2, :], bank(b, HALF), ACT.Square, bias=w.q_bias[:, f:f + 1]
                               ).then_inc(sq_ready, 1)
                if f < CK:
                    for e in range(2):
                        last = act.activation(qT[:, f, e, cols], bank(b, HALF), ACT.Identity,
                                              bias=w.q_bias_m[:, f, e:e + 1], scale=w.head_row[:, e:e + 1])
                else:
                    last = act.activation(kT[:, f - CK, cols], bank(b, HALF), ACT.Identity, bias=w.q_bias[:, f:f + 1])
                last.then_inc(raw_ready, 1)

            def qk_norm(g, u):
                b = 4 + NUMBER["qk", ("norm", u)] % 4
                act.wait_ge(n2_done, g * 8 + u + 1)
                if u >= 3:
                    act.wait_ge(qk_ready, g * 8 + u - 2)
                act.activation(inv[:, u % 3, :], bank(b, HALF), ACT.Ln, bias=N2_BIAS, scale=N2_SCALE
                               ).then_inc(n2_ln, 1)
                act.wait_ge(n2_ln, g * 8 + u + 1)
                act.activation(inv[:, u % 3, :], inv[:, u % 3, :], ACT.Exp, bias=N2_SHIFT, scale=-0.5
                               ).then_inc(inv_ready, 1)

            def qk_units(g):
                for u in range(8):
                    qk_raw(g, u)
                    if u:
                        qk_norm(g, u - 1)
                    yield
                qk_norm(g, 7)
                yield

            def two(k):
                return sc[0:S, 2 * k:2 * k + 2, :]

            def angle_steps(it):
                for k in range(HV):
                    act.wait_ge(x_ready, it * G + 2 * k + 2)
                    act.activation(two(k), two(k), ACT.Tanh, scale=0.25).then_inc(tanh_ready, 1)
                    yield
                for k in range(HV):
                    act.wait_ge(tanh_ready, it * HV + k + 1)
                    act.activation(two(k), two(k), ACT.Arctan).then_inc(atan_ready, 1)
                    yield

            def sigmoid(g, u):
                b = 4 + NUMBER["gu", ("gate", u)] % 4
                act.wait_ge(gu_done, g * UNITS + u + 1)
                if u >= 2:
                    act.wait_ge(gate_ready, g * UNITS + u - 1)
                act.activation(sig[:, u % 2, :], bank(b, HALF), ACT.Sigmoid).then_inc(sig_ready, 1)

            def power(it, k, exp):
                if not exp:
                    act.wait_ge(atan_ready, it * HV + k + 1)
                    act.activation(two(k), two(k), ACT.Ln, bias=1.0 + HALF_PI, scale=-2.0).then_inc(ln_g, 1)
                else:
                    act.wait_ge(ln_g, it * HV + k + 1)
                    act.activation(two(k), two(k), ACT.Exp, scale=POWER).then_inc(a_ready, 1)

            def before_all():
                act.preload_act_table_set(LN_EXP)
                rstd(rstd1, mv1, mv1_ready, 0, rstd1_ready, 1)
                for _ in qk_units(0):
                    pass

            def body(it, before, now):
                if -1 in now:
                    rstd(rstd2, mv2, mv2_ready, it - 1, rstd2_ready, 2 * it + 1)
                logs(it, 0)
                logs(it, 1)
                if 1 in now:
                    rstd(rstd1, mv1, mv1_ready, it + 1, rstd1_ready, 2 * it + 2)
                for s in range(2, G - 2):
                    logs(it, s)
                units = qk_units(it + 1) if 1 in now else iter(())
                for n, _ in enumerate(units):
                    if n in (2, 5):
                        logs(it, G - 2 + n // 3)
                if 1 not in now:
                    logs(it, G - 2)
                    logs(it, G - 1)
                act.preload_act_table_set(SIG_ATAN)
                angles = angle_steps(it)
                next(angles)
                for u in range(UNITS if -1 in now else 0):
                    sigmoid(it - 1, u)
                    if u % 3 < 2:
                        next(angles, None)
                for _ in angles:
                    pass
                act.preload_act_table_set(LN_EXP)
                for k in range(HV):
                    power(it, k, False)
                    if k:
                        power(it, k - 1, True)
                power(it, HV - 1, True)
                for hf in range(2):
                    for c in range(CK):
                        i = hf * CK + c
                        act.wait_ge(o_tr, it * G + SH * (hf + 1))
                        act.activation(oT[:, c, hf * HALF:(hf + 1) * HALF],
                                       bank(4 + NUMBER["oT", i] % 4, HALF), ACT.Copy).then_inc(oT_ready, 1)

            def after():
                rstd(rstd2, mv2, mv2_ready, NG - 1, rstd2_ready, 2 * NG)
                act.preload_act_table_set(SIG_ATAN)
                for u in range(UNITS):
                    sigmoid(NG - 1, u)

            iterate(act, body, before_all, after)

        @block.vector
        def _(dve):
            def moments(h, mv, done):
                for t in range(NR):
                    last = dve.bn_stats(stats[:, t, :], h[:, t, :])
                dve.drain()
                for t in range(NR):
                    last = dve.bn_aggr(mv[:, t, :], stats[:, t, :])
                last.then_inc(done, 1)

            def moments1(g):
                dve.wait_ge(h_loaded, 32 * (g + 1))
                moments(h_in, mv1, mv1_ready)

            def moments2(g):
                dve.wait_ge(h2_ready, NR * (g + 1))
                moments(h2, mv2, mv2_ready)

            def normalise(x, h, mv, rs, mv_got, rs_got, g, done):
                dve.wait_ge(mv_got, g + 1)
                dve.wait_ge(rs_got, g + 1)
                for t in range(NR):
                    dve.tensor_scalar(x[:, t, :], h[:, t, :], mv[:, t, 0:1], rs[:, t:t + 1],
                                      ALU.subtract, ALU.mult).then_inc(done, 1)

            def turned(xT, stage, tr, ready, g):
                for n in range(3):
                    b = 4 + NUMBER[stage, n] % 4
                    dve.wait_ge(tr, g * 3 + n + 1)
                    if n < CK:
                        dve.tensor_copy(xT[:, n, 0:4 * P], bank(b, 4 * P)).then_inc(ready, 1)
                    else:
                        tail = bank(b, 4 * P).rearrange("p (c n) -> p c n", c=CK)
                        rest = TG - 5 * P
                        dve.tensor_copy(xT[:, :, 4 * P:5 * P], tail[:, :, 0:P])
                        dve.tensor_copy(xT[:, :, 5 * P:TG], tail[:, :, 2 * P - rest:2 * P]).then_inc(ready, 1)

            def values(it, k):
                b = 4 + NUMBER["v", k] % 4
                dve.wait_ge(v_done, it * 4 + k + 1)
                for i in range(2):
                    last = dve.tensor_tensor(vw[0:S, 2 * k + i, :, 0:HD],
                                             bank(b, C, S, i * C).rearrange("p (h d) -> p h d", d=HD),
                                             w.v_bias[0:S].rearrange("p (h d) -> p h d", d=HD), ALU.add)
                last.then_inc(v_ready, 1)

            def clip(it, s):
                for q in range(2):
                    dve.wait_ge(s_done, it * 2 * G + 2 * s + q + 1)
                    dve.tensor_scalar(sc[0:S, s, 4 * PAIR * q:4 * PAIR * (q + 1)].rearrange("p (b n) -> p b n", b=2),
                                      ps[0:S, 2 * q:2 * q + 2, 0:2 * PAIR], -1.0 + COS_EPS, 1.0 - COS_EPS,
                                      ALU.max, ALU.min).then_inc(clip_ready, 1)

            def difference(it, s):
                dve.wait_ge(ln_ready, it * G + s + 1)
                dve.tensor_tensor(sc[0:S, s, :], lnp[0:S, s % 3, :], sc[0:S, s, :], ALU.subtract).then_inc(x_ready, 1)

            def qk_unit(g, u):
                f, hf = UNIT_OF[u]
                cols = slice(hf * HALF, (hf + 1) * HALF)
                dve.wait_ge(inv_ready, g * 8 + u + 1)
                dve.wait_ge(raw_ready, g * 8 + u + 1)
                parts = [qT[:, f, e, cols] for e in range(2)] if f < CK else [kT[:, f - CK, cols]]
                for x in parts:
                    last = dve.scalar_tensor_tensor(out=x, in0=inv[:, u % 3, :], scalar=1e12, in1=x,
                                                    op0=ALU.min, op1=ALU.mult)
                last.then_inc(qk_ready, 1)

            def mlp_unit(g, u):
                j, hf = u // 2, u % 2
                dve.wait_ge(sig_ready, g * UNITS + u + 1)
                dve.tensor_tensor(act_gate[:, u % 2, :], bank(4 + NUMBER["gu", ("gate", u)] % 4, HALF),
                                  sig[:, u % 2, :], ALU.mult).then_inc(gate_ready, 1)
                dve.wait_ge(gate_ready, g * UNITS + u + 1)
                dve.tensor_tensor(hid[:, j, hf * HALF:(hf + 1) * HALF],
                                  bank(4 + NUMBER["gu", ("up", u)] % 4, HALF), act_gate[:, u % 2, :], ALU.mult
                                  ).then_inc(hid_ready, 1)

            def result(g, t):
                dve.wait_ge(down_done, g * NR + t + 1)
                dve.tensor_tensor(h2[:, t, :], bank(4 + NUMBER["down", t] % 4, C), h2[:, t, :], ALU.add
                                  ).then_inc(y_ready, 1)

            def key_mass(it, k):
                dve.wait_ge(a_ready, it * HV + k + 1)
                dve.wait_ge(v_ready, it * 4 + k + 1)
                dve.tensor_reduce(mass[0:S, k % 2, :], sc[0:S, 2 * k:2 * k + 2, :].rearrange("p s (h q) -> p (s h) q", q=S),
                                  AX.X, ALU.add).then_inc(mass_ready, 1)
                dve.wait_ge(mass_ready, it * HV + k + 1)
                dve.reciprocal(vw[0:S, 2 * k:2 * k + 2, :, HD].rearrange("p s h -> p (s h)"), mass[0:S, k % 2, :]
                               ).then_inc(rm_ready, 1)

            def head_out(it, s):
                pv = bank(s % 4, NH * VD, S).rearrange("p (h d) -> p h d", d=VD)
                dve.wait_ge(pv_done, it * G + s + 1)
                dve.tensor_scalar(osum[0:S, s % 2, :], pv[:, :, HD], 1e-12, None, ALU.max).then_inc(osum_ready, 1)
                dve.wait_ge(osum_ready, it * G + s + 1)
                dve.reciprocal(osum[0:S, s % 2, :], osum[0:S, s % 2, :]).then_inc(orec_ready, 1)
                dve.wait_ge(orec_ready, it * G + s + 1)
                if s >= 2:
                    dve.wait_ge(o_tr, it * G + s - 1)
                dve.tensor_tensor(o[0:S, s % 2, :].rearrange("p (h d) -> p h d", d=HD), pv[:, :, 0:HD],
                                  osum[0:S, s % 2, :].unsqueeze(2).to_broadcast([S, NH, HD]), ALU.mult
                                  ).then_inc(o_ready, 1)

            def residual(it, t, stored_needed):
                dve.wait_ge(op_done, it * NR + t + 1)
                if t == 0:
                    dve.wait_ge(hb_ready, it + 1)
                    if stored_needed:
                        dve.wait_ge(stored, 32 * it)
                dve.tensor_tensor(h2[:, t, :], bank(t % 4, C), h_bias[:, t, :], ALU.add).then_inc(h2_ready, 1)

            def before_all():
                moments1(0)
                normalise(x1, h_in, mv1, rstd1, mv1_ready, rstd1_ready, 0, x1_ready)
                turned(x1T, "x1T", x1_tr, x1T_ready, 0)
                for u in range(8):
                    qk_unit(0, u)

            def body(it, before, now):
                prev, nxt = -1 in now, 1 in now
                for k in range(4):
                    values(it, k)
                if prev:
                    moments2(it - 1)
                clip(it, 0)
                clip(it, 1)
                if prev:
                    normalise(x2, h2, mv2, rstd2, mv2_ready, rstd2_ready, it - 1, x2_ready)
                difference(it, 0)
                clip(it, 2)
                if nxt:
                    moments1(it + 1)
                difference(it, 1)
                clip(it, 3)
                if prev:
                    turned(x2T, "x2T", x2_tr, x2T_ready, it - 1)
                difference(it, 2)
                clip(it, 4)
                if nxt:
                    normalise(x1, h_in, mv1, rstd1, mv1_ready, rstd1_ready, it + 1, x1_ready)
                for s in range(5, G):
                    difference(it, s - 2)
                    clip(it, s)
                if nxt:
                    turned(x1T, "x1T", x1_tr, x1T_ready, it + 1)
                    for u in range(8):
                        if u in (2, 5):
                            difference(it, G - 2 + u // 3)
                        qk_unit(it + 1, u)
                else:
                    difference(it, G - 2)
                    difference(it, G - 1)
                if prev:
                    for u in range(UNITS):
                        mlp_unit(it - 1, u)
                    for t in range(NR):
                        result(it - 1, t)
                for k in range(HV):
                    key_mass(it, k)
                for s in range(G):
                    head_out(it, s)
                for t in range(NR):
                    residual(it, t, prev)

            def after():
                moments2(NG - 1)
                normalise(x2, h2, mv2, rstd2, mv2_ready, rstd2_ready, NG - 1, x2_ready)
                turned(x2T, "x2T", x2_tr, x2T_ready, NG - 1)
                for u in range(UNITS):
                    mlp_unit(NG - 1, u)
                for t in range(NR):
                    result(NG - 1, t)

            iterate(dve, body, before_all, after)

        @block.tensor
        def _(pe):
            def values(it, k, before, now):
                b = claim(pe, it, before, now, "v", k)
                if k == 0:
                    pe.wait_ge(x1T_ready, 3 * (it + 1))
                for i in range(2):
                    c0 = (2 * k + i) * S
                    for c in range(CK):
                        last = pe.matmul(bank(b, C, S, i * C), x1T[:, c, c0:c0 + S], w.v[:, c, :],
                                         start=(c == 0), stop=(c == CK - 1))
                last.then_inc(v_done, 1)

            def scores(it, s, before):
                for q in range(2):
                    if s == 0 and q == 0:
                        pe.wait_ge(qk_ready, 8 * (it + 1))
                        if 0 in before:
                            pe.wait_ge(h2_ready, it * NR)
                    if s:
                        pe.wait_ge(clip_ready, it * 2 * G + 2 * (s - 1) + q + 1)
                    for r in (2 * q, 2 * q + 1):
                        g = slice(32 * r, 32 * r + 32)
                        for c in range(CK):
                            last = pe.matmul(bank(r, PAIR, S, c * PAIR), kT[g, c, s * S:(s + 1) * S],
                                             qT[g, c, :, s * S:(s + 1) * S], start=True, stop=True)
                    last.then_inc(s_done, 1)

            def turn(it, x, ready, stage, tr, g, before, now):
                for n in range(3):
                    b = claim(pe, it, before, now, stage, n)
                    if n == 0:
                        pe.wait_ge(ready, g * NR + 4)
                    if n == 2:
                        pe.wait_ge(ready, g * NR + NR)
                    parts = [(t, n) for t in range(4)] if n < CK else [(t, c) for c in range(CK) for t in (4, 5)]
                    for i, (t, c) in enumerate(parts):
                        last = pe.transpose(bank(b, P, P, i * P), x[:, t, c * P:(c + 1) * P], w.ident[:])
                    last.then_inc(tr, 1)

            def qk(it, before, now):
                g = it + 1
                pe.wait_ge(x1T_ready, 3 * (g + 1))
                for kind, u in QK_ORDER:
                    b = claim(pe, it, before, now, "qk", (kind, u))
                    f, hf = UNIT_OF[u]
                    if kind == "proj":
                        for c in range(CK):
                            last = pe.matmul(bank(b, HALF), w.qk[:, c, f * P:(f + 1) * P],
                                             x1T[:, c, hf * HALF:(hf + 1) * HALF], start=(c == 0), stop=(c == CK - 1))
                        last.then_inc(qk_done, 1)
                    else:
                        pe.wait_ge(sq_ready, g * 8 + u + 1)
                        pe.matmul(bank(b, HALF), w.head_sum[:], sq[:, u % 2, :], start=True, stop=True
                                  ).then_inc(n2_done, 1)

            def gate_up(it, u, before, now):
                g = it - 1
                j, hf = u // 2, u % 2
                for i, kind in enumerate(("gate", "up")):
                    b = claim(pe, it, before, now, "gu", (kind, u))
                    for c in range(CK):
                        last = pe.matmul(bank(b, HALF), w.gu[:, c, i * HID + j * P:i * HID + (j + 1) * P],
                                         x2T[:, c, hf * HALF:(hf + 1) * HALF], start=(c == 0), stop=(c == CK - 1))
                last.then_inc(gu_done, 1)

            def down(it, t, before, now):
                g = it - 1
                b = claim(pe, it, before, now, "down", t)
                if t == 0:
                    pe.wait_ge(hid_ready, UNITS * (g + 1))
                for k in range(HK):
                    last = pe.matmul(bank(b, C), hid[:, k, ROWS[t]:ROWS[t] + P], w.d[:, k, :],
                                     start=(k == 0), stop=(k == HK - 1))
                last.then_inc(down_done, 1)

            def weighted(it, s):
                if s % 2 == 0:
                    pe.wait_ge(vw_ready, it * HV + s // 2 + 1)
                if s < 4:
                    pe.wait_ge(clip_ready, (it + 1) * 2 * G)
                else:
                    pe.wait_ge(o_ready, it * G + s - 3)
                for h in range(NH):
                    last = pe.matmul(bank(s % 4, VD, S, h * VD), sc[0:S, s, h * S:(h + 1) * S], vw[0:S, s, h, :],
                                     start=True, stop=True)
                last.then_inc(pv_done, 1)

            def turn_o(it, s, before, now):
                hf, i = s // SH, s % SH
                if i == 0:
                    banks[:] = [claim(pe, it, before, now, "oT", hf * CK + c) for c in range(CK)]
                pe.wait_ge(o_ready, it * G + s + 1)
                for c in range(CK):
                    last = pe.transpose(bank(banks[c], S, P, i * S), o[0:S, s % 2, c * P:(c + 1) * P],
                                        w.ident[0:S, 0:S])
                last.then_inc(o_tr, 1)

            def project(it, t):
                pe.wait_ge(oT_ready, it * 4 + (2 if ROWS[t] + P <= HALF else 4))
                if t < 4:
                    pe.wait_ge(o_ready, it * G + 5 + t)
                else:
                    pe.wait_ge(h2_ready, it * NR + t - 3)
                for c in range(CK):
                    last = pe.matmul(bank(t % 4, C), oT[:, c, ROWS[t]:ROWS[t] + P], w.out[:, c, :],
                                     start=(c == 0), stop=(c == CK - 1))
                last.then_inc(op_done, 1)

            banks = []

            def before_all():
                turn(-1, x1, x1_ready, "x1T", x1_tr, 0, set(), {1})
                qk(-1, set(), {1})

            def body(it, before, now):
                for k in range(4):
                    values(it, k, before, now)
                for s in range(4):
                    scores(it, s, before)
                if -1 in now:
                    turn(it, x2, x2_ready, "x2T", x2_tr, it - 1, before, now)
                for s in range(4, G):
                    scores(it, s, before)
                if 1 in now:
                    turn(it, x1, x1_ready, "x1T", x1_tr, it + 1, before, now)
                    qk(it, before, now)
                if -1 in now:
                    for u in range(UNITS):
                        gate_up(it, u, before, now)
                    for t in range(NR):
                        down(it, t, before, now)
                for s in range(G):
                    weighted(it, s)
                    if s:
                        turn_o(it, s - 1, before, now)
                turn_o(it, G - 1, before, now)
                for t in range(NR):
                    project(it, t)

            def after():
                before, now = {-1, 0}, {-1}
                turn(NG, x2, x2_ready, "x2T", x2_tr, NG - 1, before, now)
                for u in range(UNITS):
                    gate_up(NG, u, before, now)
                for t in range(NR):
                    down(NG, t, before, now)

            iterate(pe, body, before_all, after)


UNIT_OF = [(f, hf) for f in range(2 * CK) for hf in range(2)]
QK_ORDER = [("proj", 0)] + [x for u in range(1, 8) for x in (("proj", u), ("norm", u - 1))] + [("norm", 7)]


def program(nc, a, out):
    h_all = nc.dram_tensor("tokens", [B, S, C], F32).ap()
    with ExitStack() as stack:
        mem = Names(nc, stack)
        w = Weights(mem)
        ps = stack.enter_context(nc.psum_tensor("ps", [P, 8, 512], F32))
        tokenizer(nc, a, w, ps, h_all)
        transformer(nc, a, w, ps, h_all, out)


def kernel(**inputs):
    import concourse.bacc as bacc
    import numpy as np
    from concourse.bass_utils import run_bass_kernel_spmd

    x = {n.removeprefix("L0_").removeprefix("tok_").removeprefix("attn_").removeprefix("ffn_"): np.asarray(v)
         for n, v in inputs.items()}
    order = [c * 8 + 2 * r + e for r in range(4) for c in range(CK) for e in range(2)]
    feats = np.array([h * HD + d for h in order for d in range(HD)])
    px = x["x"].reshape(B, 3, 2, 3, 14, 2, 3, 14).transpose(1, 4, 7, 2, 3, 6, 5, 0)
    data = {
        "patches": px.reshape(PATCH, NT * P),
        "conv_w": x["conv_w"].reshape(C, PATCH).T,
        "txt": x["txt"],
        "w_qk": x["w_qkv"][0:2 * C].T, "b_qk": x["b_qkv"][0:2 * C].reshape(2 * CK, P).T,
        "w_v": x["w_qkv"][2 * C:][feats].T, "b_v": x["b_qkv"][2 * C:][feats],
        "w_out": x["w_out"][:, feats].T, "b_out": x["b_out"],
        "w_gate": x["w_gate"].T, "w_up": x["w_up"].T, "w_down": x["w_down"].T,
        "ident": np.eye(P, dtype=np.float32),
        "pick": np.tile(np.eye(B, dtype=np.float32), (2, 1)),
        "head_sum": np.kron(np.eye(P // HD, dtype=np.float32), np.ones((HD, HD), np.float32)),
        "head_row": np.repeat(np.tile(np.eye(2, dtype=np.float32), (P // HD // 2, 1)), HD, axis=0),
    }
    gains = [x[f"{part}_ln_{side}_{kind}"] for part in ("la", "ga") for side in ("q", "kv") for kind in ("g", "b")]
    data["gains"] = np.stack(gains).reshape(8, CK, P).transpose(2, 0, 1)
    data["rows"] = np.stack([x["la_proj_b"], x["mod_b"], x["ga_proj_b"], x["class_emb"]])[None]
    for n in ("class_emb", "la_wq", "la_wkv", "la_proj_w", "ga_wq", "ga_wkv", "ga_proj_w", "mod_w"):
        data[n] = x[n]
    nc = bacc.Bacc("TRN2", target_bir_lowering=False, num_devices=1)
    arrays, aps = {}, {}
    for n, v in data.items():
        v = np.ascontiguousarray(v)
        arrays["in_" + n] = v
        aps[n] = nc.dram_tensor("in_" + n, v.shape, mybir.dt.from_np(v.dtype), kind="ExternalInput").ap()
    out = nc.dram_tensor("out", [B, S, C], F32, kind="ExternalOutput").ap()
    program(nc, aps, out)
    r = run_bass_kernel_spmd(nc, [arrays], core_ids=[0])
    return r.results[0]["out"]
```

```python
import math
from contextlib import ExitStack

import concourse.bass as bass
from concourse import mybir

F32 = mybir.dt.float32
F32R = mybir.dt.float32r
I32 = mybir.dt.int32
ALU = mybir.AluOpType
ACT = mybir.ActivationFunctionType
AX = mybir.AxisListType

P = 128
C = 256
CK = C // P
B = 64

H8, DH = 8, 32
WIN = 9
NW = 4
RT = B * NW // P
NT = RT * WIN
KP, KN = 118, 5
PATCH = 3 * 14 * 14
KL = PATCH - KP * (KN - 1)
TOK_SCALE = C ** -0.5
LN_EPS = 1e-5

TXT = 77
S = NW + 1 + TXT
T = B * S
NH, HD = 16, 16
HID = 768
HK = HID // P
G = 8
NG = B // G
TG = G * S
HALF = TG // 2
SH = G // 2
ROWS = [0, 128, 256, 384, 512, TG - P]
NR = len(ROWS)
PAIR = 2 * S
SC = NH * S
VD = HD + 1
VS = 32
VW = (NH - 1) * VD + VS
COS_EPS = 1e-7
POWER = -3.2
HALF_PI = 1.5707963267948966
N2_SCALE = 2.0 ** 30
N2_BIAS = 2.0 ** -63
N2_SHIFT = 15 * 0.6931471805599453
SCALE_Q = 1.0 / 127.0

LN_EXP = "natural_log_exp_and_others"
SIG_ATAN = "sigmoid_and_others"


class Names:

    def __init__(self, nc, stack):
        self.nc, self.stack = nc, stack

    def sb(self, name, *shape, dt=F32):
        return self.stack.enter_context(self.nc.sbuf_tensor(name, [P, *shape], dt))

    def sem(self, name):
        return self.stack.enter_context(self.nc.semaphore(name))


class Weights:

    def __init__(self, mem):
        self.ident = mem.sb("ident", P)
        self.head_sum = mem.sb("head_sum", P)
        self.head_row = mem.sb("head_row", 2)
        self.q_bias = mem.sb("q_bias", 4)
        self.q_bias_m = mem.sb("q_bias_m", 2, 2)
        self.qk = mem.sb("w_qk", CK, 2 * C)
        self.v = mem.sb("w_v", CK, C)
        self.v_bias = mem.sb("v_bias", C)
        self.out = mem.sb("w_out", CK, C)
        self.out_bias = mem.sb("out_bias", C)
        self.gu = mem.sb("w_gate_up", CK, 2 * HID)
        self.d = mem.sb("w_down", HK, C)


def tokenizer(nc, a, w, ps, h_all):
    with ExitStack() as stack:
        mem = Names(nc, stack)
        sb, sem = mem.sb, mem.sem
        patches = sb("patches", KN, NT * P)
        ints = patches[:].rearrange("p k n -> p (k n)").bitcast(I32)
        gu_int = ints[:, 0:CK * 2 * HID].rearrange("p (k n) -> p k n", k=CK)
        d_int = ints[:, CK * 2 * HID:CK * 2 * HID + HK * C].rearrange("p (k n) -> p k n", k=HK)
        used = [CK * 2 * HID + HK * C]

        def late(*shape):
            n = math.prod(shape)
            view = patches[:].rearrange("p k n -> p (k n)")[:, used[0]:used[0] + n]
            used[0] += n
            assert used[0] <= KN * NT * P
            names = "abc"[:len(shape)]
            spec = f"p ({' '.join(names)}) -> p {' '.join(names)}"
            return view.rearrange(spec, **dict(zip(names[:-1], shape[:-1])))

        conv_w = sb("conv_w", KN, C)
        pe = sb("pe", NT, C)
        hat = sb("hat", NT, C)
        kvT = sb("kvT", 4, CK, P)
        kv = sb("kv", NT, 2 * C)
        wq, wkv, wproj = sb("la_wq", CK, C), sb("la_wkv", CK, 2 * C), sb("la_proj", CK, C)
        gwq, gwkv, gproj = sb("ga_wq", CK, C), sb("ga_wkv", CK, 2 * C), sb("ga_proj", CK, C)
        mod = sb("mod_w", CK, C)
        gains = sb("gains", 8, CK)
        rows = sb("rows", 4, C)
        ones = sb("ones_row", P)
        pick = sb("pick", B)
        cls_in = sb("cls_in", C)
        st = sb("patch_stats", NT, 6)
        mv = sb("patch_mv", NT, 2)
        rstd = sb("patch_rstd", NT)
        red = sb("red", RT, C)
        rst, rmv, rrs = sb("red_stats", RT, 6), sb("red_mv", RT, 2), sb("red_rstd", RT)
        rhat = sb("red_hat", RT, C)
        rT = sb("redT", RT, CK, P)
        q = late(RT, C)
        s = sb("s", RT, WIN, H8)
        smax = sb("smax", RT, H8)
        den = sb("den", RT, H8)
        agg = late(RT, C)
        aggT = late(RT, CK, P)
        lo = late(RT, C)
        loT = late(RT, CK, P)
        patch_out = late(RT, C)
        lst, lmv, lrs = sb("lo_stats", RT, 6), sb("lo_mv", RT, 2), sb("lo_rstd", RT)
        lhat = late(RT, C)
        lhT = late(RT, CK, P)
        gkv = late(RT, 2 * C)
        cst, cmv, crs = sb("cls_stats", 6), sb("cls_mv", 2), sb("cls_rstd", 1)
        chat = sb("cls_hat", C)
        cT = sb("cls_hatT", CK, P)
        gq = late(C)
        gprod = late(RT, C)
        gs = sb("gs", RT, H8)
        gsT = late(RT * P)
        gm, gd = sb("gmax", B), sb("gden", B)
        gp = sb("gp", RT, H8)
        gaT = late(CK, B)
        cls_out = late(C)

        conv_loaded, weights_loaded, main_loaded = sem("conv_loaded"), sem("weights_loaded"), sem("main_loaded")
        patches_loaded = [sem(f"patches_loaded_{j}") for j in range(RT)]
        txt_copied, tok_stored = sem("txt_copied"), sem("tok_stored")
        consts = sem("consts")
        conv_done, pe_ready = sem("conv_done"), sem("pe_ready")
        hat_done, tr_done, kvT_ready = sem("hat_done"), sem("tr_done"), sem("kvT_ready")
        kv_done, kv_ready = sem("kv_done"), sem("kv_ready")
        rstd_ready = sem("rstd_ready")
        red_mv_ready, red_rstd_ready, red_hat_ready = sem("red_mv_ready"), sem("red_rstd_ready"), sem("red_hat_ready")
        mv_ready = sem("mv_ready")
        red_tr, red_T, q_done, q_ready = sem("red_tr"), sem("red_T"), sem("q_done"), sem("q_ready")
        qk_prod, s_ready, e_ready, p_ready = sem("qk_prod"), sem("s_ready"), sem("e_ready"), sem("p_ready")
        pv_prod, agg_ready, agg_tr, agg_T = sem("pv_prod"), sem("agg_ready"), sem("agg_tr"), sem("agg_T")
        proj_done, lo_ready, lo_tr, lo_T = sem("proj_done"), sem("lo_ready"), sem("lo_tr"), sem("lo_T")
        patch_done, patch_ready = sem("patch_done"), sem("patch_ready")
        lo_mv_ready, lo_rstd_ready, lo_hat_ready = sem("lo_mv_ready"), sem("lo_rstd_ready"), sem("lo_hat_ready")
        lh_tr, lh_T, gkv_done, gkv_ready = sem("lh_tr"), sem("lh_T"), sem("gkv_done"), sem("gkv_ready")
        cls_mv_ready, cls_rstd_ready, cls_hat_ready = sem("cls_mv_ready"), sem("cls_rstd_ready"), sem("cls_hat_ready")
        cls_tr, cls_T, gq_done, gq_ready = sem("cls_tr"), sem("cls_T"), sem("gq_done"), sem("gq_ready")
        gk_prod, gs_ready, gs_tr, gs_T = sem("gk_prod"), sem("gs_ready"), sem("gs_tr"), sem("gs_T")
        ge_ready, gp_T, gp_tr, gp_ready = sem("ge_ready"), sem("gp_T"), sem("gp_tr"), sem("gp_ready")
        gv_prod, ga_done, ga_T, cls_done, cls_ready = (
            sem("gv_prod"), sem("ga_done"), sem("ga_T"), sem("cls_done"), sem("cls_ready"))
        act_step = sem("act_step")
        dve_step = sem("dve_step")
        block = stack.enter_context(nc.Block())

        def cols(bank, c, n):
            return ps[:, bank, c:c + n]

        @block.sync
        def _(sync):
            def patch_load(j):
                c0, c1 = j * WIN * P, (j + 1) * WIN * P
                sync.dma_start(patches[0:KP, 0:KN - 1, c0:c1],
                               a["patches"][0:KP * (KN - 1), c0:c1].rearrange("(k p) n -> p k n", p=KP)
                               ).then_inc(patches_loaded[j], 16)
                sync.dma_start(patches[0:KL, KN - 1, c0:c1], a["patches"][KP * (KN - 1):PATCH, c0:c1]
                               ).then_inc(patches_loaded[j], 16)

            sync.dma_start(conv_w[0:KP, 0:KN - 1, :],
                           a["conv_w"][0:KP * (KN - 1), :].rearrange("(k p) n -> p k n", p=KP)).then_inc(conv_loaded, 16)
            sync.dma_start(conv_w[0:KL, KN - 1, :], a["conv_w"][KP * (KN - 1):PATCH, :]).then_inc(conv_loaded, 16)
            patch_load(0)
            patch_load(1)
            sync.dma_start(h_all[:, NW + 1:S, :], a["txt"]).then_inc(txt_copied, 16)
            sync.wait_ge(patch_ready, RT)
            for j in range(RT):
                for hx in range(2):
                    sync.dma_start(h_all[:, 2 * j + hx, :], patch_out[64 * hx:64 * hx + B, j, :]).then_inc(tok_stored, 16)
            sync.wait_ge(cls_ready, 1)
            sync.dma_start(h_all[:, NW, :], cls_out[0:B, :]).then_inc(tok_stored, 16)
            sync.wait_ge(tok_stored, 16 * (2 * RT + 1))
            sync.wait_ge(txt_copied, 16)

        @block.gpsimd
        def _(pool):
            pool.memset(ones[:], 1.0).then_inc(consts, 1)
            pool.dma_start(w.ident[:], a["ident"]).then_inc(weights_loaded, 16)
            pool.dma_start(pick[:], a["pick"]).then_inc(weights_loaded, 16)
            for dst, src in ((wkv[:], a["la_wkv"]), (wq[:], a["la_wq"]), (gwq[:], a["ga_wq"]), (wproj[:], a["la_proj_w"]),
                             (mod[:], a["mod_w"]), (gwkv[:], a["ga_wkv"]), (gproj[:], a["ga_proj_w"])):
                pool.dma_start(dst, src.rearrange("(k p) n -> p k n", p=P)).then_inc(weights_loaded, 16)
            pool.dma_start(gains[:], a["gains"]).then_inc(weights_loaded, 16)
            pool.dma_start(rows[0:1], a["rows"]).then_inc(weights_loaded, 16)
            pool.dma_start(cls_in[:], a["class_emb"].partition_broadcast(P)).then_inc(weights_loaded, 16)
            for dst, src in ((w.qk[:], a["w_qk"]), (w.v[:], a["w_v"]), (w.out[:], a["w_out"]),
                             (gu_int[:, :, 0:HID], a["w_gate"]), (gu_int[:, :, HID:2 * HID], a["w_up"]),
                             (d_int, a["w_down"])):
                if src is a["w_gate"]:
                    pool.wait_ge(conv_done, NT)
                pool.dma_start(dst, src.rearrange("(k p) n -> p k n", p=P)).then_inc(main_loaded, 16)
            pool.dma_start(w.q_bias[:], a["b_qk"]).then_inc(main_loaded, 16)
            pool.dma_start(w.head_row[:], a["head_row"]).then_inc(main_loaded, 16)
            pool.dma_start(w.head_sum[:], a["head_sum"]).then_inc(main_loaded, 16)
            pool.dma_start(w.v_bias[:], a["b_v"].partition_broadcast(P)).then_inc(main_loaded, 16)
            pool.dma_start(w.out_bias[:], a["b_out"].partition_broadcast(P)).then_inc(main_loaded, 16)
            pool.wait_ge(kv_ready, WIN)
            for j in range(RT):
                t0, t1 = j * WIN, (j + 1) * WIN
                pool.wait_ge(kv_ready, t1)
                pool.wait_ge(q_ready, j + 1)
                pool.wait_ge(tr_done, t1)
                pool.tensor_tensor(hat[:, t0:t1, :], kv[:, t0:t1, 0:C],
                                   q[:, j:j + 1, :].to_broadcast([P, WIN, C]), ALU.mult).then_inc(qk_prod, 1)
            for j in range(RT):
                t0, t1 = j * WIN, (j + 1) * WIN
                pool.wait_ge(p_ready, j + 1)
                pool.tensor_tensor(
                    hat[:, t0:t1, :].rearrange("p n (h d) -> p (n h) d", d=DH),
                    kv[:, t0:t1, C:2 * C].rearrange("p n (h d) -> p n h d", d=DH),
                    s[:, j, :, :].unsqueeze(3).to_broadcast([P, WIN, H8, DH]), ALU.mult).then_inc(pv_prod, 1)
            for j in range(RT):
                pool.wait_ge(gkv_ready, j + 1)
                pool.wait_ge(gq_ready, 1)
                pool.tensor_tensor(gprod[:, j, :], gkv[:, j, 0:C], gq[:], ALU.mult).then_inc(gk_prod, 1)
            for j in range(RT):
                pool.wait_ge(gp_ready, j + 1)
                pool.tensor_tensor(gprod[:, j, :].rearrange("p (h d) -> p h d", d=DH),
                                   gkv[:, j, C:2 * C].rearrange("p (h d) -> p h d", d=DH),
                                   gp[:, j, :].unsqueeze(2).to_broadcast([P, H8, DH]), ALU.mult).then_inc(gv_prod, 1)

        @block.scalar
        def _(act):
            act.preload_act_table_set(LN_EXP)

            act_count = [0]

            def rsqrt(dst, var, got, n, done):
                act.wait_ge(got, n)
                act.activation(dst, var, ACT.Ln, bias=LN_EPS).then_inc(act_step, 1)
                act_count[0] += 1
                act.wait_ge(act_step, act_count[0])
                act.activation(dst, dst, ACT.Exp, scale=-0.5).then_inc(done, 1)

            def evac_pe(t):
                act.wait_ge(conv_done, t + 1)
                act.activation(pe[:, t, :], cols(t % 4, 0, C), ACT.Copy).then_inc(pe_ready, 1)

            def evac_kv(t):
                act.wait_ge(kv_done, t + 1)
                act.activation(kv[:, t, :], cols(6 + t % 2, 0, 2 * C), ACT.Copy).then_inc(kv_ready, 1)

            for t in range(WIN):
                evac_pe(t)
            rsqrt(rstd[:, 0:WIN], mv[:, 0:WIN, 1], mv_ready, 1, rstd_ready)
            rsqrt(rrs[:, 0:1], rmv[:, 0, 1:2], red_mv_ready, 1, red_rstd_ready)
            rsqrt(crs[:], cmv[:, 1:2], cls_mv_ready, 1, cls_rstd_ready)
            for t in range(WIN, NT):
                evac_pe(t)
            rsqrt(rstd[:, WIN:NT], mv[:, WIN:NT, 1], mv_ready, 2, rstd_ready)
            rsqrt(rrs[:, 1:2], rmv[:, 1, 1:2], red_mv_ready, 2, red_rstd_ready)
            for t in range(NT):
                evac_kv(t)
            for j in range(RT):
                act.wait_ge(q_done, j + 1)
                act.activation(q[:, j, :], cols(j, 0, C), ACT.Copy, scale=TOK_SCALE).then_inc(q_ready, 1)
            act.wait_ge(gq_done, 1)
            act.activation(gq[:], cols(2, 0, C), ACT.Copy, scale=TOK_SCALE).then_inc(gq_ready, 1)
            for j in range(RT):
                act.wait_ge(s_ready, j + 1)
                act.activation(s[:, j], s[:, j], ACT.Exp).then_inc(e_ready, 1)
            for j in range(RT):
                rsqrt(lrs[:, j:j + 1], lmv[:, j, 1:2], lo_mv_ready, j + 1, lo_rstd_ready)
            for j in range(RT):
                act.wait_ge(patch_done, j + 1)
                act.activation(patch_out[:, j, :], cols(2 + j, 0, C), ACT.Copy).then_inc(patch_ready, 1)
            for j in range(RT):
                act.wait_ge(gkv_done, j + 1)
                act.activation(gkv[:, j, :], cols(4 + j, 0, 2 * C), ACT.Copy).then_inc(gkv_ready, 1)
            act.wait_ge(gs_T, 1)
            act.activation(gsT[0:H8, :], gsT[0:H8, :], ACT.Exp).then_inc(ge_ready, 1)

        @block.vector
        def _(dve):
            count = [0]

            def link(ins):
                count[0] += 1
                ins.then_inc(dve_step, 1)
                dve.wait_ge(dve_step, count[0])

            def step(ins):
                count[0] += 1
                ins.then_inc(dve_step, 1)

            def stats(st_, mv_, x, done):
                link(dve.bn_stats(st_, x))
                dve.bn_aggr(mv_, st_).then_inc(done, 1)

            def patch_stats(j):
                for t in range(j * WIN, (j + 1) * WIN):
                    dve.wait_ge(pe_ready, t + 1)
                    step(dve.bn_stats(st[:, t, :], pe[:, t, :]))
                dve.wait_ge(dve_step, count[0])
                for t in range(j * WIN, (j + 1) * WIN):
                    last = dve.bn_aggr(mv[:, t, :], st[:, t, :])
                    step(last) if t < (j + 1) * WIN - 1 else last.then_inc(mv_ready, 1)

            def patch_hats(j):
                dve.wait_ge(rstd_ready, j + 1)
                dve.wait_ge(mv_ready, j + 1)
                for t in range(j * WIN, (j + 1) * WIN):
                    dve.tensor_scalar(hat[:, t, :], pe[:, t, :], mv[:, t, 0:1], rstd[:, t:t + 1],
                                      ALU.subtract, ALU.mult).then_inc(hat_done, 1)

            def window_mean(j):
                link(dve.tensor_reduce(red[:, j, :], pe[:, j * WIN:(j + 1) * WIN, :].rearrange("p n c -> p c n"),
                                       AX.X, ALU.add))
                link(dve.tensor_scalar(red[:, j, :], red[:, j, :], 1.0 / WIN, None, ALU.mult))
                stats(rst[:, j, :], rmv[:, j, :], red[:, j, :], red_mv_ready)

            def gained(dst, bank, c0, gb):
                for c in range(CK):
                    ins = dve.tensor_scalar(dst[:, c, :], cols(bank, c0 + c * P, P), gains[:, gb, c:c + 1],
                                            gains[:, gb + 1, c:c + 1], ALU.mult, ALU.add)
                    if c < CK - 1:
                        step(ins)
                return ins

            def kvT_tile(t):
                dve.wait_ge(tr_done, t + 1)
                if t >= 4:
                    dve.wait_ge(kv_done, t - 3)
                gained(kvT[:, t % 4], 4 + t % 2, 0, 2).then_inc(kvT_ready, 1)

            patch_stats(0)
            window_mean(0)
            dve.wait_ge(weights_loaded, 16 * 12)
            stats(cst[:], cmv[:], cls_in[:], cls_mv_ready)
            patch_hats(0)
            dve.wait_ge(red_rstd_ready, 1)
            dve.wait_ge(red_mv_ready, 1)
            dve.tensor_scalar(rhat[:, 0, :], red[:, 0, :], rmv[:, 0, 0:1], rrs[:, 0:1], ALU.subtract, ALU.mult
                              ).then_inc(red_hat_ready, 1)
            dve.wait_ge(cls_rstd_ready, 1)
            dve.wait_ge(cls_mv_ready, 1)
            dve.tensor_scalar(chat[:], cls_in[:], cmv[:, 0:1], crs[:, 0:1], ALU.subtract, ALU.mult
                              ).then_inc(cls_hat_ready, 1)
            patch_stats(1)
            window_mean(1)
            for t in range(WIN):
                kvT_tile(t)
            patch_hats(1)
            dve.wait_ge(red_rstd_ready, 2)
            dve.wait_ge(red_mv_ready, 2)
            dve.tensor_scalar(rhat[:, 1, :], red[:, 1, :], rmv[:, 1, 0:1], rrs[:, 1:2], ALU.subtract, ALU.mult
                              ).then_inc(red_hat_ready, 1)
            for t in range(WIN, NT):
                kvT_tile(t)
            for j in range(RT):
                dve.wait_ge(red_tr, j + 1)
                gained(rT[:, j], 4 + j, 0, 0).then_inc(red_T, 1)
            dve.wait_ge(cls_tr, 1)
            gained(cT, 4, C, 4).then_inc(cls_T, 1)
            for j in range(RT):
                dve.wait_ge(qk_prod, j + 1)
                t0, t1 = j * WIN, (j + 1) * WIN
                link(dve.tensor_reduce(s[:, j].rearrange("p n h -> p (n h)"),
                                       hat[:, t0:t1, :].rearrange("p n (h d) -> p (n h) d", d=DH), AX.X, ALU.add))
                link(dve.tensor_reduce(smax[:, j, :], s[:, j].rearrange("p n h -> p h n"), AX.X, ALU.max))
                dve.tensor_tensor(s[:, j], s[:, j], smax[:, j:j + 1, :].to_broadcast([P, WIN, H8]), ALU.subtract
                                  ).then_inc(s_ready, 1)
            for j in range(RT):
                dve.wait_ge(e_ready, j + 1)
                link(dve.tensor_reduce(den[:, j, :], s[:, j].rearrange("p n h -> p h n"), AX.X, ALU.add))
                link(dve.reciprocal(den[:, j, :], den[:, j, :]))
                dve.tensor_tensor(s[:, j], s[:, j], den[:, j:j + 1, :].to_broadcast([P, WIN, H8]), ALU.mult
                                  ).then_inc(p_ready, 1)
            for j in range(RT):
                dve.wait_ge(pv_prod, j + 1)
                dve.tensor_reduce(agg[:, j, :], hat[:, j * WIN:(j + 1) * WIN, :].rearrange("p n c -> p c n"),
                                  AX.X, ALU.add).then_inc(agg_ready, 1)
            for j in range(RT):
                dve.wait_ge(agg_tr, j + 1)
                dve.tensor_copy(aggT[:, j].rearrange("p c n -> p (c n)"), cols(4 + j, 0, C)).then_inc(agg_T, 1)
            for j in range(RT):
                dve.wait_ge(proj_done, j + 1)
                dve.tensor_tensor(lo[:, j, :], cols(j, 0, C), red[:, j, :], ALU.add).then_inc(lo_ready, 1)
                dve.wait_ge(lo_ready, j + 1)
                stats(lst[:, j, :], lmv[:, j, :], lo[:, j, :], lo_mv_ready)
            for j in range(RT):
                dve.wait_ge(lo_rstd_ready, j + 1)
                dve.wait_ge(lo_mv_ready, j + 1)
                dve.tensor_scalar(lhat[:, j, :], lo[:, j, :], lmv[:, j, 0:1], lrs[:, j:j + 1], ALU.subtract, ALU.mult
                                  ).then_inc(lo_hat_ready, 1)
            for j in range(RT):
                dve.wait_ge(lo_tr, j + 1)
                dve.tensor_copy(loT[:, j].rearrange("p c n -> p (c n)"), cols(4 + j, 0, C)).then_inc(lo_T, 1)
            for j in range(RT):
                dve.wait_ge(lh_tr, j + 1)
                gained(lhT[:, j], 6 + j, 0, 6).then_inc(lh_T, 1)
            for j in range(RT):
                dve.wait_ge(gk_prod, j + 1)
                dve.tensor_reduce(gs[:, j, :], gprod[:, j, :].rearrange("p (h d) -> p h d", d=DH), AX.X, ALU.add
                                  ).then_inc(gs_ready, 1)
            dve.wait_ge(gs_tr, 1)
            scores = cols(6, 0, RT * P)[0:H8]
            by_sample = scores.rearrange("p (w b) -> p b w", b=B)
            link(dve.tensor_reduce(gm[0:H8, :], by_sample, AX.X, ALU.max))
            dve.tensor_tensor(gsT[0:H8, :].rearrange("p (w b) -> p w b", b=B),
                              scores.rearrange("p (w b) -> p w b", b=B),
                              gm[0:H8, :].unsqueeze(1).to_broadcast([H8, NW, B]), ALU.subtract).then_inc(gs_T, 1)
            dve.wait_ge(ge_ready, 1)
            link(dve.tensor_reduce(gd[0:H8, :], gsT[0:H8, :].rearrange("p (w b) -> p b w", b=B), AX.X, ALU.add))
            link(dve.reciprocal(gd[0:H8, :], gd[0:H8, :]))
            dve.tensor_tensor(gsT[0:H8, :].rearrange("p (w b) -> p w b", b=B),
                              gsT[0:H8, :].rearrange("p (w b) -> p w b", b=B),
                              gd[0:H8, :].unsqueeze(1).to_broadcast([H8, NW, B]), ALU.mult).then_inc(gp_T, 1)
            dve.wait_ge(gp_tr, 1)
            dve.tensor_copy(gp[:], cols(7, 0, RT * H8).rearrange("p (j h) -> p j h", h=H8)).then_inc(gp_ready, RT)
            dve.wait_ge(ga_done, 1)
            dve.tensor_copy(gaT[:], cols(0, 0, CK * B).rearrange("p (c b) -> p c b", b=B)).then_inc(ga_T, 1)
            dve.wait_ge(cls_done, 1)
            dve.tensor_copy(cls_out[0:B, :], cols(1, 0, C)[0:B]).then_inc(cls_ready, 1)
            dve.wait_ge(main_loaded, 16 * 11)
            for k in range(CK):
                step(dve.tensor_scalar(w.gu[:, k, :], gu_int[:, k, :], SCALE_Q, None, ALU.mult))
            step(dve.tensor_scalar(w.d[:], d_int, SCALE_Q, None, ALU.mult))
            for e in range(2):
                step(dve.tensor_scalar(w.q_bias_m[:, :, e], w.q_bias[:, 0:2], w.head_row[:, e:e + 1], None, ALU.mult))

        @block.tensor
        def _(pe_):
            def conv(t):
                pe_.wait_ge(patches_loaded[t // WIN], 32)
                if t >= 4:
                    pe_.wait_ge(pe_ready, t - 3)
                for k in range(KN):
                    kk = KP if k < KN - 1 else KL
                    last = pe_.matmul(cols(t % 4, 0, C), patches[0:kk, k, t * P:(t + 1) * P], conv_w[0:kk, k, :],
                                      start=(k == 0), stop=(k == KN - 1))
                last.then_inc(conv_done, 1)

            def transposes(bank, c0, src, done):
                for c in range(CK):
                    last = pe_.transpose(cols(bank, c0 + c * P, P), src[:, c * P:(c + 1) * P], w.ident[:])
                last.then_inc(done, 1)

            def tr(t):
                pe_.wait_ge(hat_done, t + 1)
                if t >= 2:
                    pe_.wait_ge(kvT_ready, t - 1)
                transposes(4 + t % 2, 0, hat[:, t, :], tr_done)

            def product(out, lhsT, rhs, done, bias=None, m=P):
                extra = [] if bias is None else bias
                for c in range(CK):
                    last = pe_.matmul(out, lhsT[:, c, :], rhs[:, c, :], start=(c == 0),
                                      stop=(c == CK - 1 and not extra))
                for n, r in enumerate(extra):
                    last = pe_.matmul(out, ones[0:1, 0:m], rows[0:1, r, :], start=False, stop=(n == len(extra) - 1))
                last.then_inc(done, 1)

            def kv_tile(t):
                pe_.wait_ge(kvT_ready, t + 1)
                if t >= 2:
                    pe_.wait_ge(kv_ready, t - 1)
                product(cols(6 + t % 2, 0, 2 * C), kvT[:, t % 4], wkv, kv_done)

            pe_.wait_ge(conv_loaded, 32)
            for t in range(NT):
                conv(t)
            pe_.wait_ge(consts, 1)
            pe_.wait_ge(weights_loaded, 16 * 12)
            tr(0)
            for t in range(NT):
                if t + 1 < NT:
                    tr(t + 1)
                kv_tile(t)
            pe_.wait_ge(kvT_ready, NT)
            for j in range(RT):
                pe_.wait_ge(red_hat_ready, j + 1)
                transposes(4 + j, 0, rhat[:, j, :], red_tr)
            pe_.wait_ge(cls_hat_ready, 1)
            pe_.wait_ge(red_T, 1)
            transposes(4, C, chat[:], cls_tr)
            pe_.wait_ge(pe_ready, NT)
            for j in range(RT):
                pe_.wait_ge(red_T, j + 1)
                product(cols(j, 0, C), rT[:, j], wq, q_done)
            pe_.wait_ge(cls_T, 1)
            product(cols(2, 0, C), cT, gwq, gq_done)
            for j in range(RT):
                pe_.wait_ge(agg_ready, j + 1)
                transposes(4 + j, 0, agg[:, j, :], agg_tr)
            for j in range(RT):
                pe_.wait_ge(agg_T, j + 1)
                pe_.wait_ge(q_ready, j + 1)
                product(cols(j, 0, C), aggT[:, j], wproj, proj_done, bias=[0])
            for j in range(RT):
                pe_.wait_ge(lo_ready, j + 1)
                transposes(4 + j, 0, lo[:, j, :], lo_tr)
            pe_.wait_ge(kv_ready, NT)
            for j in range(RT):
                pe_.wait_ge(lo_hat_ready, j + 1)
                transposes(6 + j, 0, lhat[:, j, :], lh_tr)
            pe_.wait_ge(gq_ready, 1)
            for j in range(RT):
                pe_.wait_ge(lo_T, j + 1)
                product(cols(2 + j, 0, C), loT[:, j], mod, patch_done, bias=[1])
            for j in range(RT):
                pe_.wait_ge(lh_T, j + 1)
                product(cols(4 + j, 0, 2 * C), lhT[:, j], gwkv, gkv_done)
            for j in range(RT):
                pe_.wait_ge(gs_ready, j + 1)
                last = pe_.transpose(cols(6, j * P, P)[0:H8], gs[:, j, :], w.ident[:])
            last.then_inc(gs_tr, 1)
            pe_.wait_ge(gp_T, 1)
            for j in range(RT):
                last = pe_.transpose(cols(7, j * H8, H8), gsT[0:H8, j * P:(j + 1) * P], w.ident[0:H8, 0:H8])
            last.then_inc(gp_tr, 1)
            pe_.wait_ge(lo_ready, RT)
            pe_.wait_ge(gv_prod, RT)
            for c in range(CK):
                for j in range(RT):
                    last = pe_.matmul(cols(0, c * B, B), gprod[:, j, c * P:(c + 1) * P], pick[:],
                                      start=(j == 0), stop=(j == RT - 1))
            last.then_inc(ga_done, 1)
            pe_.wait_ge(ga_T, 1)
            product(cols(1, 0, C)[0:B], gaT, gproj, cls_done, bias=[2, 3], m=B)


def transformer(nc, a, w, ps, h_all, out):
    with ExitStack() as stack:
        mem = Names(nc, stack)
        sb, sem = mem.sb, mem.sem
        h_in = sb("h_in", NR, C)
        h_bias = sb("h_bias", NR, C)
        h2 = sb("h2", NR, C)
        x1, x2 = h_in, sb("x2", NR, C)
        x1T, x2T = sb("x1T", CK, TG), sb("x2T", CK, TG)
        stats = sb("stats", NR, 6)
        mv1, mv2 = sb("mv1", NR, 2), sb("mv2", NR, 2)
        rstd1, rstd2 = sb("rstd1", NR), sb("rstd2", NR)
        qT, qT_lo = sb("qT", CK, 2, TG, dt=F32R), sb("qT_lo", CK, 2, TG, dt=F32R)
        kT, kT_lo = sb("kT", CK, TG, dt=F32R), sb("kT_lo", CK, TG, dt=F32R)
        raw = sb("qk_raw", 3, 2, HALF)
        sq = sb("sq", 2, HALF)
        inv = sb("inv_norm", 3, HALF)
        vw_all = sb("v_weighted", G, VW)
        vw = vw_all[:, :, 0:NH * VD].rearrange("p s (h d) -> p s h d", d=VD)
        outT = sb("outT", 2, NH * S // 4)
        sc = sb("scores", G, SC)
        lnp = sb("ln_one_plus_cos", 3, SC)
        mass = sb("key_mass", 2, 2 * NH)
        osum = sb("o_sum", 2, NH)
        o = sb("o", 2, C)
        oT = sb("oT", CK, TG)
        hid = sb("hidden", HK, TG)
        sig = sb("sigmoid", 2, HALF)
        act_gate = sb("silu_gate", 2, HALF)

        h_loaded, hr_loaded = sem("h_loaded"), sem("hr_loaded")
        hb_ready = sem("hb_ready")
        mv1_ready, mv2_ready = sem("mv1_ready"), sem("mv2_ready")
        rstd1_ready, rstd2_ready = sem("rstd1_ready"), sem("rstd2_ready")
        x1_ready, x2_ready = sem("x1_ready"), sem("x2_ready")
        x1_tr, x2_tr = sem("x1_tr"), sem("x2_tr")
        x1T_ready, x2T_ready = sem("x1T_ready"), sem("x2T_ready")
        v_done, v_ready = sem("v_done"), sem("v_ready")
        qk_done, sq_ready, raw_ready = sem("qk_done"), sem("sq_ready"), sem("raw_ready")
        n2_done, n2_ln, inv_ready = sem("n2_done"), sem("n2_ln"), sem("inv_ready")
        unit_ready, hi_ready = sem("unit_ready"), sem("hi_ready")
        q_lo_ready, k_lo_ready = sem("q_lo_ready"), sem("k_lo_ready")
        s_done, clip_ready = sem("s_done"), sem("clip_ready")
        ln_ready, x_ready = sem("ln_ready"), sem("x_ready")
        tanh_ready, atan_ready = sem("tanh_ready"), sem("atan_ready")
        ln_g, a_ready = sem("ln_g"), sem("a_ready")
        mass_ready, rm_ready, vw_ready = sem("mass_ready"), sem("rm_ready"), sem("vw_ready")
        pv_done, outT_ready, out_tr = sem("pv_done"), sem("outT_ready"), sem("out_tr")
        osum_ready, orec_ready, o_ready = sem("osum_ready"), sem("orec_ready"), sem("o_ready")
        pad_ready = sem("pad_ready")
        o_tr = sem("o_tr")
        oT_ready = sem("oT_ready")
        op_done, h2_ready = sem("op_done"), sem("h2_ready")
        gu_done, sig_ready = sem("gu_done"), sem("sig_ready")
        gate_ready, hid_ready = sem("gate_ready"), sem("hid_ready")
        down_done, y_ready = sem("down_done"), sem("y_ready")
        stored = sem("stored")
        rstd_ln = sem("rstd_ln")
        block = stack.enter_context(nc.Block())

        HV = G // 2
        UNITS = 2 * HK

        STEPS_AT = [[], [("logs", 0)], [("logs", 1)],
                    [("logs", 2), ("set", SIG_ATAN), ("tanh", 0)],
                    [("atan", 0), ("set", LN_EXP), ("logs", 3)],
                    [("ln", 0), ("logs", 4)], [("exp", 0), ("logs", 5)], [("logs", 6)]]
        ANGLES_AT = {-1: (1, "tanh"), 1: (2, "tanh"), 3: (3, "tanh"), 5: (1, "atan"), 7: (2, "atan"), 9: (3, "atan")}
        POWERS = [(1, "ln"), (1, "exp"), (2, "ln"), (3, "ln"), (2, "exp"), (3, "exp")]
        MASS_AT = {0: 1, 1: 2, 3: 3}
        X2_AT = 2
        OUT_ON_DVE = {0, 1}
        V_AT = {4: 0, 5: 1, 6: 2, 7: 3}
        DOWN_AT = {-1: (0,), 0: (1,), 1: (2,), 2: (3,), 3: (4,), 4: (5,)}
        JOBS = []
        for s in range(-1, G + 1):
            if 0 <= s < G:
                JOBS.append(("pv", s, 0, outT_ready, G, s))
                JOBS.append(("out", s, 0, o_ready, G, s))
            if s > 0:
                JOBS.append(("oT", s - 1, 0, oT_ready, G, s - 1))
            JOBS += [("down", t, -1, y_ready, NR, t) for t in DOWN_AT.get(s, ())]
            if s in V_AT:
                JOBS.append(("v", V_AT[s], 1, v_ready, 4, V_AT[s]))
        JOBS += [("x1T", n, 2, x1T_ready, 3, n) for n in range(3)]
        JOBS += [("qk", (kind, u), 2, raw_ready if kind == "proj" else n2_ln, 8, u) for kind, u in QK_ORDER]
        JOBS += [("x2T", n, 0, x2T_ready, 3, n) for n in range(3)]
        JOBS += [("gu", (kind, u), 0, gate_ready if kind == "gate" else hid_ready, UNITS, u)
                 for u in range(UNITS) for kind in ("gate", "up")]
        assert len(JOBS) % 4 == 0
        NUMBER = {(j[0], j[1]): n for n, j in enumerate(JOBS)}

        def claim(eng, it, before, now, stage, which):
            n = NUMBER[stage, which]
            bank, back, offs = 4 + n % 4, 0, now
            n -= 4
            while True:
                if n < 0:
                    if back:
                        return bank
                    n, back, offs = n + len(JOBS), 1, before
                _, _, off, read, per, i = JOBS[n]
                if off in offs:
                    eng.wait_ge(read, (it + off - back) * per + i + 1)
                    return bank
                n -= 4

        def bank(b, n, rows=P, c=0):
            return ps[0:rows, b, c:c + n]

        def iterate(eng, body):
            every = {-1, 0, 1, 2}
            body(-2, set(), {2})
            body(-1, {2}, {1, 2})
            body(0, {1, 2}, {0, 1, 2})
            with eng.Fori(1, NG - 2) as it:
                body(it, every, every)
            body(NG - 2, every, {-1, 0, 1})
            body(NG - 1, {-1, 0, 1}, {-1, 0})
            body(NG, {-1, 0}, {-1})

        def qk_parts(u, q, k):
            f, hf = UNIT_OF[u]
            cols = slice(hf * HALF, (hf + 1) * HALF)
            if f < CK:
                return q[:, f, :, cols], raw[:, u % 3]
            return k[:, f - CK, cols], raw[:, u % 3, 0]

        @block.sync
        def _(sync):
            rows_in = h_all.rearrange("b s c -> (b s) c")
            rows_out = out.rearrange("b s c -> (b s) c")

            def part(rows, g):
                return rows[g * TG:(g + 1) * TG] if isinstance(g, int) else rows[bass.ds(g * TG, TG)]

            def load(dst, g, done):
                rows = part(rows_in, g)
                sync.dma_start(dst[:, 0:NR - 1, :],
                               rows[0:P * (NR - 1)].rearrange("(t p) c -> p t c", p=P)).then_inc(done, 16)
                sync.dma_start(dst[:, NR - 1, :], rows[TG - P:TG]).then_inc(done, 16)

            def body(it, before, now):
                if 2 in now:
                    if 2 in before:
                        sync.wait_ge(x1_tr, (it + 2) * 3)
                    load(h_in, it + 2, h_loaded)
                if -1 in now:
                    sync.wait_ge(y_ready, it * NR)
                    dst = part(rows_out, it - 1)
                    sync.dma_start(dst[0:P * (NR - 1)].rearrange("(t p) c -> p t c", p=P), h2[:, 0:NR - 1, :]
                                   ).then_inc(stored, 16)
                    rest = TG - P * (NR - 1)
                    sync.dma_start(dst[P * (NR - 1):TG], h2[P - rest:P, NR - 1, :]).then_inc(stored, 16)
                if 1 in now:
                    if 0 in now:
                        sync.wait_ge(h2_ready, (it + 1) * NR)
                    load(h_bias, it + 1, hr_loaded)

            iterate(sync, body)
            sync.wait_ge(stored, 32 * NG)

        @block.gpsimd
        def _(pool):
            pool.memset(vw_all[:, :, NH * VD:VW], 0.0).then_inc(pad_ready, 1)

            def scale_values(it, k):
                pool.wait_ge(rm_ready, it * HV + k + 1)
                for s in (2 * k, 2 * k + 1):
                    last = pool.tensor_tensor(vw[0:S, s, :, 0:HD], vw[0:S, s, :, 0:HD],
                                              vw[0:S, s, :, HD:VD].to_broadcast([S, NH, HD]), ALU.mult)
                last.then_inc(vw_ready, 1)

            def difference(g, s):
                pool.wait_ge(ln_ready, g * G + s + 1)
                pool.tensor_tensor(sc[0:S, s, :], lnp[0:S, s % 3, :], sc[0:S, s, :], ALU.subtract).then_inc(x_ready, 1)

            def add_bias(it):
                pool.wait_ge(hr_loaded, 32 * (it + 1))
                pool.tensor_tensor(h_bias[:], h_bias[:], w.out_bias[:].unsqueeze(1).to_broadcast([P, NR, C]), ALU.add
                                   ).then_inc(hb_ready, 1)

            def body(it, before, now):
                for s in range(G):
                    if 0 in now and s in MASS_AT:
                        scale_values(it, MASS_AT[s])
                    if 0 in now and s == 4:
                        add_bias(it)
                    if 1 in now and s:
                        difference(it + 1, s - 1)
                if 1 in now:
                    difference(it + 1, G - 1)
                for u in range(4, 8 if 2 in now else 0):
                    pool.wait_ge(hi_ready, (it + 2) * 8 + u + 1)
                    (lo, x), (hi, _) = qk_parts(u, qT_lo, kT_lo), qk_parts(u, qT, kT)
                    pool.tensor_tensor(lo, x, hi, ALU.subtract).then_inc(k_lo_ready, 1)
                if 1 in now:
                    scale_values(it + 1, 0)

            iterate(pool, body)

        @block.scalar
        def _(act):
            def rstd_order(it, which):
                if isinstance(it, int) and it < 0:
                    return it + 3
                if isinstance(it, int) and it > NG - 3:
                    return NG + it + 1
                return 2 * it + 2 + which

            def rstd(dst, mv, got, g, done, order):
                act.wait_ge(got, g + 1)
                act.activation(dst[:], mv[:, :, 1], ACT.Ln, bias=LN_EPS).then_inc(rstd_ln, 1)
                act.wait_ge(rstd_ln, order)
                act.activation(dst[:], dst[:], ACT.Exp, scale=-0.5).then_inc(done, 1)

            def logs(it, s):
                act.wait_ge(clip_ready, it * 2 * G + 2 * s + 2)
                if s >= 3:
                    act.wait_ge(x_ready, it * G + s - 2)
                act.activation(lnp[0:S, s % 3, :], sc[0:S, s, :], ACT.Ln, bias=1.0)
                act.activation(sc[0:S, s, :], sc[0:S, s, :], ACT.Ln, bias=1.0, scale=-1.0).then_inc(ln_ready, 1)

            def qk_raw(g, u):
                f, hf = UNIT_OF[u]
                b = 4 + NUMBER["qk", ("proj", u)] % 4
                act.wait_ge(qk_done, g * 8 + u + 1)
                if u >= 2:
                    act.wait_ge(n2_done, g * 8 + u - 1)
                act.activation(sq[:, u % 2, :], bank(b, HALF), ACT.Square, bias=w.q_bias[:, f:f + 1]
                               ).then_inc(sq_ready, 1)
                if u >= 3:
                    act.wait_ge(q_lo_ready if u < 7 else k_lo_ready, g * 4 + (u - 3) % 4 + 1)
                if f < CK:
                    for e in range(2):
                        last = act.activation(raw[:, u % 3, e, :], bank(b, HALF), ACT.Identity,
                                              bias=w.q_bias_m[:, f, e:e + 1], scale=w.head_row[:, e:e + 1])
                else:
                    last = act.activation(raw[:, u % 3, 0, :], bank(b, HALF), ACT.Identity, bias=w.q_bias[:, f:f + 1])
                last.then_inc(raw_ready, 1)

            def qk_norm(g, u):
                b = 4 + NUMBER["qk", ("norm", u)] % 4
                act.wait_ge(n2_done, g * 8 + u + 1)
                if u >= 3:
                    act.wait_ge(unit_ready, g * 8 + u - 2)
                act.activation(inv[:, u % 3, :], bank(b, HALF), ACT.Ln, bias=N2_BIAS, scale=N2_SCALE
                               ).then_inc(n2_ln, 1)
                act.wait_ge(n2_ln, g * 8 + u + 1)
                act.activation(inv[:, u % 3, :], inv[:, u % 3, :], ACT.Exp, bias=N2_SHIFT, scale=-0.5
                               ).then_inc(inv_ready, 1)

            def two(k):
                return sc[0:S, 2 * k:2 * k + 2, :]

            def angle(g, k, step):
                if step == "tanh":
                    act.wait_ge(x_ready, g * G + 2 * k + 2)
                    act.activation(two(k), two(k), ACT.Tanh, scale=0.25).then_inc(tanh_ready, 1)
                else:
                    act.wait_ge(tanh_ready, g * HV + k + 1)
                    act.activation(two(k), two(k), ACT.Arctan).then_inc(atan_ready, 1)

            def sigmoid(g, u):
                b = 4 + NUMBER["gu", ("gate", u)] % 4
                act.wait_ge(gu_done, g * UNITS + u + 1)
                if u >= 2:
                    act.wait_ge(gate_ready, g * UNITS + u - 1)
                act.activation(sig[:, u % 2, :], bank(b, HALF), ACT.Sigmoid).then_inc(sig_ready, 1)

            def power(g, k, step):
                if step == "ln":
                    act.wait_ge(atan_ready, g * HV + k + 1)
                    act.activation(two(k), two(k), ACT.Ln, bias=1.0 + HALF_PI, scale=-2.0).then_inc(ln_g, 1)
                else:
                    act.wait_ge(ln_g, g * HV + k + 1)
                    act.activation(two(k), two(k), ACT.Exp, scale=POWER).then_inc(a_ready, 1)

            def out_turned(it, s):
                act.wait_ge(o_tr, it * G + s + 1)
                act.activation(oT[:, :, s * S:(s + 1) * S],
                               bank(4 + NUMBER["oT", s] % 4, CK * S).rearrange("p (c n) -> p c n", c=CK), ACT.Copy
                               ).then_inc(oT_ready, 1)

            def weighted_out(it, s):
                act.wait_ge(pv_done, it * G + s + 1)
                act.activation(outT[:, s % 2, :], bank(4 + NUMBER["pv", s] % 4, NH * S // 4), ACT.Copy
                               ).then_inc(outT_ready, 1)

            def body(it, before, now):
                if now == {2}:
                    act.preload_act_table_set(LN_EXP)
                for s in range(G):
                    if 0 in now and s not in OUT_ON_DVE:
                        weighted_out(it, s)
                    if s == 2 and 2 in now:
                        rstd(rstd1, mv1, mv1_ready, it + 2, rstd1_ready, rstd_order(it, 1))
                    for step, n in STEPS_AT[s] if 1 in now else ():
                        if step == "logs":
                            logs(it + 1, n)
                        elif step == "set":
                            act.preload_act_table_set(n)
                        elif step in ("tanh", "atan"):
                            angle(it + 1, n, step)
                        else:
                            power(it + 1, n, step)
                    if 0 in now and s:
                        out_turned(it, s - 1)
                if 1 in now:
                    logs(it + 1, G - 1)
                if 0 in now:
                    out_turned(it, G - 1)
                    if 2 not in now:
                        rstd(rstd2, mv2, mv2_ready, it, rstd2_ready, rstd_order(it, 2))
                for u in range(8 if 2 in now else 0):
                    qk_raw(it + 2, u)
                    if u:
                        qk_norm(it + 2, u - 1)
                    if u == X2_AT - 1 and 0 in now:
                        rstd(rstd2, mv2, mv2_ready, it, rstd2_ready, rstd_order(it, 2))
                if 2 in now:
                    qk_norm(it + 2, 7)
                if now & {0, 1}:
                    act.preload_act_table_set(SIG_ATAN)
                for u in range(-1, UNITS):
                    if u >= 0 and 0 in now:
                        sigmoid(it, u)
                    if 1 in now and u in ANGLES_AT:
                        angle(it + 1, *ANGLES_AT[u])
                if 1 in now:
                    act.preload_act_table_set(LN_EXP)
                    for k, step in POWERS:
                        power(it + 1, k, step)

            iterate(act, body)

        @block.vector
        def _(dve):
            def moments(h, mv, done):
                for t in range(NR):
                    last = dve.bn_stats(stats[:, t, :], h[:, t, :])
                dve.drain()
                for t in range(NR):
                    last = dve.bn_aggr(mv[:, t, :], stats[:, t, :])
                last.then_inc(done, 1)

            def moments1(g):
                dve.wait_ge(h_loaded, 32 * (g + 1))
                moments(h_in, mv1, mv1_ready)

            def moments2(g):
                dve.wait_ge(h2_ready, NR * (g + 1))
                moments(h2, mv2, mv2_ready)

            def normalise(x, h, mv, rs, mv_got, rs_got, g, done):
                dve.wait_ge(mv_got, g + 1)
                dve.wait_ge(rs_got, g + 1)
                for t in range(NR):
                    dve.tensor_scalar(x[:, t, :], h[:, t, :], mv[:, t, 0:1], rs[:, t:t + 1],
                                      ALU.subtract, ALU.mult).then_inc(done, 1)

            def turned(xT, stage, tr, ready, g):
                for n in range(3):
                    b = 4 + NUMBER[stage, n] % 4
                    dve.wait_ge(tr, g * 3 + n + 1)
                    if n < CK:
                        dve.tensor_copy(xT[:, n, 0:4 * P], bank(b, 4 * P)).then_inc(ready, 1)
                    else:
                        tail = bank(b, 4 * P).rearrange("p (c n) -> p c n", c=CK)
                        rest = TG - 5 * P
                        dve.tensor_copy(xT[:, :, 4 * P:5 * P], tail[:, :, 0:P])
                        dve.tensor_copy(xT[:, :, 5 * P:TG], tail[:, :, 2 * P - rest:2 * P]).then_inc(ready, 1)

            def values(it, k):
                b = 4 + NUMBER["v", k] % 4
                dve.wait_ge(v_done, it * 4 + k + 1)
                for i in range(2):
                    last = dve.tensor_tensor(vw[0:S, 2 * k + i, :, 0:HD],
                                             bank(b, C, S, i * C).rearrange("p (h d) -> p h d", d=HD),
                                             w.v_bias[0:S].rearrange("p (h d) -> p h d", d=HD), ALU.add)
                last.then_inc(v_ready, 1)

            def clip(g, s, q):
                dve.wait_ge(s_done, g * 2 * G + 2 * s + q + 1)
                dve.tensor_scalar(sc[0:S, s, 4 * PAIR * q:4 * PAIR * (q + 1)].rearrange("p (b n) -> p b n", b=2),
                                  ps[0:S, 2 * q:2 * q + 2, 0:2 * PAIR], -1.0 + COS_EPS, 1.0 - COS_EPS,
                                  ALU.max, ALU.min).then_inc(clip_ready, 1)

            def qk_unit(g, u):
                dve.wait_ge(inv_ready, g * 8 + u + 1)
                dve.wait_ge(raw_ready, g * 8 + u + 1)
                for e in range(2 if UNIT_OF[u][0] < CK else 1):
                    last = dve.scalar_tensor_tensor(out=raw[:, u % 3, e, :], in0=inv[:, u % 3, :], scalar=1e12,
                                                    in1=raw[:, u % 3, e, :], op0=ALU.min, op1=ALU.mult)
                last.then_inc(unit_ready, 1)

            def qk_high(g, u):
                dve.wait_ge(unit_ready, g * 8 + u + 1)
                dve.tensor_copy(*qk_parts(u, qT, kT)).then_inc(hi_ready, 1)

            def q_low(g, u):
                dve.wait_ge(hi_ready, g * 8 + u + 1)
                (lo, x), (hi, _) = qk_parts(u, qT_lo, kT_lo), qk_parts(u, qT, kT)
                dve.tensor_tensor(lo, x, hi, ALU.subtract).then_inc(q_lo_ready, 1)

            def mlp_unit(g, u):
                j, hf = u % HK, u // HK
                dve.wait_ge(sig_ready, g * UNITS + u + 1)
                dve.tensor_tensor(act_gate[:, u % 2, :], bank(4 + NUMBER["gu", ("gate", u)] % 4, HALF),
                                  sig[:, u % 2, :], ALU.mult).then_inc(gate_ready, 1)
                dve.wait_ge(gate_ready, g * UNITS + u + 1)
                dve.tensor_tensor(hid[:, j, hf * HALF:(hf + 1) * HALF],
                                  bank(4 + NUMBER["gu", ("up", u)] % 4, HALF), act_gate[:, u % 2, :], ALU.mult
                                  ).then_inc(hid_ready, 1)

            def result(g, t):
                dve.wait_ge(down_done, g * NR + t + 1)
                dve.tensor_tensor(h2[:, t, :], bank(4 + NUMBER["down", t] % 4, C), h2[:, t, :], ALU.add
                                  ).then_inc(y_ready, 1)

            def key_mass(it, k):
                dve.wait_ge(a_ready, it * HV + k + 1)
                dve.wait_ge(v_ready, it * 4 + k + 1)
                dve.tensor_reduce(mass[0:S, k % 2, :], sc[0:S, 2 * k:2 * k + 2, :].rearrange("p s (h q) -> p (s h) q", q=S),
                                  AX.X, ALU.add).then_inc(mass_ready, 1)
                dve.wait_ge(mass_ready, it * HV + k + 1)
                dve.reciprocal(vw[0:S, 2 * k:2 * k + 2, :, HD], mass[0:S, k % 2, :].rearrange("p (s h) -> p s h", h=NH)
                               ).then_inc(rm_ready, 1)

            def weighted_out(it, s):
                dve.wait_ge(pv_done, it * G + s + 1)
                dve.tensor_copy(outT[:, s % 2, :], bank(4 + NUMBER["pv", s] % 4, NH * S // 4)).then_inc(outT_ready, 1)

            def head_out(it, s):
                pv = bank(4 + NUMBER["out", s] % 4, NH * VS, S).rearrange("p (h d) -> p h d", d=VS)
                dve.wait_ge(out_tr, it * G + s + 1)
                dve.tensor_scalar(osum[0:S, s % 2, :], pv[:, :, HD], 1e-12, None, ALU.max).then_inc(osum_ready, 1)
                dve.wait_ge(osum_ready, it * G + s + 1)
                dve.reciprocal(osum[0:S, s % 2, :], osum[0:S, s % 2, :]).then_inc(orec_ready, 1)
                dve.wait_ge(orec_ready, it * G + s + 1)
                if s >= 2:
                    dve.wait_ge(o_tr, it * G + s - 1)
                dve.tensor_tensor(o[0:S, s % 2, :].rearrange("p (h d) -> p h d", d=HD), pv[:, :, 0:HD],
                                  osum[0:S, s % 2, :].unsqueeze(2).to_broadcast([S, NH, HD]), ALU.mult
                                  ).then_inc(o_ready, 1)

            def residual(it, t, before):
                dve.wait_ge(op_done, it * NR + t + 1)
                if t == 0:
                    dve.wait_ge(hb_ready, it + 1)
                    if 0 in before:
                        dve.wait_ge(stored, 32 * it)
                dve.tensor_tensor(h2[:, t, :], bank(t % 4, C), h_bias[:, t, :], ALU.add).then_inc(h2_ready, 1)

            def body(it, before, now):
                out_, score, proj = 0 in now, 1 in now, 2 in now
                down = -1 in now
                for t in DOWN_AT[-1] if down else ():
                    result(it - 1, t)
                if proj:
                    if not out_:
                        moments1(it + 2)
                for s in range(G):
                    if out_ and s in OUT_ON_DVE:
                        weighted_out(it, s)
                    if score:
                        clip(it + 1, s, 0)
                    if out_:
                        head_out(it, s)
                    if score:
                        clip(it + 1, s, 1)
                    if out_ and s in MASS_AT:
                        key_mass(it, MASS_AT[s])
                    for t in DOWN_AT.get(s, ()) if down else ():
                        result(it - 1, t)
                    if score and s in V_AT:
                        values(it + 1, V_AT[s])
                    if proj and out_ and s == 1:
                        moments1(it + 2)
                    if proj and s == 6:
                        normalise(x1, h_in, mv1, rstd1, mv1_ready, rstd1_ready, it + 2, x1_ready)
                if out_:
                    for t in range(NR):
                        residual(it, t, before)
                if proj:
                    turned(x1T, "x1T", x1_tr, x1T_ready, it + 2)
                if out_:
                    moments2(it)
                    if not proj:
                        normalise(x2, h2, mv2, rstd2, mv2_ready, rstd2_ready, it, x2_ready)
                if proj:
                    for u in range(8):
                        if out_ and u == X2_AT:
                            normalise(x2, h2, mv2, rstd2, mv2_ready, rstd2_ready, it, x2_ready)
                        qk_unit(it + 2, u)
                        qk_high(it + 2, u)
                        if u < 4:
                            q_low(it + 2, u)
                if out_:
                    turned(x2T, "x2T", x2_tr, x2T_ready, it)
                if score:
                    key_mass(it + 1, 0)
                if out_:
                    for u in range(UNITS):
                        mlp_unit(it, u)

            iterate(dve, body)

        @block.tensor
        def _(pe):
            def values(it, k, before, now):
                b = claim(pe, it, before, now, "v", k)
                if k == 0:
                    pe.wait_ge(x1T_ready, 3 * (it + 2))
                for i in range(2):
                    c0 = (2 * k + i) * S
                    for c in range(CK):
                        last = pe.matmul(bank(b, C, S, i * C), x1T[:, c, c0:c0 + S], w.v[:, c, :],
                                         start=(c == 0), stop=(c == CK - 1))
                last.then_inc(v_done, 1)

            def scores(it, s, q, before):
                g = it + 1
                if s == 0 and q == 0:
                    pe.wait_ge(hi_ready, 8 * (g + 1))
                    pe.wait_ge(q_lo_ready, 4 * (g + 1))
                    pe.wait_ge(k_lo_ready, 4 * (g + 1))
                    if 0 in before:
                        pe.wait_ge(h2_ready, it * NR)
                if s:
                    pe.wait_ge(clip_ready, g * 2 * G + 2 * (s - 1) + q + 1)
                at = slice(s * S, (s + 1) * S)
                for r in (2 * q, 2 * q + 1):
                    rows = slice(32 * r, 32 * r + 32)
                    for c in range(CK):
                        for n, (k_, q_) in enumerate(((kT, qT), (kT, qT_lo), (kT_lo, qT))):
                            last = pe.matmul(bank(r, PAIR, S, c * PAIR), k_[rows, c, at], q_[rows, c, :, at],
                                             start=(n == 0), stop=(n == 2))
                last.then_inc(s_done, 1)

            def turn(it, x, ready, stage, tr, g, before, now):
                for n in range(3):
                    b = claim(pe, it, before, now, stage, n)
                    if n == 0:
                        pe.wait_ge(ready, g * NR + 4)
                    if n == 2:
                        pe.wait_ge(ready, g * NR + NR)
                    parts = [(t, n) for t in range(4)] if n < CK else [(t, c) for c in range(CK) for t in (4, 5)]
                    for i, (t, c) in enumerate(parts):
                        last = pe.transpose(bank(b, P, P, i * P), x[:, t, c * P:(c + 1) * P], w.ident[:])
                    last.then_inc(tr, 1)

            def qk(it, before, now):
                g = it + 2
                pe.wait_ge(x1T_ready, 3 * g + 2)
                for kind, u in QK_ORDER:
                    b = claim(pe, it, before, now, "qk", (kind, u))
                    f, hf = UNIT_OF[u]
                    if (kind, u) == ("proj", 1):
                        pe.wait_ge(x1T_ready, 3 * (g + 1))
                    if kind == "proj":
                        for c in range(CK):
                            last = pe.matmul(bank(b, HALF), w.qk[:, c, f * P:(f + 1) * P],
                                             x1T[:, c, hf * HALF:(hf + 1) * HALF], start=(c == 0), stop=(c == CK - 1))
                        last.then_inc(qk_done, 1)
                    else:
                        pe.wait_ge(sq_ready, g * 8 + u + 1)
                        pe.matmul(bank(b, HALF), w.head_sum[:], sq[:, u % 2, :], start=True, stop=True
                                  ).then_inc(n2_done, 1)

            def gate_up(it, u, before, now):
                j, hf = u % HK, u // HK
                if j == 0:
                    pe.wait_ge(x2T_ready, 3 * it + 2 + hf)
                for i, kind in enumerate(("gate", "up")):
                    b = claim(pe, it, before, now, "gu", (kind, u))
                    for c in range(CK):
                        last = pe.matmul(bank(b, HALF), w.gu[:, c, i * HID + j * P:i * HID + (j + 1) * P],
                                         x2T[:, c, hf * HALF:(hf + 1) * HALF], start=(c == 0), stop=(c == CK - 1))
                last.then_inc(gu_done, 1)

            def down(it, t, before, now):
                b = claim(pe, it, before, now, "down", t)
                if t == 0:
                    pe.wait_ge(hid_ready, UNITS * (it - 1) + HK)
                elif t == HALF // P:
                    pe.wait_ge(hid_ready, UNITS * it)
                for k in range(HK):
                    last = pe.matmul(bank(b, C), hid[:, k, ROWS[t]:ROWS[t] + P], w.d[:, k, :],
                                     start=(k == 0), stop=(k == HK - 1))
                last.then_inc(down_done, 1)

            def weighted(it, s, before, now):
                b = claim(pe, it, before, now, "pv", s)
                if s == 0 and isinstance(it, int) and it == 0:
                    pe.wait_ge(pad_ready, 1)
                if s % 2 == 0:
                    pe.wait_ge(vw_ready, it * HV + s // 2 + 1)
                for h in range(NH):
                    i = h % 4
                    last = pe.matmul(ps[VS * i:VS * (i + 1), b, (h // 4) * S:(h // 4 + 1) * S],
                                     vw_all[0:S, s, h * VD:h * VD + VS], sc[0:S, s, h * S:(h + 1) * S],
                                     start=True, stop=True)
                last.then_inc(pv_done, 1)

            def turn_back(it, s, before, now):
                b = claim(pe, it, before, now, "out", s)
                pe.wait_ge(outT_ready, it * G + s + 1)
                for n in range(NH // 4):
                    last = pe.transpose(bank(b, P, S, n * P), outT[:, s % 2, n * S:(n + 1) * S], w.ident[:])
                last.then_inc(out_tr, 1)

            def turn_o(it, s, before, now):
                b = claim(pe, it, before, now, "oT", s)
                pe.wait_ge(o_ready, it * G + s + 1)
                for c in range(CK):
                    last = pe.transpose(bank(b, S, P, c * S), o[0:S, s % 2, c * P:(c + 1) * P],
                                        w.ident[0:S, 0:S])
                last.then_inc(o_tr, 1)

            def project(it, t, now):
                pe.wait_ge(oT_ready, it * G + -(-(ROWS[t] + P) // S))
                if t >= 4:
                    pe.wait_ge(h2_ready, it * NR + t - 3)
                elif t == 0 and 1 in now:
                    pe.wait_ge(clip_ready, (it + 2) * 2 * G)
                for c in range(CK):
                    last = pe.matmul(bank(t % 4, C), oT[:, c, ROWS[t]:ROWS[t] + P], w.out[:, c, :],
                                     start=(c == 0), stop=(c == CK - 1))
                last.then_inc(op_done, 1)

            def body(it, before, now):
                for s in range(-1, G):
                    if s >= 0 and 0 in now:
                        weighted(it, s, before, now)
                    if s >= 0 and 1 in now:
                        scores(it, s, 0, before)
                    if s >= 0 and 0 in now:
                        turn_back(it, s, before, now)
                        if s:
                            turn_o(it, s - 1, before, now)
                    if s >= 0 and 1 in now:
                        scores(it, s, 1, before)
                    for t in DOWN_AT.get(s, ()) if -1 in now else ():
                        down(it, t, before, now)
                    if s in V_AT and 1 in now:
                        values(it, V_AT[s], before, now)
                if 0 in now:
                    turn_o(it, G - 1, before, now)
                    for t in range(NR):
                        project(it, t, now)
                if 2 in now:
                    turn(it, x1, x1_ready, "x1T", x1_tr, it + 2, before, now)
                    qk(it, before, now)
                if 0 in now:
                    turn(it, x2, x2_ready, "x2T", x2_tr, it, before, now)
                    for u in range(UNITS):
                        gate_up(it, u, before, now)

            iterate(pe, body)


UNIT_OF = [(f, hf) for f in range(2 * CK) for hf in range(2)]
QK_ORDER = [("proj", 0)] + [x for u in range(1, 8) for x in (("proj", u), ("norm", u - 1))] + [("norm", 7)]


def program(nc, a, out):
    h_all = nc.dram_tensor("tokens", [B, S, C], F32).ap()
    with ExitStack() as stack:
        mem = Names(nc, stack)
        w = Weights(mem)
        ps = stack.enter_context(nc.psum_tensor("ps", [P, 8, 512], F32))
        tokenizer(nc, a, w, ps, h_all)
        transformer(nc, a, w, ps, h_all, out)


def kernel(**inputs):
    import concourse.bacc as bacc
    import numpy as np
    from concourse.bass_utils import run_bass_kernel_spmd

    x = {n.removeprefix("L0_").removeprefix("tok_").removeprefix("attn_").removeprefix("ffn_"): np.asarray(v)
         for n, v in inputs.items()}
    order = [c * 8 + 2 * r + e for r in range(4) for c in range(CK) for e in range(2)]
    feats = np.array([h * HD + d for h in order for d in range(HD)])
    px = x["x"].reshape(B, 3, 2, 3, 14, 2, 3, 14).transpose(1, 4, 7, 2, 3, 6, 5, 0)
    data = {
        "patches": px.reshape(PATCH, NT * P),
        "conv_w": x["conv_w"].reshape(C, PATCH).T,
        "txt": x["txt"],
        "w_qk": x["w_qkv"][0:2 * C].T, "b_qk": x["b_qkv"][0:2 * C].reshape(2 * CK, P).T,
        "w_v": x["w_qkv"][2 * C:][feats].T, "b_v": x["b_qkv"][2 * C:][feats],
        "w_out": x["w_out"][:, feats].T, "b_out": x["b_out"],
        "w_gate": x["w_gate"].T, "w_up": x["w_up"].T, "w_down": x["w_down"].T,
        "ident": np.eye(P, dtype=np.float32),
        "pick": np.tile(np.eye(B, dtype=np.float32), (2, 1)),
        "head_sum": np.kron(np.eye(P // HD, dtype=np.float32), np.ones((HD, HD), np.float32)),
        "head_row": np.repeat(np.tile(np.eye(2, dtype=np.float32), (P // HD // 2, 1)), HD, axis=0),
    }
    gains = [x[f"{part}_ln_{side}_{kind}"] for part in ("la", "ga") for side in ("q", "kv") for kind in ("g", "b")]
    data["gains"] = np.stack(gains).reshape(8, CK, P).transpose(2, 0, 1)
    data["rows"] = np.stack([x["la_proj_b"], x["mod_b"], x["ga_proj_b"], x["class_emb"]])[None]
    for n in ("class_emb", "la_wq", "la_wkv", "la_proj_w", "ga_wq", "ga_wkv", "ga_proj_w", "mod_w"):
        data[n] = x[n]
    nc = bacc.Bacc("TRN2", target_bir_lowering=False, num_devices=1)
    arrays, aps = {}, {}
    for n, v in data.items():
        v = np.ascontiguousarray(v)
        arrays["in_" + n] = v
        aps[n] = nc.dram_tensor("in_" + n, v.shape, mybir.dt.from_np(v.dtype), kind="ExternalInput").ap()
    out = nc.dram_tensor("out", [B, S, C], F32, kind="ExternalOutput").ap()
    program(nc, aps, out)
    r = run_bass_kernel_spmd(nc, [arrays], core_ids=[0])
    return r.results[0]["out"]
```

```python
import math
from contextlib import ExitStack

import concourse.bass as bass
from concourse import mybir

F32 = mybir.dt.float32
F32R = mybir.dt.float32r
I32 = mybir.dt.int32
ALU = mybir.AluOpType
ACT = mybir.ActivationFunctionType
AX = mybir.AxisListType

P = 128
C = 256
CK = C // P
B = 64

H8, DH = 8, 32
WIN = 9
NW = 4
RT = B * NW // P
NT = RT * WIN
LOADS = [0, 3, 9]
KP, KN = 118, 5
PATCH = 3 * 14 * 14
KL = PATCH - KP * (KN - 1)
TOK_SCALE = C ** -0.5
LN_EPS = 1e-5

TXT = 77
S = NW + 1 + TXT
T = B * S
NH, HD = 16, 16
HID = 768
HK = HID // P
G = 8
NG = B // G
TG = G * S
HALF = TG // 2
SH = G // 2
ROWS = [0, 128, 256, 384, 512, TG - P]
NR = len(ROWS)
PAIR = 2 * S
SC = NH * S
VD = HD + 1
VS = 32
VW = (NH - 1) * VD + VS
COS_EPS = 1e-7
POWER = -3.2
HALF_PI = 1.5707963267948966
N2_SCALE = 2.0 ** 30
N2_BIAS = 2.0 ** -63
N2_SHIFT = 15 * 0.6931471805599453
SCALE_Q = 1.0 / 127.0

LN_EXP = "natural_log_exp_and_others"
SIG_ATAN = "sigmoid_and_others"


class Names:

    def __init__(self, nc, stack):
        self.nc, self.stack = nc, stack

    def sb(self, name, *shape, dt=F32):
        return self.stack.enter_context(self.nc.sbuf_tensor(name, [P, *shape], dt))

    def sem(self, name):
        return self.stack.enter_context(self.nc.semaphore(name))


class Weights:

    def __init__(self, mem):
        self.ident = mem.sb("ident", P)
        self.head_sum = mem.sb("head_sum", P)
        self.head_row = mem.sb("head_row", 2)
        self.q_bias = mem.sb("q_bias", 4)
        self.qk = mem.sb("w_qk", CK, 2 * C)
        self.v = mem.sb("w_v", CK, C)
        self.v_bias = mem.sb("v_bias", C)
        self.out = mem.sb("w_out", CK, C)
        self.out_bias = mem.sb("out_bias", C)
        self.gu = mem.sb("w_gate_up", CK, 2 * HID, dt=F32R)
        self.gu_lo = mem.sb("w_gate_up_lo", CK, 2 * HID, dt=F32R)
        self.d = mem.sb("w_down", HK, C)


def tokenizer(nc, a, w, ps, h_all):
    with ExitStack() as stack:
        mem = Names(nc, stack)
        sb, sem = mem.sb, mem.sem
        patches = sb("patches", KN, NT * P)
        ints = patches[:].rearrange("p k n -> p (k n)").bitcast(I32)
        gu_int = ints[:, 0:CK * 2 * HID].rearrange("p (k n) -> p k n", k=CK)
        gu_float = gu_int.bitcast(F32)
        d_int = ints[:, CK * 2 * HID:CK * 2 * HID + HK * C].rearrange("p (k n) -> p k n", k=HK)
        used = [CK * 2 * HID + HK * C]

        def late(*shape):
            n = math.prod(shape)
            view = patches[:].rearrange("p k n -> p (k n)")[:, used[0]:used[0] + n]
            used[0] += n
            assert used[0] <= KN * NT * P
            names = "abc"[:len(shape)]
            spec = f"p ({' '.join(names)}) -> p {' '.join(names)}"
            return view.rearrange(spec, **dict(zip(names[:-1], shape[:-1])))

        conv_w = sb("conv_w", KN, C)
        pe = sb("pe", NT, C)
        hat = pe
        kvT = sb("kvT", 4, CK, P)
        kv = sb("kv", NT, 2 * C)
        wq, wkv, wproj = sb("la_wq", CK, C), sb("la_wkv", CK, 2 * C), sb("la_proj", CK, C)
        gwq, gwkv, gproj = sb("ga_wq", CK, C), sb("ga_wkv", CK, 2 * C), sb("ga_proj", CK, C)
        mod = sb("mod_w", CK, C)
        gains = sb("gains", 8, CK)
        rows = sb("rows", 4, C)
        ones = sb("ones_row", P)
        pick = sb("pick", B)
        cls_in = sb("cls_in", C)
        st = sb("patch_stats", NT, 6)
        mv = sb("patch_mv", NT, 2)
        rstd = sb("patch_rstd", NT)
        red = sb("red", RT, C)
        rst, rmv, rrs = sb("red_stats", RT, 6), sb("red_mv", RT, 2), sb("red_rstd", RT)
        rhat = sb("red_hat", RT, C)
        rT = sb("redT", RT, CK, P)
        q = late(RT, C)
        s = sb("s", RT, WIN, H8)
        smax = sb("smax", RT, H8)
        den = sb("den", RT, H8)
        agg = late(RT, C)
        aggT = late(RT, CK, P)
        lo = late(RT, C)
        loT = late(RT, CK, P)
        patch_out = late(RT, C)
        lst, lmv, lrs = sb("lo_stats", RT, 6), sb("lo_mv", RT, 2), sb("lo_rstd", RT)
        lhat = late(RT, C)
        lhT = late(RT, CK, P)
        gkv = late(RT, 2 * C)
        cst, cmv, crs = sb("cls_stats", 6), sb("cls_mv", 2), sb("cls_rstd", 1)
        chat = sb("cls_hat", C)
        cT = sb("cls_hatT", CK, P)
        gq = late(C)
        gprod = late(RT, C)
        gs = sb("gs", RT, H8)
        gsT = late(RT * P)
        gm, gd = sb("gmax", B), sb("gden", B)
        gp = sb("gp", RT, H8)
        gaT = late(CK, B)
        cls_out = late(C)

        gu_scaled, d_scaled = sem("gu_scaled"), sem("d_scaled")
        gu_high, gu_split = sem("gu_high"), sem("gu_split")
        cls_loaded, first_loaded = sem("cls_loaded"), sem("first_loaded")
        conv_loaded, weights_loaded, main_loaded = sem("conv_loaded"), sem("weights_loaded"), sem("main_loaded")
        patches_loaded = [sem(f"patches_loaded_{n}") for n in range(len(LOADS))]
        txt_copied, tok_stored = sem("txt_copied"), sem("tok_stored")
        consts = sem("consts")
        conv_done, pe_ready = sem("conv_done"), sem("pe_ready")
        hat_done, tr_done, kvT_ready = sem("hat_done"), sem("tr_done"), sem("kvT_ready")
        kv_done, kv_ready = sem("kv_done"), sem("kv_ready")
        rstd_ready = sem("rstd_ready")
        red_mv_ready, red_rstd_ready, red_hat_ready = sem("red_mv_ready"), sem("red_rstd_ready"), sem("red_hat_ready")
        mv_ready = sem("mv_ready")
        red_tr, red_T, q_done, q_ready = sem("red_tr"), sem("red_T"), sem("q_done"), sem("q_ready")
        qk_prod, s_ready, e_ready, p_ready = sem("qk_prod"), sem("s_ready"), sem("e_ready"), sem("p_ready")
        dve_pv = sem("dve_pv")
        pv_prod, agg_ready, agg_tr, agg_T = sem("pv_prod"), sem("agg_ready"), sem("agg_tr"), sem("agg_T")
        proj_done, lo_ready, lo_tr, lo_T = sem("proj_done"), sem("lo_ready"), sem("lo_tr"), sem("lo_T")
        patch_done, patch_ready = sem("patch_done"), sem("patch_ready")
        lo_mv_ready, lo_rstd_ready, lo_hat_ready = sem("lo_mv_ready"), sem("lo_rstd_ready"), sem("lo_hat_ready")
        lh_tr, lh_T, gkv_done, gkv_ready = sem("lh_tr"), sem("lh_T"), sem("gkv_done"), sem("gkv_ready")
        cls_mv_ready, cls_rstd_ready, cls_hat_ready = sem("cls_mv_ready"), sem("cls_rstd_ready"), sem("cls_hat_ready")
        cls_tr, cls_T, gq_done, gq_ready = sem("cls_tr"), sem("cls_T"), sem("gq_done"), sem("gq_ready")
        gk_prod, gs_ready, gs_tr, gs_T = sem("gk_prod"), sem("gs_ready"), sem("gs_tr"), sem("gs_T")
        ge_ready, gp_T, gp_tr, gp_ready = sem("ge_ready"), sem("gp_T"), sem("gp_tr"), sem("gp_ready")
        gv_prod, ga_done, ga_T, cls_done, cls_ready = (
            sem("gv_prod"), sem("ga_done"), sem("ga_T"), sem("cls_done"), sem("cls_ready"))
        act_step = sem("act_step")
        dve_step = sem("dve_step")
        block = stack.enter_context(nc.Block())

        def cols(bank, c, n):
            return ps[:, bank, c:c + n]

        def pv_product(eng, j, n0, n1):
            t0, t1 = j * WIN + n0, j * WIN + n1
            eng.wait_ge(p_ready, j + 1)
            return eng.tensor_tensor(
                hat[:, t0:t1, :].rearrange("p n (h d) -> p (n h) d", d=DH),
                kv[:, t0:t1, C:2 * C].rearrange("p n (h d) -> p n h d", d=DH),
                s[:, j, n0:n1, :].unsqueeze(3).to_broadcast([P, n1 - n0, H8, DH]), ALU.mult)

        LAG = 3
        CLS_AT = 14
        Q1_AT = 5
        POOL_PV = 3

        @block.sync
        def _(sync):
            def patch_load(n):
                c0, c1 = LOADS[n] * P, (LOADS + [NT])[n + 1] * P
                sync.dma_start(patches[0:KP, 0:KN - 1, c0:c1],
                               a["patches"][0:KP * (KN - 1), c0:c1].rearrange("(k p) n -> p k n", p=KP)
                               ).then_inc(patches_loaded[n], 16)
                sync.dma_start(patches[0:KL, KN - 1, c0:c1], a["patches"][KP * (KN - 1):PATCH, c0:c1]
                               ).then_inc(patches_loaded[n], 16)

            sync.dma_start(conv_w[0:KP, 0:KN - 1, :],
                           a["conv_w"][0:KP * (KN - 1), :].rearrange("(k p) n -> p k n", p=KP)).then_inc(conv_loaded, 16)
            sync.dma_start(conv_w[0:KL, KN - 1, :], a["conv_w"][KP * (KN - 1):PATCH, :]).then_inc(conv_loaded, 16)
            for n in range(len(LOADS)):
                patch_load(n)
            sync.dma_start(h_all[:, NW + 1:S, :], a["txt"]).then_inc(txt_copied, 16)
            sync.wait_ge(patch_ready, RT)
            for j in range(RT):
                for hx in range(2):
                    sync.dma_start(h_all[:, 2 * j + hx, :], patch_out[64 * hx:64 * hx + B, j, :]).then_inc(tok_stored, 16)
            sync.wait_ge(cls_ready, 1)
            sync.dma_start(h_all[:, NW, :], cls_out[0:B, :]).then_inc(tok_stored, 16)
            sync.wait_ge(tok_stored, 16 * (2 * RT + 1))
            sync.wait_ge(txt_copied, 16)

        @block.gpsimd
        def _(pool):
            pool.memset(ones[:], 1.0).then_inc(consts, 1)
            pool.dma_start(cls_in[:], a["class_emb"].partition_broadcast(P)).then_inc(cls_loaded, 16)
            pool.dma_start(w.ident[:], a["ident"]).then_inc(first_loaded, 16)
            pool.dma_start(gains[:], a["gains"]).then_inc(first_loaded, 16)
            for dst, src, done in ((wq[:], a["la_wq"], first_loaded), (gwq[:], a["ga_wq"], first_loaded),
                                   (wkv[:], a["la_wkv"], weights_loaded), (wproj[:], a["la_proj_w"], weights_loaded),
                                   (mod[:], a["mod_w"], weights_loaded), (gwkv[:], a["ga_wkv"], weights_loaded),
                                   (gproj[:], a["ga_proj_w"], weights_loaded)):
                pool.dma_start(dst, src.rearrange("(k p) n -> p k n", p=P)).then_inc(done, 16)
            pool.dma_start(rows[0:1], a["rows"]).then_inc(weights_loaded, 16)
            pool.dma_start(pick[:], a["pick"]).then_inc(weights_loaded, 16)
            pool.wait_ge(conv_done, LOADS[-1] + 1)
            for dst, src in ((w.qk[:], a["w_qk"]), (w.v[:], a["w_v"]), (w.out[:], a["w_out"]),
                             (gu_int[:, :, 0:HID], a["w_gate"]), (gu_int[:, :, HID:2 * HID], a["w_up"]),
                             (d_int, a["w_down"])):
                if src is a["w_gate"]:
                    pool.wait_ge(conv_done, NT)
                pool.dma_start(dst, src.rearrange("(k p) n -> p k n", p=P)).then_inc(main_loaded, 16)
            pool.dma_start(w.q_bias[:], a["b_qk"]).then_inc(main_loaded, 16)
            pool.dma_start(w.head_row[:], a["head_row"]).then_inc(main_loaded, 16)
            pool.dma_start(w.head_sum[:], a["head_sum"]).then_inc(main_loaded, 16)
            pool.dma_start(w.v_bias[:], a["b_v"].partition_broadcast(P)).then_inc(main_loaded, 16)
            pool.dma_start(w.out_bias[:], a["b_out"].partition_broadcast(P)).then_inc(main_loaded, 16)
            def qk_product(t):
                pool.wait_ge(kv_ready, t + 1)
                pool.wait_ge(q_ready, t // WIN + 1)
                pool.wait_ge(tr_done, t + 1)
                pool.tensor_tensor(hat[:, t, :], kv[:, t, 0:C], q[:, t // WIN, :], ALU.mult).then_inc(qk_prod, 1)

            for t in range(NT):
                qk_product(t)
                if t == WIN + LAG + 2:
                    pv_product(pool, 0, 0, WIN).then_inc(pv_prod, 1)
            pv_product(pool, 1, 0, POOL_PV).then_inc(pv_prod, 1)
            for j in range(RT):
                pool.wait_ge(gkv_ready, j + 1)
                pool.wait_ge(gq_ready, 1)
                pool.tensor_tensor(gprod[:, j, :], gkv[:, j, 0:C], gq[:], ALU.mult).then_inc(gk_prod, 1)
            pool.wait_ge(gu_high, 1)
            pool.tensor_tensor(w.gu_lo[:], gu_float, w.gu[:], ALU.subtract).then_inc(gu_split, 1)
            for j in range(RT):
                pool.wait_ge(gp_ready, j + 1)
                pool.tensor_tensor(gprod[:, j, :].rearrange("p (h d) -> p h d", d=DH),
                                   gkv[:, j, C:2 * C].rearrange("p (h d) -> p h d", d=DH),
                                   gp[:, j, :].unsqueeze(2).to_broadcast([P, H8, DH]), ALU.mult).then_inc(gv_prod, 1)

        @block.scalar
        def _(act):
            act.preload_act_table_set(LN_EXP)

            act_count = [0]

            def rsqrt(dst, var, got, n, done):
                act.wait_ge(got, n)
                act.activation(dst, var, ACT.Ln, bias=LN_EPS).then_inc(act_step, 1)
                act_count[0] += 1
                act.wait_ge(act_step, act_count[0])
                act.activation(dst, dst, ACT.Exp, scale=-0.5).then_inc(done, 1)

            def evac_pe(t):
                act.wait_ge(conv_done, t + 1)
                act.activation(pe[:, t, :], cols(t % 4, 0, C), ACT.Copy).then_inc(pe_ready, 1)

            def evac_kv(t):
                act.wait_ge(kv_done, t + 1)
                act.activation(kv[:, t, :], cols(6 + t % 2, 0, 2 * C), ACT.Copy).then_inc(kv_ready, 1)

            for t in range(WIN):
                evac_pe(t)
            rsqrt(rstd[:, 0:WIN], mv[:, 0:WIN, 1], mv_ready, 1, rstd_ready)
            rsqrt(rrs[:, 0:1], rmv[:, 0, 1:2], red_mv_ready, 1, red_rstd_ready)
            rsqrt(crs[:], cmv[:, 1:2], cls_mv_ready, 1, cls_rstd_ready)
            for t in range(WIN, NT):
                evac_pe(t)
            rsqrt(rstd[:, WIN:NT], mv[:, WIN:NT, 1], mv_ready, 2, rstd_ready)
            rsqrt(rrs[:, 1:2], rmv[:, 1, 1:2], red_mv_ready, 2, red_rstd_ready)
            def scaled_q(j):
                act.wait_ge(q_done, j + 1)
                act.activation(q[:, j, :], cols(7 - 6 * j, 0, C), ACT.Copy, scale=TOK_SCALE).then_inc(q_ready, 1)

            def window_exp(j):
                act.wait_ge(s_ready, j + 1)
                act.activation(s[:, j], s[:, j], ACT.Exp).then_inc(e_ready, 1)

            def evac_gkv(j):
                act.wait_ge(gkv_done, j + 1)
                act.activation(gkv[:, j, :], cols(4 + j, 0, 2 * C), ACT.Copy).then_inc(gkv_ready, 1)

            def evac_patch(j):
                act.wait_ge(patch_done, j + 1)
                act.activation(patch_out[:, j, :], cols(2 + j, 0, C), ACT.Copy).then_inc(patch_ready, 1)

            scaled_q(0)
            act.wait_ge(gq_done, 1)
            act.activation(gq[:], cols(5, 0, C), ACT.Copy, scale=TOK_SCALE).then_inc(gq_ready, 1)
            for t in range(NT):
                evac_kv(t)
                if t == Q1_AT:
                    scaled_q(1)
                if t == WIN + LAG + 1:
                    window_exp(0)
            window_exp(1)
            for j in range(RT):
                rsqrt(lrs[:, j:j + 1], lmv[:, j, 1:2], lo_mv_ready, j + 1, lo_rstd_ready)
                evac_gkv(j)
            for j in range(RT):
                evac_patch(j)
            act.wait_ge(gu_scaled, 1)
            act.activation(w.gu[:], gu_float, ACT.Copy).then_inc(gu_high, 1)
            act.wait_ge(gs_T, 1)
            act.activation(gsT[0:H8, :], gsT[0:H8, :], ACT.Exp).then_inc(ge_ready, 1)

        @block.vector
        def _(dve):
            count = [0]

            def link(ins):
                count[0] += 1
                ins.then_inc(dve_step, 1)
                dve.wait_ge(dve_step, count[0])

            def step(ins):
                count[0] += 1
                ins.then_inc(dve_step, 1)

            def stats(st_, mv_, x, done):
                link(dve.bn_stats(st_, x))
                dve.bn_aggr(mv_, st_).then_inc(done, 1)

            def patch_stats(j):
                for t in range(j * WIN, (j + 1) * WIN):
                    dve.wait_ge(pe_ready, t + 1)
                    step(dve.bn_stats(st[:, t, :], pe[:, t, :]))
                    if t == CLS_AT + 1:
                        dve.wait_ge(first_loaded, 16 * 4)
                        dve.wait_ge(red_tr, 1)
                        gained(rT[:, 0], 7, 0, 0).then_inc(red_T, 1)
                        dve.wait_ge(cls_tr, 1)
                        gained(cT, 6, 0, 4).then_inc(cls_T, 1)
                dve.wait_ge(dve_step, count[0])
                for t in range(j * WIN, (j + 1) * WIN):
                    last = dve.bn_aggr(mv[:, t, :], st[:, t, :])
                    step(last) if t < (j + 1) * WIN - 1 else last.then_inc(mv_ready, 1)

            def patch_hats(j):
                dve.wait_ge(rstd_ready, j + 1)
                dve.wait_ge(mv_ready, j + 1)
                for t in range(j * WIN, (j + 1) * WIN):
                    dve.tensor_scalar(hat[:, t, :], pe[:, t, :], mv[:, t, 0:1], rstd[:, t:t + 1],
                                      ALU.subtract, ALU.mult).then_inc(hat_done, 1)

            def window_mean(j):
                link(dve.tensor_reduce(red[:, j, :], pe[:, j * WIN:(j + 1) * WIN, :].rearrange("p n c -> p c n"),
                                       AX.X, ALU.add))
                link(dve.tensor_scalar(red[:, j, :], red[:, j, :], 1.0 / WIN, None, ALU.mult))
                stats(rst[:, j, :], rmv[:, j, :], red[:, j, :], red_mv_ready)

            def gained(dst, bank, c0, gb):
                for c in range(CK):
                    ins = dve.tensor_scalar(dst[:, c, :], cols(bank, c0 + c * P, P), gains[:, gb, c:c + 1],
                                            gains[:, gb + 1, c:c + 1], ALU.mult, ALU.add)
                    if c < CK - 1:
                        step(ins)
                return ins

            def kvT_tile(t):
                dve.wait_ge(tr_done, t + 1)
                if t >= 4:
                    dve.wait_ge(kv_done, t - 3)
                gained(kvT[:, t % 4], 4 + t % 2, 0, 2).then_inc(kvT_ready, 1)

            patch_stats(0)
            window_mean(0)
            dve.wait_ge(cls_loaded, 16)
            stats(cst[:], cmv[:], cls_in[:], cls_mv_ready)
            patch_hats(0)
            dve.wait_ge(red_rstd_ready, 1)
            dve.wait_ge(red_mv_ready, 1)
            dve.tensor_scalar(rhat[:, 0, :], red[:, 0, :], rmv[:, 0, 0:1], rrs[:, 0:1], ALU.subtract, ALU.mult
                              ).then_inc(red_hat_ready, 1)
            dve.wait_ge(cls_rstd_ready, 1)
            dve.wait_ge(cls_mv_ready, 1)
            dve.tensor_scalar(chat[:], cls_in[:], cmv[:, 0:1], crs[:, 0:1], ALU.subtract, ALU.mult
                              ).then_inc(cls_hat_ready, 1)
            patch_stats(1)
            window_mean(1)
            def scores(t):
                dve.wait_ge(qk_prod, t + 1)
                step(dve.tensor_reduce(s[:, t // WIN, t % WIN, :], hat[:, t, :].rearrange("p (h d) -> p h d", d=DH),
                                       AX.X, ALU.add))

            def less_max(j):
                dve.wait_ge(dve_step, count[0])
                link(dve.tensor_reduce(smax[:, j, :], s[:, j].rearrange("p n h -> p h n"), AX.X, ALU.max))
                dve.tensor_tensor(s[:, j], s[:, j], smax[:, j:j + 1, :].to_broadcast([P, WIN, H8]), ALU.subtract
                                  ).then_inc(s_ready, 1)

            def probabilities(j):
                dve.wait_ge(e_ready, j + 1)
                link(dve.tensor_reduce(den[:, j, :], s[:, j].rearrange("p n h -> p h n"), AX.X, ALU.add))
                link(dve.reciprocal(den[:, j, :], den[:, j, :]))
                dve.tensor_tensor(s[:, j], s[:, j], den[:, j:j + 1, :].to_broadcast([P, WIN, H8]), ALU.mult
                                  ).then_inc(p_ready, 1)

            def aggregate(j):
                dve.wait_ge(pv_prod, j + 1)
                dve.tensor_reduce(agg[:, j, :], hat[:, j * WIN:(j + 1) * WIN, :].rearrange("p n c -> p c n"),
                                  AX.X, ALU.add).then_inc(agg_ready, 1)

            def agg_turned(j):
                dve.wait_ge(agg_tr, j + 1)
                dve.tensor_copy(aggT[:, j].rearrange("p c n -> p (c n)"), cols(4 + j, 0, C)).then_inc(agg_T, 1)

            def local_out(j):
                dve.wait_ge(proj_done, j + 1)
                dve.tensor_tensor(lo[:, j, :], cols(j, 0, C), red[:, j, :], ALU.add).then_inc(lo_ready, 1)
                dve.wait_ge(lo_ready, j + 1)
                stats(lst[:, j, :], lmv[:, j, :], lo[:, j, :], lo_mv_ready)

            def local_hat(j):
                dve.wait_ge(lo_rstd_ready, j + 1)
                dve.wait_ge(lo_mv_ready, j + 1)
                dve.tensor_scalar(lhat[:, j, :], lo[:, j, :], lmv[:, j, 0:1], lrs[:, j:j + 1], ALU.subtract, ALU.mult
                                  ).then_inc(lo_hat_ready, 1)

            def local_turned(j):
                dve.wait_ge(lh_tr, j + 1)
                gained(lhT[:, j], 6 + j, 0, 6).then_inc(lh_T, 1)
                dve.wait_ge(lo_tr, j + 1)
                dve.tensor_copy(loT[:, j].rearrange("p c n -> p (c n)"), cols(4 + j, 0, C)).then_inc(lo_T, 1)

            for t in range(NT):
                kvT_tile(t)
                if t == 1:
                    dve.wait_ge(red_rstd_ready, 2)
                    dve.wait_ge(red_mv_ready, 2)
                    dve.tensor_scalar(rhat[:, 1, :], red[:, 1, :], rmv[:, 1, 0:1], rrs[:, 1:2], ALU.subtract, ALU.mult
                                      ).then_inc(red_hat_ready, 1)
                if t == 3:
                    patch_hats(1)
                if t == Q1_AT:
                    dve.wait_ge(red_tr, 2)
                    gained(rT[:, 1], 2, 0, 0).then_inc(red_T, 1)
                if t >= LAG:
                    scores(t - LAG)
                if t == WIN + LAG:
                    less_max(0)
                if t == WIN + LAG + 1:
                    probabilities(0)
            for t in range(NT - LAG, NT):
                scores(t)
            less_max(1)
            aggregate(0)
            probabilities(1)
            pv_product(dve, 1, POOL_PV, WIN).then_inc(dve_pv, 1)
            agg_turned(0)
            dve.wait_ge(dve_pv, 1)
            aggregate(1)
            local_out(0)
            agg_turned(1)
            local_hat(0)
            local_out(1)
            local_turned(0)
            local_hat(1)
            local_turned(1)
            dve.wait_ge(main_loaded, 16 * 11)
            dve.tensor_scalar(gu_float, gu_int, SCALE_Q, None, ALU.mult).then_inc(gu_scaled, 1)
            dve.tensor_scalar(w.d[:], d_int, SCALE_Q, None, ALU.mult).then_inc(d_scaled, 1)
            for j in range(RT):
                dve.wait_ge(gk_prod, j + 1)
                dve.tensor_reduce(gs[:, j, :], gprod[:, j, :].rearrange("p (h d) -> p h d", d=DH), AX.X, ALU.add
                                  ).then_inc(gs_ready, 1)
            dve.wait_ge(gs_tr, 1)
            scores = cols(6, 0, RT * P)[0:H8]
            by_sample = scores.rearrange("p (w b) -> p b w", b=B)
            link(dve.tensor_reduce(gm[0:H8, :], by_sample, AX.X, ALU.max))
            dve.tensor_tensor(gsT[0:H8, :].rearrange("p (w b) -> p w b", b=B),
                              scores.rearrange("p (w b) -> p w b", b=B),
                              gm[0:H8, :].unsqueeze(1).to_broadcast([H8, NW, B]), ALU.subtract).then_inc(gs_T, 1)
            dve.wait_ge(ge_ready, 1)
            link(dve.tensor_reduce(gd[0:H8, :], gsT[0:H8, :].rearrange("p (w b) -> p b w", b=B), AX.X, ALU.add))
            link(dve.reciprocal(gd[0:H8, :], gd[0:H8, :]))
            dve.tensor_tensor(gsT[0:H8, :].rearrange("p (w b) -> p w b", b=B),
                              gsT[0:H8, :].rearrange("p (w b) -> p w b", b=B),
                              gd[0:H8, :].unsqueeze(1).to_broadcast([H8, NW, B]), ALU.mult).then_inc(gp_T, 1)
            dve.wait_ge(gp_tr, 1)
            dve.tensor_copy(gp[:], cols(7, 0, RT * H8).rearrange("p (j h) -> p j h", h=H8)).then_inc(gp_ready, RT)
            dve.wait_ge(ga_done, 1)
            dve.tensor_copy(gaT[:], cols(0, 0, CK * B).rearrange("p (c b) -> p c b", b=B)).then_inc(ga_T, 1)
            dve.wait_ge(cls_done, 1)
            dve.tensor_copy(cls_out[0:B, :], cols(1, 0, C)[0:B]).then_inc(cls_ready, 1)

        @block.tensor
        def _(pe_):
            def conv(t):
                pe_.wait_ge(patches_loaded[sum(t >= t0 for t0 in LOADS) - 1], 32)
                if t >= 4:
                    pe_.wait_ge(pe_ready, t - 3)
                for k in range(KN):
                    kk = KP if k < KN - 1 else KL
                    last = pe_.matmul(cols(t % 4, 0, C), patches[0:kk, k, t * P:(t + 1) * P], conv_w[0:kk, k, :],
                                      start=(k == 0), stop=(k == KN - 1))
                last.then_inc(conv_done, 1)

            def transposes(bank, c0, src, done):
                for c in range(CK):
                    last = pe_.transpose(cols(bank, c0 + c * P, P), src[:, c * P:(c + 1) * P], w.ident[:])
                last.then_inc(done, 1)

            def tr(t):
                pe_.wait_ge(hat_done, t + 1)
                if t >= 2:
                    pe_.wait_ge(kvT_ready, t - 1)
                transposes(4 + t % 2, 0, hat[:, t, :], tr_done)

            def product(out, lhsT, rhs, done, bias=None, m=P):
                extra = [] if bias is None else bias
                for c in range(CK):
                    last = pe_.matmul(out, lhsT[:, c, :], rhs[:, c, :], start=(c == 0),
                                      stop=(c == CK - 1 and not extra))
                for n, r in enumerate(extra):
                    last = pe_.matmul(out, ones[0:1, 0:m], rows[0:1, r, :], start=False, stop=(n == len(extra) - 1))
                last.then_inc(done, 1)

            def kv_tile(t):
                pe_.wait_ge(kvT_ready, t + 1)
                if t >= 2:
                    pe_.wait_ge(kv_ready, t - 1)
                product(cols(6 + t % 2, 0, 2 * C), kvT[:, t % 4], wkv, kv_done)

            pe_.wait_ge(conv_loaded, 32)
            for t in range(NT):
                conv(t)
                if t == CLS_AT:
                    pe_.wait_ge(first_loaded, 16 * 4)
                    pe_.wait_ge(red_hat_ready, 1)
                    transposes(7, 0, rhat[:, 0, :], red_tr)
                    pe_.wait_ge(cls_hat_ready, 1)
                    transposes(6, 0, chat[:], cls_tr)
            pe_.wait_ge(consts, 1)
            pe_.wait_ge(red_T, 1)
            product(cols(7, 0, C), rT[:, 0], wq, q_done)
            pe_.wait_ge(cls_T, 1)
            product(cols(5, 0, C), cT, gwq, gq_done)
            tr(0)
            pe_.wait_ge(weights_loaded, 16 * 7)
            for t in range(NT):
                if t + 1 < NT:
                    if t == 0:
                        pe_.wait_ge(gq_ready, 1)
                    tr(t + 1)
                if t == 1:
                    pe_.wait_ge(q_ready, 1)
                kv_tile(t)
                if t == Q1_AT - 1:
                    pe_.wait_ge(red_hat_ready, 2)
                    pe_.wait_ge(pe_ready, NT)
                    transposes(2, 0, rhat[:, 1, :], red_tr)
                if t == Q1_AT:
                    pe_.wait_ge(red_T, 2)
                    product(cols(1, 0, C), rT[:, 1], wq, q_done)

            def agg_turn(j):
                pe_.wait_ge(agg_ready, j + 1)
                pe_.wait_ge(kvT_ready, NT)
                transposes(4 + j, 0, agg[:, j, :], agg_tr)

            def local_proj(j):
                pe_.wait_ge(agg_T, j + 1)
                pe_.wait_ge(q_ready, RT)
                product(cols(j, 0, C), aggT[:, j], wproj, proj_done, bias=[0])

            def local_turn(j):
                pe_.wait_ge(kv_ready, NT)
                pe_.wait_ge(lo_hat_ready, j + 1)
                transposes(6 + j, 0, lhat[:, j, :], lh_tr)
                transposes(4 + j, 0, lo[:, j, :], lo_tr)

            def global_kv(j):
                pe_.wait_ge(lh_T, j + 1)
                pe_.wait_ge(lo_T, j + 1)
                product(cols(4 + j, 0, 2 * C), lhT[:, j], gwkv, gkv_done)

            def patch_product(j):
                product(cols(2 + j, 0, C), loT[:, j], mod, patch_done, bias=[1])

            agg_turn(0)
            local_proj(0)
            agg_turn(1)
            local_proj(1)
            local_turn(0)
            global_kv(0)
            local_turn(1)
            global_kv(1)
            for j in range(RT):
                patch_product(j)
            for j in range(RT):
                pe_.wait_ge(gs_ready, j + 1)
                last = pe_.transpose(cols(6, j * P, P)[0:H8], gs[:, j, :], w.ident[:])
            last.then_inc(gs_tr, 1)
            pe_.wait_ge(gp_T, 1)
            for j in range(RT):
                last = pe_.transpose(cols(7, j * H8, H8), gsT[0:H8, j * P:(j + 1) * P], w.ident[0:H8, 0:H8])
            last.then_inc(gp_tr, 1)
            pe_.wait_ge(lo_ready, RT)
            pe_.wait_ge(gv_prod, RT)
            for c in range(CK):
                for j in range(RT):
                    last = pe_.matmul(cols(0, c * B, B), gprod[:, j, c * P:(c + 1) * P], pick[:],
                                      start=(j == 0), stop=(j == RT - 1))
            last.then_inc(ga_done, 1)
            pe_.wait_ge(ga_T, 1)
            product(cols(1, 0, C)[0:B], gaT, gproj, cls_done, bias=[2, 3], m=B)


def transformer(nc, a, w, ps, h_all, out):
    with ExitStack() as stack:
        mem = Names(nc, stack)
        sb, sem = mem.sb, mem.sem
        h_in = sb("h_in", NR, C)
        h_bias = sb("h_bias", NR, C)
        h2 = sb("h2", NR, C)
        x1, x2 = h_in, h_in
        x1T = sb("x1T", CK, TG)
        x2T, x2T_lo = sb("x2T", CK, TG, dt=F32R), sb("x2T_lo", CK, TG, dt=F32R)
        stats = sb("stats", NR, 6)
        mv1, mv2 = sb("mv1", NR, 2), sb("mv2", NR, 2)
        rstd1, rstd2 = sb("rstd1", NR), sb("rstd2", NR)
        qT, qT_lo = sb("qT", CK, 2, TG, dt=F32R), sb("qT_lo", CK, 2, TG, dt=F32R)
        kT, kT_lo = sb("kT", CK, TG, dt=F32R), sb("kT_lo", CK, TG, dt=F32R)
        raw = sb("qk_raw", 3, HALF)
        sq = sb("sq", 2, HALF)
        inv = sb("inv_norm", 2, HALF)
        vw_all = sb("v_weighted", G, VW)
        vw = vw_all[:, :, 0:NH * VD].rearrange("p s (h d) -> p s h d", d=VD)
        outT = sb("outT", 2, NH * S // 4)
        sc = sb("scores", G, SC)
        lnp = sb("ln_one_plus_cos", 2, SC)
        mass = sb("key_mass", 2, 2 * NH)
        osum = sb("o_sum", 2, NH)
        o = sb("o", 2, C)
        oT = sb("oT", CK, TG)
        hid = sb("hidden", HK, TG)
        sig = sb("sigmoid", 2, HALF)
        act_gate = sig

        h_loaded, hr_loaded = sem("h_loaded"), sem("hr_loaded")
        hb_ready = sem("hb_ready")
        mv1_ready, mv2_ready = sem("mv1_ready"), sem("mv2_ready")
        rstd1_ready, rstd2_ready = sem("rstd1_ready"), sem("rstd2_ready")
        x1_ready, x2_ready = sem("x1_ready"), sem("x2_ready")
        x1_tr, x2_tr = sem("x1_tr"), sem("x2_tr")
        x1T_ready, x2T_ready = sem("x1T_ready"), sem("x2T_ready")
        x2_high = sem("x2_high")
        v_done, v_ready = sem("v_done"), sem("v_ready")
        qk_done, sq_ready, raw_ready = sem("qk_done"), sem("sq_ready"), sem("raw_ready")
        n2_done, n2_ln, inv_ready = sem("n2_done"), sem("n2_ln"), sem("inv_ready")
        unit_ready, hi_ready = sem("unit_ready"), sem("hi_ready")
        q_lo_ready, k_lo_ready = sem("q_lo_ready"), sem("k_lo_ready")
        s_done, clip_ready = sem("s_done"), sem("clip_ready")
        ln_ready, x_ready = sem("ln_ready"), sem("x_ready")
        tanh_ready, atan_ready = sem("tanh_ready"), sem("atan_ready")
        ln_g, a_ready = sem("ln_g"), sem("a_ready")
        mass_ready, rm_ready, vw_ready = sem("mass_ready"), sem("rm_ready"), sem("vw_ready")
        pv_done, outT_ready, out_tr = sem("pv_done"), sem("outT_ready"), sem("out_tr")
        osum_ready, orec_ready, o_ready = sem("osum_ready"), sem("orec_ready"), sem("o_ready")
        pad_ready = sem("pad_ready")
        o_tr = sem("o_tr")
        oT_ready = sem("oT_ready")
        op_done, h2_ready = sem("op_done"), sem("h2_ready")
        gu_done, sig_ready = sem("gu_done"), sem("sig_ready")
        gate_ready, hid_ready = sem("gate_ready"), sem("hid_ready")
        down_done, y_ready = sem("down_done"), sem("y_ready")
        stored = sem("stored")
        rstd_ln = sem("rstd_ln")
        block = stack.enter_context(nc.Block())

        HV = G // 2
        UNITS = 2 * HK

        STEPS_AT = [[], [("logs", 0)], [("logs", 1)],
                    [("logs", 2), ("set", SIG_ATAN), ("tanh", 0)],
                    [("atan", 0), ("set", LN_EXP), ("logs", 3)],
                    [("ln", 0), ("logs", 4)], [("exp", 0), ("logs", 5)], [("logs", 6)]]
        ANGLES_AT = {-1: (1, "tanh"), 1: (2, "tanh"), 3: (3, "tanh"), 5: (1, "atan"), 7: (2, "atan"), 9: (3, "atan")}
        POWERS = [(1, "ln"), (1, "exp"), (2, "ln"), (3, "ln"), (2, "exp"), (3, "exp")]
        MASS_AT = {0: 1, 1: 2, 3: 3}
        X2_AT = 5
        OUT_ON_DVE = {0, 1}
        V_AT = {4: 0, 5: 1, 6: 2, 7: 3}
        DOWN_AT = {-1: (0,), 0: (1,), 1: (2,), 2: (3,), 3: (4,), 4: (5,)}
        JOBS = []
        for s in range(-1, G + 1):
            if 0 <= s < G:
                JOBS.append(("pv", s, 0, outT_ready, G, s))
                JOBS.append(("out", s, 0, o_ready, G, s))
            if s > 0:
                JOBS.append(("oT", s - 1, 0, oT_ready, G, s - 1))
            JOBS += [("down", t, -1, y_ready, NR, t) for t in DOWN_AT.get(s, ())]
            if s in V_AT:
                JOBS.append(("v", V_AT[s], 1, v_ready, 4, V_AT[s]))
        JOBS += [("x1T", n, 2, x1T_ready, 3, n) for n in range(3)]
        JOBS += [("qk", (kind, u), 2, raw_ready if kind == "proj" else n2_ln, 8, u) for kind, u in QK_ORDER]
        JOBS += [("x2T", n, 0, x2T_ready, 3, n) for n in range(3)]
        JOBS += [("gu", (kind, u), 0, gate_ready if kind == "gate" else hid_ready, UNITS, u)
                 for u in range(UNITS) for kind in ("gate", "up")]
        assert len(JOBS) % 4 == 0
        NUMBER = {(j[0], j[1]): n for n, j in enumerate(JOBS)}

        def claim(eng, it, before, now, stage, which):
            n = NUMBER[stage, which]
            bank, back, offs = 4 + n % 4, 0, now
            n -= 4
            while True:
                if n < 0:
                    if back:
                        return bank
                    n, back, offs = n + len(JOBS), 1, before
                _, _, off, read, per, i = JOBS[n]
                if off in offs:
                    eng.wait_ge(read, (it + off - back) * per + i + 1)
                    return bank
                n -= 4

        def bank(b, n, rows=P, c=0):
            return ps[0:rows, b, c:c + n]

        def iterate(eng, body):
            every = {-1, 0, 1, 2}
            body(-2, set(), {2})
            body(-1, {2}, {1, 2})
            body(0, {1, 2}, {0, 1, 2})
            with eng.Fori(1, NG - 2) as it:
                body(it, every, every)
            body(NG - 2, every, {-1, 0, 1})
            body(NG - 1, {-1, 0, 1}, {-1, 0})
            body(NG, {-1, 0}, {-1})

        def unit_place(u, q, k, e=0):
            f, hf = UNIT_OF[u]
            cols = slice(hf * HALF, (hf + 1) * HALF)
            return q[:, f, e, cols] if f < CK else k[:, f - CK, cols]

        @block.sync
        def _(sync):
            rows_in = h_all.rearrange("b s c -> (b s) c")
            rows_out = out.rearrange("b s c -> (b s) c")

            def part(rows, g):
                return rows[g * TG:(g + 1) * TG] if isinstance(g, int) else rows[bass.ds(g * TG, TG)]

            def load(dst, g, done):
                rows = part(rows_in, g)
                sync.dma_start(dst[:, 0:NR - 1, :],
                               rows[0:P * (NR - 1)].rearrange("(t p) c -> p t c", p=P)).then_inc(done, 16)
                sync.dma_start(dst[:, NR - 1, :], rows[TG - P:TG]).then_inc(done, 16)

            def body(it, before, now):
                if 2 in now:
                    if 2 in before:
                        sync.wait_ge(x1_tr, (it + 2) * 3)
                    if 0 in before:
                        sync.wait_ge(x2_tr, (it - 1) * 3 + 3)
                    load(h_in, it + 2, h_loaded)
                if -1 in now:
                    sync.wait_ge(y_ready, it * NR)
                    dst = part(rows_out, it - 1)
                    sync.dma_start(dst[0:P * (NR - 1)].rearrange("(t p) c -> p t c", p=P), h2[:, 0:NR - 1, :]
                                   ).then_inc(stored, 16)
                    rest = TG - P * (NR - 1)
                    sync.dma_start(dst[P * (NR - 1):TG], h2[P - rest:P, NR - 1, :]).then_inc(stored, 16)
                if 1 in now:
                    if 0 in now:
                        sync.wait_ge(h2_ready, (it + 1) * NR)
                    load(h_bias, it + 1, hr_loaded)

            iterate(sync, body)
            sync.wait_ge(stored, 32 * NG)

        @block.gpsimd
        def _(pool):
            pool.memset(vw_all[:, :, NH * VD:VW], 0.0).then_inc(pad_ready, 1)

            def scale_values(it, k):
                pool.wait_ge(rm_ready, it * HV + k + 1)
                for s in (2 * k, 2 * k + 1):
                    last = pool.tensor_tensor(vw[0:S, s, :, 0:HD], vw[0:S, s, :, 0:HD],
                                              vw[0:S, s, :, HD:VD].to_broadcast([S, NH, HD]), ALU.mult)
                last.then_inc(vw_ready, 1)

            def difference(g, s):
                pool.wait_ge(ln_ready, g * G + s + 1)
                pool.tensor_tensor(sc[0:S, s, :], lnp[0:S, s % 2, :], sc[0:S, s, :], ALU.subtract).then_inc(x_ready, 1)

            def add_bias(it):
                pool.wait_ge(hr_loaded, 32 * (it + 1))
                pool.tensor_tensor(h_bias[:], h_bias[:], w.out_bias[:].unsqueeze(1).to_broadcast([P, NR, C]), ALU.add
                                   ).then_inc(hb_ready, 1)

            def body(it, before, now):
                for s in range(G):
                    if 0 in now and s in MASS_AT:
                        scale_values(it, MASS_AT[s])
                    if 0 in now and s == 4:
                        add_bias(it)
                    if 1 in now and s:
                        difference(it + 1, s - 1)
                if 1 in now:
                    difference(it + 1, G - 1)
                for u in range(4, 8 if 2 in now else 0):
                    pool.wait_ge(hi_ready, (it + 2) * 8 + u + 1)
                    pool.tensor_tensor(unit_place(u, qT_lo, kT_lo), raw[:, u % 3, :], unit_place(u, qT, kT),
                                       ALU.subtract).then_inc(k_lo_ready, 1)
                if 1 in now:
                    scale_values(it + 1, 0)

            iterate(pool, body)

        @block.scalar
        def _(act):
            def rstd_order(it, which):
                if isinstance(it, int) and it < 0:
                    return it + 3
                if isinstance(it, int) and it > NG - 3:
                    return NG + it + 1
                return 2 * it + 2 + which

            def rstd(dst, mv, got, g, done, order):
                act.wait_ge(got, g + 1)
                act.activation(dst[:], mv[:, :, 1], ACT.Ln, bias=LN_EPS).then_inc(rstd_ln, 1)
                act.wait_ge(rstd_ln, order)
                act.activation(dst[:], dst[:], ACT.Exp, scale=-0.5).then_inc(done, 1)

            def logs(it, s):
                act.wait_ge(clip_ready, it * 2 * G + 2 * s + 2)
                if s >= 2:
                    act.wait_ge(x_ready, it * G + s - 1)
                act.activation(lnp[0:S, s % 2, :], sc[0:S, s, :], ACT.Ln, bias=1.0)
                act.activation(sc[0:S, s, :], sc[0:S, s, :], ACT.Ln, bias=1.0, scale=-1.0).then_inc(ln_ready, 1)

            def qk_raw(g, u):
                f, hf = UNIT_OF[u]
                b = 4 + NUMBER["qk", ("proj", u)] % 4
                act.wait_ge(qk_done, g * 8 + u + 1)
                if u >= 2:
                    act.wait_ge(n2_done, g * 8 + u - 1)
                act.activation(sq[:, u % 2, :], bank(b, HALF), ACT.Square, bias=w.q_bias[:, f:f + 1]
                               ).then_inc(sq_ready, 1)
                if u >= 3:
                    act.wait_ge(q_lo_ready if u < 7 else k_lo_ready, g * 4 + (u - 3) % 4 + 1)
                act.activation(raw[:, u % 3, :], bank(b, HALF), ACT.Identity, bias=w.q_bias[:, f:f + 1]
                               ).then_inc(raw_ready, 1)

            def qk_norm(g, u):
                b = 4 + NUMBER["qk", ("norm", u)] % 4
                act.wait_ge(n2_done, g * 8 + u + 1)
                if u >= 2:
                    act.wait_ge(unit_ready, g * 8 + u - 1)
                act.activation(inv[:, u % 2, :], bank(b, HALF), ACT.Ln, bias=N2_BIAS, scale=N2_SCALE
                               ).then_inc(n2_ln, 1)
                act.wait_ge(n2_ln, g * 8 + u + 1)
                act.activation(inv[:, u % 2, :], inv[:, u % 2, :], ACT.Exp, bias=N2_SHIFT, scale=-0.5
                               ).then_inc(inv_ready, 1)

            def two(k):
                return sc[0:S, 2 * k:2 * k + 2, :]

            def angle(g, k, step):
                if step == "tanh":
                    act.wait_ge(x_ready, g * G + 2 * k + 2)
                    act.activation(two(k), two(k), ACT.Tanh, scale=0.25).then_inc(tanh_ready, 1)
                else:
                    act.wait_ge(tanh_ready, g * HV + k + 1)
                    act.activation(two(k), two(k), ACT.Arctan).then_inc(atan_ready, 1)

            def sigmoid(g, u):
                b = 4 + NUMBER["gu", ("gate", u)] % 4
                act.wait_ge(gu_done, g * UNITS + u + 1)
                if u >= 2:
                    act.wait_ge(gate_ready, g * UNITS + u - 1)
                act.activation(sig[:, u % 2, :], bank(b, HALF), ACT.Sigmoid).then_inc(sig_ready, 1)

            def power(g, k, step):
                if step == "ln":
                    act.wait_ge(atan_ready, g * HV + k + 1)
                    act.activation(two(k), two(k), ACT.Ln, bias=1.0 + HALF_PI, scale=-2.0).then_inc(ln_g, 1)
                else:
                    act.wait_ge(ln_g, g * HV + k + 1)
                    act.activation(two(k), two(k), ACT.Exp, scale=POWER).then_inc(a_ready, 1)

            def out_turned(it, s):
                act.wait_ge(o_tr, it * G + s + 1)
                act.activation(oT[:, :, s * S:(s + 1) * S],
                               bank(4 + NUMBER["oT", s] % 4, CK * S).rearrange("p (c n) -> p c n", c=CK), ACT.Copy
                               ).then_inc(oT_ready, 1)

            def weighted_out(it, s):
                act.wait_ge(pv_done, it * G + s + 1)
                act.activation(outT[:, s % 2, :], bank(4 + NUMBER["pv", s] % 4, NH * S // 4), ACT.Copy
                               ).then_inc(outT_ready, 1)

            def body(it, before, now):
                if now == {2}:
                    act.preload_act_table_set(LN_EXP)
                for s in range(G):
                    if 0 in now and s not in OUT_ON_DVE:
                        weighted_out(it, s)
                    if s == 2 and 2 in now:
                        rstd(rstd1, mv1, mv1_ready, it + 2, rstd1_ready, rstd_order(it, 1))
                    for step, n in STEPS_AT[s] if 1 in now else ():
                        if step == "logs":
                            logs(it + 1, n)
                        elif step == "set":
                            act.preload_act_table_set(n)
                        elif step in ("tanh", "atan"):
                            angle(it + 1, n, step)
                        else:
                            power(it + 1, n, step)
                    if 0 in now and s:
                        out_turned(it, s - 1)
                if 1 in now:
                    logs(it + 1, G - 1)
                if 0 in now:
                    out_turned(it, G - 1)
                    if 2 not in now:
                        rstd(rstd2, mv2, mv2_ready, it, rstd2_ready, rstd_order(it, 2))
                for u in range(8 if 2 in now else 0):
                    qk_raw(it + 2, u)
                    if u:
                        qk_norm(it + 2, u - 1)
                    if u == X2_AT - 1 and 0 in now:
                        rstd(rstd2, mv2, mv2_ready, it, rstd2_ready, rstd_order(it, 2))
                if 2 in now:
                    qk_norm(it + 2, 7)
                if now & {0, 1}:
                    act.preload_act_table_set(SIG_ATAN)
                for u in range(-1, UNITS):
                    if u >= 0 and 0 in now:
                        sigmoid(it, u)
                    if 1 in now and u in ANGLES_AT:
                        angle(it + 1, *ANGLES_AT[u])
                if 1 in now:
                    act.preload_act_table_set(LN_EXP)
                    for k, step in POWERS:
                        power(it + 1, k, step)

            iterate(act, body)

        @block.vector
        def _(dve):
            def moments(h, mv, done):
                for t in range(NR):
                    last = dve.bn_stats(stats[:, t, :], h[:, t, :])
                dve.drain()
                for t in range(NR):
                    last = dve.bn_aggr(mv[:, t, :], stats[:, t, :])
                last.then_inc(done, 1)

            def moments1(g):
                dve.wait_ge(h_loaded, 32 * (g + 1))
                moments(h_in, mv1, mv1_ready)

            def moments2(g):
                dve.wait_ge(h2_ready, NR * (g + 1))
                moments(h2, mv2, mv2_ready)

            def turned2(g):
                rest = TG - 5 * P
                both = slice(0, CK)
                tail = bank(4 + NUMBER["x2T", CK] % 4, 4 * P).rearrange("p (c n) -> p c n", c=CK)
                places = [[(slice(0, 4 * P), bank(4 + NUMBER["x2T", n] % 4, 4 * P), n)] for n in range(CK)]
                places += [[(slice(4 * P, 5 * P), tail[:, :, 0:P], both),
                            (slice(5 * P, TG), tail[:, :, 2 * P - rest:2 * P], both)]]
                for n, parts in enumerate(places):
                    dve.wait_ge(x2_tr, g * 3 + n + 1)
                    for cols, x, c in parts:
                        last = dve.tensor_copy(x2T[:, c, cols], x)
                    last.then_inc(x2_high, 1)
                for n, parts in enumerate(places):
                    dve.wait_ge(x2_high, g * 3 + n + 1)
                    for cols, x, c in parts:
                        last = dve.tensor_tensor(x2T_lo[:, c, cols], x, x2T[:, c, cols], ALU.subtract)
                    last.then_inc(x2T_ready, 1)

            def normalise(x, h, mv, rs, mv_got, rs_got, g, done):
                dve.wait_ge(mv_got, g + 1)
                dve.wait_ge(rs_got, g + 1)
                for t in range(NR):
                    dve.tensor_scalar(x[:, t, :], h[:, t, :], mv[:, t, 0:1], rs[:, t:t + 1],
                                      ALU.subtract, ALU.mult).then_inc(done, 1)

            def turned(xT, stage, tr, ready, g):
                for n in range(3):
                    b = 4 + NUMBER[stage, n] % 4
                    dve.wait_ge(tr, g * 3 + n + 1)
                    if n < CK:
                        dve.tensor_copy(xT[:, n, 0:4 * P], bank(b, 4 * P)).then_inc(ready, 1)
                    else:
                        tail = bank(b, 4 * P).rearrange("p (c n) -> p c n", c=CK)
                        rest = TG - 5 * P
                        dve.tensor_copy(xT[:, :, 4 * P:5 * P], tail[:, :, 0:P])
                        dve.tensor_copy(xT[:, :, 5 * P:TG], tail[:, :, 2 * P - rest:2 * P]).then_inc(ready, 1)

            def values(it, k):
                b = 4 + NUMBER["v", k] % 4
                dve.wait_ge(v_done, it * 4 + k + 1)
                for i in range(2):
                    last = dve.tensor_tensor(vw[0:S, 2 * k + i, :, 0:HD],
                                             bank(b, C, S, i * C).rearrange("p (h d) -> p h d", d=HD),
                                             w.v_bias[0:S].rearrange("p (h d) -> p h d", d=HD), ALU.add)
                last.then_inc(v_ready, 1)

            def clip(g, s, q):
                dve.wait_ge(s_done, g * 2 * G + 2 * s + q + 1)
                dve.tensor_scalar(sc[0:S, s, 4 * PAIR * q:4 * PAIR * (q + 1)].rearrange("p (b n) -> p b n", b=2),
                                  ps[0:S, 2 * q:2 * q + 2, 0:2 * PAIR], -1.0 + COS_EPS, 1.0 - COS_EPS,
                                  ALU.max, ALU.min).then_inc(clip_ready, 1)

            def qk_unit(g, u):
                dve.wait_ge(inv_ready, g * 8 + u + 1)
                dve.wait_ge(raw_ready, g * 8 + u + 1)
                dve.scalar_tensor_tensor(out=raw[:, u % 3, :], in0=inv[:, u % 2, :], scalar=1e12,
                                         in1=raw[:, u % 3, :], op0=ALU.min, op1=ALU.mult).then_inc(unit_ready, 1)

            def qk_high(g, u):
                dve.wait_ge(unit_ready, g * 8 + u + 1)
                if u < 4:
                    for e in range(2):
                        last = dve.tensor_scalar(unit_place(u, qT, kT, e), raw[:, u % 3, :], w.head_row[:, e:e + 1],
                                                 None, ALU.mult)
                else:
                    last = dve.tensor_copy(unit_place(u, qT, kT), raw[:, u % 3, :])
                last.then_inc(hi_ready, 1)

            def q_low(g, u):
                dve.wait_ge(hi_ready, g * 8 + u + 1)
                for e in range(2):
                    last = dve.scalar_tensor_tensor(
                        out=unit_place(u, qT_lo, kT_lo, e), in0=raw[:, u % 3, :], scalar=w.head_row[:, e:e + 1],
                        in1=unit_place(u, qT, kT, e), op0=ALU.mult, op1=ALU.subtract)
                last.then_inc(q_lo_ready, 1)

            def mlp_unit(g, u):
                j, hf = u % HK, u // HK
                dve.wait_ge(sig_ready, g * UNITS + u + 1)
                dve.tensor_tensor(act_gate[:, u % 2, :], bank(4 + NUMBER["gu", ("gate", u)] % 4, HALF),
                                  sig[:, u % 2, :], ALU.mult).then_inc(gate_ready, 1)
                dve.wait_ge(gate_ready, g * UNITS + u + 1)
                dve.tensor_tensor(hid[:, j, hf * HALF:(hf + 1) * HALF],
                                  bank(4 + NUMBER["gu", ("up", u)] % 4, HALF), act_gate[:, u % 2, :], ALU.mult
                                  ).then_inc(hid_ready, 1)

            def result(g, t):
                dve.wait_ge(down_done, g * NR + t + 1)
                dve.tensor_tensor(h2[:, t, :], bank(4 + NUMBER["down", t] % 4, C), h2[:, t, :], ALU.add
                                  ).then_inc(y_ready, 1)

            def key_mass(it, k):
                dve.wait_ge(a_ready, it * HV + k + 1)
                dve.wait_ge(v_ready, it * 4 + k + 1)
                dve.tensor_reduce(mass[0:S, k % 2, :], sc[0:S, 2 * k:2 * k + 2, :].rearrange("p s (h q) -> p (s h) q", q=S),
                                  AX.X, ALU.add).then_inc(mass_ready, 1)
                dve.wait_ge(mass_ready, it * HV + k + 1)
                dve.reciprocal(vw[0:S, 2 * k:2 * k + 2, :, HD], mass[0:S, k % 2, :].rearrange("p (s h) -> p s h", h=NH)
                               ).then_inc(rm_ready, 1)

            def weighted_out(it, s):
                dve.wait_ge(pv_done, it * G + s + 1)
                dve.tensor_copy(outT[:, s % 2, :], bank(4 + NUMBER["pv", s] % 4, NH * S // 4)).then_inc(outT_ready, 1)

            def head_out(it, s):
                pv = bank(4 + NUMBER["out", s] % 4, NH * VS, S).rearrange("p (h d) -> p h d", d=VS)
                dve.wait_ge(out_tr, it * G + s + 1)
                dve.tensor_scalar(osum[0:S, s % 2, :], pv[:, :, HD], 1e-12, None, ALU.max).then_inc(osum_ready, 1)
                dve.wait_ge(osum_ready, it * G + s + 1)
                dve.reciprocal(osum[0:S, s % 2, :], osum[0:S, s % 2, :]).then_inc(orec_ready, 1)
                dve.wait_ge(orec_ready, it * G + s + 1)
                if s >= 2:
                    dve.wait_ge(o_tr, it * G + s - 1)
                dve.tensor_tensor(o[0:S, s % 2, :].rearrange("p (h d) -> p h d", d=HD), pv[:, :, 0:HD],
                                  osum[0:S, s % 2, :].unsqueeze(2).to_broadcast([S, NH, HD]), ALU.mult
                                  ).then_inc(o_ready, 1)

            def residual(it, t, before):
                dve.wait_ge(op_done, it * NR + t + 1)
                if t == 0:
                    dve.wait_ge(hb_ready, it + 1)
                    if 0 in before:
                        dve.wait_ge(stored, 32 * it)
                dve.tensor_tensor(h2[:, t, :], bank(t % 4, C), h_bias[:, t, :], ALU.add).then_inc(h2_ready, 1)

            def body(it, before, now):
                out_, score, proj = 0 in now, 1 in now, 2 in now
                down = -1 in now
                for t in DOWN_AT[-1] if down else ():
                    result(it - 1, t)
                if proj:
                    if not out_:
                        moments1(it + 2)
                for s in range(G):
                    if out_ and s in OUT_ON_DVE:
                        weighted_out(it, s)
                    if score:
                        clip(it + 1, s, 0)
                    if out_:
                        head_out(it, s)
                    if score:
                        clip(it + 1, s, 1)
                    if out_ and s in MASS_AT:
                        key_mass(it, MASS_AT[s])
                    for t in DOWN_AT.get(s, ()) if down else ():
                        result(it - 1, t)
                    if score and s in V_AT:
                        values(it + 1, V_AT[s])
                    if proj and out_ and s == 1:
                        moments1(it + 2)
                    if proj and s == 6:
                        normalise(x1, h_in, mv1, rstd1, mv1_ready, rstd1_ready, it + 2, x1_ready)
                if out_:
                    for t in range(NR):
                        residual(it, t, before)
                if proj:
                    turned(x1T, "x1T", x1_tr, x1T_ready, it + 2)
                if out_:
                    moments2(it)
                    if not proj:
                        normalise(x2, h2, mv2, rstd2, mv2_ready, rstd2_ready, it, x2_ready)
                if proj:
                    for u in range(8):
                        if out_ and u == X2_AT:
                            normalise(x2, h2, mv2, rstd2, mv2_ready, rstd2_ready, it, x2_ready)
                        if out_ and u == 7:
                            turned2(it)
                        qk_unit(it + 2, u)
                        qk_high(it + 2, u)
                        if u < 4:
                            q_low(it + 2, u)
                elif out_:
                    turned2(it)
                if score:
                    key_mass(it + 1, 0)
                if out_:
                    for u in range(UNITS):
                        mlp_unit(it, u)

            iterate(dve, body)

        @block.tensor
        def _(pe):
            def values(it, k, before, now):
                b = claim(pe, it, before, now, "v", k)
                if k == 0:
                    pe.wait_ge(x1T_ready, 3 * (it + 2))
                for i in range(2):
                    c0 = (2 * k + i) * S
                    for c in range(CK):
                        last = pe.matmul(bank(b, C, S, i * C), x1T[:, c, c0:c0 + S], w.v[:, c, :],
                                         start=(c == 0), stop=(c == CK - 1))
                last.then_inc(v_done, 1)

            def scores(it, s, q, before):
                g = it + 1
                if s == 0 and q == 0:
                    pe.wait_ge(hi_ready, 8 * (g + 1))
                    pe.wait_ge(q_lo_ready, 4 * (g + 1))
                    pe.wait_ge(k_lo_ready, 4 * (g + 1))
                    if 0 in before:
                        pe.wait_ge(h2_ready, it * NR)
                if s:
                    pe.wait_ge(clip_ready, g * 2 * G + 2 * (s - 1) + q + 1)
                at = slice(s * S, (s + 1) * S)
                for r in (2 * q, 2 * q + 1):
                    rows = slice(32 * r, 32 * r + 32)
                    for c in range(CK):
                        for n, (k_, q_) in enumerate(((kT, qT), (kT, qT_lo), (kT_lo, qT))):
                            last = pe.matmul(bank(r, PAIR, S, c * PAIR), k_[rows, c, at], q_[rows, c, :, at],
                                             start=(n == 0), stop=(n == 2))
                last.then_inc(s_done, 1)

            def turn(it, x, ready, stage, tr, g, before, now):
                for n in range(3):
                    b = claim(pe, it, before, now, stage, n)
                    if n == 0:
                        pe.wait_ge(ready, g * NR + 4)
                    if n == 2:
                        pe.wait_ge(ready, g * NR + NR)
                    parts = [(t, n) for t in range(4)] if n < CK else [(t, c) for c in range(CK) for t in (4, 5)]
                    for i, (t, c) in enumerate(parts):
                        last = pe.transpose(bank(b, P, P, i * P), x[:, t, c * P:(c + 1) * P], w.ident[:])
                    last.then_inc(tr, 1)

            def qk(it, before, now):
                g = it + 2
                pe.wait_ge(x1T_ready, 3 * g + 2)
                for kind, u in QK_ORDER:
                    b = claim(pe, it, before, now, "qk", (kind, u))
                    f, hf = UNIT_OF[u]
                    if (kind, u) == ("proj", 1):
                        pe.wait_ge(x1T_ready, 3 * (g + 1))
                    if kind == "proj":
                        for c in range(CK):
                            last = pe.matmul(bank(b, HALF), w.qk[:, c, f * P:(f + 1) * P],
                                             x1T[:, c, hf * HALF:(hf + 1) * HALF], start=(c == 0), stop=(c == CK - 1))
                        last.then_inc(qk_done, 1)
                    else:
                        pe.wait_ge(sq_ready, g * 8 + u + 1)
                        pe.matmul(bank(b, HALF), w.head_sum[:], sq[:, u % 2, :], start=True, stop=True
                                  ).then_inc(n2_done, 1)

            def gate_up(it, u, before, now):
                j, hf = u % HK, u // HK
                if j == 0:
                    pe.wait_ge(x2_high, 3 * it + 2 + hf)
                for i, kind in enumerate(("gate", "up")):
                    b = claim(pe, it, before, now, "gu", (kind, u))
                    feats, toks = slice(i * HID + j * P, i * HID + (j + 1) * P), slice(hf * HALF, (hf + 1) * HALF)
                    terms = [(w_, x_, c) for w_, x_ in ((w.gu, x2T), (w.gu_lo, x2T), (w.gu, x2T_lo)) for c in range(CK)]
                    for n, (w_, x_, c) in enumerate(terms):
                        if j == 0 and n == 2 * CK and i == 0:
                            pe.wait_ge(x2T_ready, 3 * it + 2 + hf)
                        last = pe.matmul(bank(b, HALF), w_[:, c, feats], x_[:, c, toks],
                                         start=(n == 0), stop=(n == len(terms) - 1))
                last.then_inc(gu_done, 1)

            def down(it, t, before, now):
                b = claim(pe, it, before, now, "down", t)
                if t == 0:
                    pe.wait_ge(hid_ready, UNITS * (it - 1) + HK)
                elif t == HALF // P:
                    pe.wait_ge(hid_ready, UNITS * it)
                for k in range(HK):
                    last = pe.matmul(bank(b, C), hid[:, k, ROWS[t]:ROWS[t] + P], w.d[:, k, :],
                                     start=(k == 0), stop=(k == HK - 1))
                last.then_inc(down_done, 1)

            def weighted(it, s, before, now):
                b = claim(pe, it, before, now, "pv", s)
                if s == 0 and isinstance(it, int) and it == 0:
                    pe.wait_ge(pad_ready, 1)
                if s % 2 == 0:
                    pe.wait_ge(vw_ready, it * HV + s // 2 + 1)
                for h in range(NH):
                    i = h % 4
                    last = pe.matmul(ps[VS * i:VS * (i + 1), b, (h // 4) * S:(h // 4 + 1) * S],
                                     vw_all[0:S, s, h * VD:h * VD + VS], sc[0:S, s, h * S:(h + 1) * S],
                                     start=True, stop=True)
                last.then_inc(pv_done, 1)

            def turn_back(it, s, before, now):
                b = claim(pe, it, before, now, "out", s)
                pe.wait_ge(outT_ready, it * G + s + 1)
                for n in range(NH // 4):
                    last = pe.transpose(bank(b, P, S, n * P), outT[:, s % 2, n * S:(n + 1) * S], w.ident[:])
                last.then_inc(out_tr, 1)

            def turn_o(it, s, before, now):
                b = claim(pe, it, before, now, "oT", s)
                pe.wait_ge(o_ready, it * G + s + 1)
                for c in range(CK):
                    last = pe.transpose(bank(b, S, P, c * S), o[0:S, s % 2, c * P:(c + 1) * P],
                                        w.ident[0:S, 0:S])
                last.then_inc(o_tr, 1)

            def project(it, t, now):
                pe.wait_ge(oT_ready, it * G + -(-(ROWS[t] + P) // S))
                if t >= 4:
                    pe.wait_ge(h2_ready, it * NR + t - 3)
                elif t == 0 and 1 in now:
                    pe.wait_ge(clip_ready, (it + 2) * 2 * G)
                for c in range(CK):
                    last = pe.matmul(bank(t % 4, C), oT[:, c, ROWS[t]:ROWS[t] + P], w.out[:, c, :],
                                     start=(c == 0), stop=(c == CK - 1))
                last.then_inc(op_done, 1)

            def body(it, before, now):
                for s in range(-1, G):
                    if s >= 0 and 0 in now:
                        weighted(it, s, before, now)
                    if s >= 0 and 1 in now:
                        scores(it, s, 0, before)
                    if s >= 0 and 0 in now:
                        turn_back(it, s, before, now)
                        if s:
                            turn_o(it, s - 1, before, now)
                    if s >= 0 and 1 in now:
                        scores(it, s, 1, before)
                    for t in DOWN_AT.get(s, ()) if -1 in now else ():
                        down(it, t, before, now)
                    if s in V_AT and 1 in now:
                        values(it, V_AT[s], before, now)
                if 0 in now:
                    turn_o(it, G - 1, before, now)
                    for t in range(NR):
                        project(it, t, now)
                if 2 in now:
                    turn(it, x1, x1_ready, "x1T", x1_tr, it + 2, before, now)
                    qk(it, before, now)
                if 0 in now:
                    turn(it, x2, x2_ready, "x2T", x2_tr, it, before, now)
                    for u in range(UNITS):
                        gate_up(it, u, before, now)

            iterate(pe, body)


UNIT_OF = [(f, hf) for f in range(2 * CK) for hf in range(2)]
QK_ORDER = [("proj", 0)] + [x for u in range(1, 8) for x in (("proj", u), ("norm", u - 1))] + [("norm", 7)]


def program(nc, a, out):
    h_all = nc.dram_tensor("tokens", [B, S, C], F32).ap()
    with ExitStack() as stack:
        mem = Names(nc, stack)
        w = Weights(mem)
        ps = stack.enter_context(nc.psum_tensor("ps", [P, 8, 512], F32))
        tokenizer(nc, a, w, ps, h_all)
        transformer(nc, a, w, ps, h_all, out)


def kernel(**inputs):
    import concourse.bacc as bacc
    import numpy as np
    from concourse.bass_utils import run_bass_kernel_spmd

    x = {n.removeprefix("L0_").removeprefix("tok_").removeprefix("attn_").removeprefix("ffn_"): np.asarray(v)
         for n, v in inputs.items()}
    order = [c * 8 + 2 * r + e for r in range(4) for c in range(CK) for e in range(2)]
    feats = np.array([h * HD + d for h in order for d in range(HD)])
    px = x["x"].reshape(B, 3, 2, 3, 14, 2, 3, 14).transpose(1, 4, 7, 2, 3, 6, 5, 0)
    data = {
        "patches": px.reshape(PATCH, NT * P),
        "conv_w": x["conv_w"].reshape(C, PATCH).T,
        "txt": x["txt"],
        "w_qk": x["w_qkv"][0:2 * C].T, "b_qk": x["b_qkv"][0:2 * C].reshape(2 * CK, P).T,
        "w_v": x["w_qkv"][2 * C:][feats].T, "b_v": x["b_qkv"][2 * C:][feats],
        "w_out": x["w_out"][:, feats].T, "b_out": x["b_out"],
        "w_gate": x["w_gate"].T, "w_up": x["w_up"].T, "w_down": x["w_down"].T,
        "ident": np.eye(P, dtype=np.float32),
        "pick": np.tile(np.eye(B, dtype=np.float32), (2, 1)),
        "head_sum": np.kron(np.eye(P // HD, dtype=np.float32), np.ones((HD, HD), np.float32)),
        "head_row": np.repeat(np.tile(np.eye(2, dtype=np.float32), (P // HD // 2, 1)), HD, axis=0),
    }
    gains = [x[f"{part}_ln_{side}_{kind}"] for part in ("la", "ga") for side in ("q", "kv") for kind in ("g", "b")]
    data["gains"] = np.stack(gains).reshape(8, CK, P).transpose(2, 0, 1)
    data["rows"] = np.stack([x["la_proj_b"], x["mod_b"], x["ga_proj_b"], x["class_emb"]])[None]
    for n in ("class_emb", "la_wq", "la_wkv", "la_proj_w", "ga_wq", "ga_wkv", "ga_proj_w", "mod_w"):
        data[n] = x[n]
    nc = bacc.Bacc("TRN2", target_bir_lowering=False, num_devices=1)
    arrays, aps = {}, {}
    for n, v in data.items():
        v = np.ascontiguousarray(v)
        arrays["in_" + n] = v
        aps[n] = nc.dram_tensor("in_" + n, v.shape, mybir.dt.from_np(v.dtype), kind="ExternalInput").ap()
    out = nc.dram_tensor("out", [B, S, C], F32, kind="ExternalOutput").ap()
    program(nc, aps, out)
    r = run_bass_kernel_spmd(nc, [arrays], core_ids=[0])
    return r.results[0]["out"]
```
